# Optimizing a Trainium2 kernel written in Bass

```python
import numpy as np
import jax
import jax.numpy as jnp

def _softmax(x, axis=-1):
    return jax.nn.softmax(x, axis=axis)

def _gelu(x):
    return jax.nn.gelu(x, approximate=True)

def _silu(x):
    return jax.nn.silu(x)

def _sigmoid(x):
    return jax.nn.sigmoid(x)

def _layernorm(x, axis=-1, eps=1e-05):
    m = jnp.mean(x, axis=axis, keepdims=True)
    v = jnp.var(x, axis=axis, keepdims=True)
    return (x - m) / jnp.sqrt(v + eps)

def _scatter_add(tgt, idx, src, axis=0):
    return tgt.at[idx].add(src)

def _segment_sum(src, seg, n):
    return jax.ops.segment_sum(src, seg, n)
kernel_name = 'mk_decoder_preln_d1_seqx_r4_c02fbc'

def setup_inputs(seed: int=0):
    np.random.seed(seed)
    _w = jnp.asarray

    def _rec_inputs():
        import jax
        import jax.numpy as jnp
        _rk = jax.random.key(seed)
        x = -0.0003929 + 0.9999 * jax.random.normal(jax.random.fold_in(_rk, 1), (16, 256, 256), jnp.float32)
        _lenS = 256 - jax.random.randint(jax.random.fold_in(_rk, 7), (16,), 0, max(1, 256 // 4) + 1, jnp.int32)
        _lenS2 = 256 - jax.random.randint(jax.random.fold_in(_rk, 8), (16,), 0, max(1, 256 // 4) + 1, jnp.int32)
        _ctx_1024P = jax.random.normal(jax.random.fold_in(_rk, 11), (16, 16, 256), jnp.float32)
        _ctx_1024c = jax.random.dirichlet(jax.random.fold_in(_rk, 511), 0.3 * jnp.ones((16,), jnp.float32), (16, 256))
        _ctx_1024t = jnp.einsum('bsk,bkd->bsd', _ctx_1024c, _ctx_1024P)
        _ctx_1024t = _ctx_1024t * jax.lax.rsqrt(jnp.mean(jnp.square(_ctx_1024t)) + 1e-12) * 0.953939
        ctx_1024 = -1.52775e-05 + 0.999936 * (_ctx_1024t + 0.3 * jax.random.normal(jax.random.fold_in(_rk, 611), (16, 256, 256), jnp.float32))
        return (x, ctx_1024)
    x, ctx_1024 = _rec_inputs()

    def _L0_attn_setup():
        import jax, jax.numpy as jnp
        import numpy as np
        DIMS = 256
        HEAD = 16
        HD = DIMS // HEAD
        EPS = 1e-05

        def _freqs_base():
            hd2 = HD // 2
            top = 2595.0 * jnp.log10(jnp.asarray(1.0 + 4000.0 / 200.0, dtype=jnp.float32))
            mel = jnp.power(10.0, jnp.linspace(0.0, top, hd2, dtype=jnp.float32) / 2595.0) - 1.0
            return 200.0 * mel / 1000.0

        def _rope(x, theta):
            T = x.shape[2]
            freqs = theta / 220.0 * _freqs_base()
            ang = jnp.arange(T, dtype=jnp.float32)[:, None] * freqs
            cos, sin = (jnp.cos(ang), jnp.sin(ang))
            xr = x.reshape(*x.shape[:-1], HD // 2, 2)
            a, b = (xr[..., 0], xr[..., 1])
            rot = jnp.stack([a * cos - b * sin, a * sin + b * cos], axis=-1)
            return rot.reshape(x.shape).astype(x.dtype)

        def _taylor_softmax(x):
            t = 1.0 + x + 0.5 * x * x
            return t / jnp.sum(t, axis=-1, keepdims=True)
        key = jax.random.key(seed)
        ks = jax.random.split(key, 4)
        B, T = (1, 512)
        s = 1.0 / np.sqrt(DIMS)
        return {'x': jax.random.normal(ks[0], (B, T, DIMS), dtype=jnp.float32), 'ln_w': jnp.ones((DIMS,), dtype=jnp.float32), 'ln_b': jnp.zeros((DIMS,), dtype=jnp.float32), 'w_q': jax.random.normal(ks[1], (DIMS, DIMS), dtype=jnp.float32) * s, 'w_kv': jax.random.normal(ks[2], (DIMS, 2 * DIMS), dtype=jnp.float32) * s, 'w_o': jax.random.normal(ks[3], (DIMS, DIMS), dtype=jnp.float32) * s, 'theta': jnp.asarray(10000.0, dtype=jnp.float32)}
    _L0_attn_all = _L0_attn_setup()
    _L0_attn_in = {k: v for k, v in _L0_attn_all.items() if k in ('ln_w', 'ln_b', 'w_q', 'w_kv', 'w_o', 'theta')}
    del _L0_attn_all

    def _L0_xattn_setup():
        import jax, jax.numpy as jnp
        import numpy as np
        DIM = 256
        key = jax.random.key(seed)
        k1, k2, k3, k4 = jax.random.split(key, 4)
        decoder_states = jax.random.normal(k1, (32, 128, DIM), dtype=jnp.float32)
        encoder_states = jax.random.normal(k2, (32, 256, DIM), dtype=jnp.float32)
        bound = 1.0 / np.sqrt(2 * DIM)
        mlp_weight = jax.random.uniform(k3, (1, 2 * DIM), minval=-bound, maxval=bound, dtype=jnp.float32)
        mlp_bias = jax.random.uniform(k4, (1,), minval=-bound, maxval=bound, dtype=jnp.float32)
        return {'decoder_states': decoder_states, 'encoder_states': encoder_states, 'step': 0, 'mlp_weight': mlp_weight, 'mlp_bias': mlp_bias}
    _L0_xattn_all = _L0_xattn_setup()
    _L0_xattn_in = {k: v for k, v in _L0_xattn_all.items() if k in ('mlp_weight', 'mlp_bias')}
    del _L0_xattn_all

    def _L0_ffn_setup():
        import jax, jax.numpy as jnp
        import numpy as np
        H = 256
        M = 128
        E = 16
        TOP_K = 2
        SCALE = 2.5
        NORM_TOPK = True
        B, S = (1, 256)

        def _moe(x, gate_w, w_gate, w_up, w_down, ws_gate, ws_up, ws_down):
            T = x.shape[0]
            shared = jax.nn.silu(x @ ws_gate) * (x @ ws_up) @ ws_down
            scores = jax.nn.sigmoid(x.astype(jnp.float32) @ gate_w.T.astype(jnp.float32))
            topk_w, topk_idx = jax.lax.top_k(scores, TOP_K)
            if NORM_TOPK and TOP_K > 1:
                topk_w = topk_w / (topk_w.sum(-1, keepdims=True) + 1e-20)
            topk_w = topk_w * SCALE
            route = jnp.zeros((T, E), topk_w.dtype).at[jnp.arange(T)[:, None], topk_idx].set(topk_w)
            g = jnp.einsum('th,ehm->etm', x, w_gate)
            u = jnp.einsum('th,ehm->etm', x, w_up)
            eo = jnp.einsum('etm,emh->eth', jax.nn.silu(g) * u, w_down)
            routed = jnp.einsum('te,eth->th', route.astype(x.dtype), eo)
            return routed + shared
        key = jax.random.key(seed)
        ks = jax.random.split(key, 8)
        std = 0.02
        return {'hidden_states': jax.random.normal(ks[0], (B, S, H), jnp.float32), 'gate_w': jax.random.normal(ks[1], (E, H), jnp.float32) * std, 'w_gate': jax.random.normal(ks[2], (E, H, M), jnp.float32) * std, 'w_up': jax.random.normal(ks[3], (E, H, M), jnp.float32) * std, 'w_down': jax.random.normal(ks[4], (E, M, H), jnp.float32) * std, 'ws_gate': jax.random.normal(ks[5], (H, M), jnp.float32) * std, 'ws_up': jax.random.normal(ks[6], (H, M), jnp.float32) * std, 'ws_down': jax.random.normal(ks[7], (M, H), jnp.float32) * std}
    _L0_ffn_all = _L0_ffn_setup()
    _L0_ffn_in = {k: v for k, v in _L0_ffn_all.items() if k in ('gate_w', 'w_gate', 'w_up', 'w_down', 'ws_gate', 'ws_up', 'ws_down')}
    del _L0_ffn_all
    return {'x': x, 'ctx_1024': ctx_1024, 'L0_attn_ln_w': _L0_attn_in['ln_w'], 'L0_attn_ln_b': _L0_attn_in['ln_b'], 'L0_attn_w_q': _L0_attn_in['w_q'], 'L0_attn_w_kv': _L0_attn_in['w_kv'], 'L0_attn_w_o': _L0_attn_in['w_o'], 'L0_attn_theta': _L0_attn_in['theta'], 'L0_xattn_mlp_weight': _L0_xattn_in['mlp_weight'], 'L0_xattn_mlp_bias': _L0_xattn_in['mlp_bias'], 'L0_ffn_gate_w': _L0_ffn_in['gate_w'], 'L0_ffn_w_gate': _L0_ffn_in['w_gate'], 'L0_ffn_w_up': _L0_ffn_in['w_up'], 'L0_ffn_w_down': _L0_ffn_in['w_down'], 'L0_ffn_ws_gate': _L0_ffn_in['ws_gate'], 'L0_ffn_ws_up': _L0_ffn_in['ws_up'], 'L0_ffn_ws_down': _L0_ffn_in['ws_down']}

def reference(x, ctx_1024, L0_attn_ln_w, L0_attn_ln_b, L0_attn_w_q, L0_attn_w_kv, L0_attn_w_o, L0_attn_theta, L0_xattn_mlp_weight, L0_xattn_mlp_bias, L0_ffn_gate_w, L0_ffn_w_gate, L0_ffn_w_up, L0_ffn_w_down, L0_ffn_ws_gate, L0_ffn_ws_up, L0_ffn_ws_down):
    import jax
    import jax.numpy as jnp

    def _L0_attn_ref(x, ln_w, ln_b, w_q, w_kv, w_o, theta):
        import jax, jax.numpy as jnp
        import numpy as np
        DIMS = 256
        HEAD = 16
        HD = DIMS // HEAD
        EPS = 1e-05

        def _freqs_base():
            hd2 = HD // 2
            top = 2595.0 * jnp.log10(jnp.asarray(1.0 + 4000.0 / 200.0, dtype=jnp.float32))
            mel = jnp.power(10.0, jnp.linspace(0.0, top, hd2, dtype=jnp.float32) / 2595.0) - 1.0
            return 200.0 * mel / 1000.0

        def _rope(x, theta):
            T = x.shape[2]
            freqs = theta / 220.0 * _freqs_base()
            ang = jnp.arange(T, dtype=jnp.float32)[:, None] * freqs
            cos, sin = (jnp.cos(ang), jnp.sin(ang))
            xr = x.reshape(*x.shape[:-1], HD // 2, 2)
            a, b = (xr[..., 0], xr[..., 1])
            rot = jnp.stack([a * cos - b * sin, a * sin + b * cos], axis=-1)
            return rot.reshape(x.shape).astype(x.dtype)

        def _taylor_softmax(x):
            t = 1.0 + x + 0.5 * x * x
            return t / jnp.sum(t, axis=-1, keepdims=True)
        B, T, _ = x.shape
        mu = jnp.mean(x, axis=-1, keepdims=True)
        var = jnp.mean(jnp.square(x - mu), axis=-1, keepdims=True)
        h = (x - mu) * jax.lax.rsqrt(var + EPS) * ln_w + ln_b
        q = h @ w_q
        kv = h @ w_kv
        k, v = (kv[..., :DIMS], kv[..., DIMS:])

        def to_heads(t):
            return t.reshape(B, T, HEAD, HD).transpose(0, 2, 1, 3)
        q, k, v = (to_heads(q), to_heads(k), to_heads(v))
        scale = HD ** (-0.5)
        q = _rope(q, theta)
        k = _rope(k, theta)
        qk = jnp.einsum('bhkd,bhqd->bhkq', q, k) * scale
        attn = _taylor_softmax(qk)
        wv = jnp.einsum('bhkq,bhqd->bhkd', attn, v)
        wv = wv.transpose(0, 2, 1, 3).reshape(B, T, DIMS)
        return wv @ w_o

    def _L0_xattn_ref(decoder_states, encoder_states, step, mlp_weight, mlp_bias):
        import jax, jax.numpy as jnp
        import numpy as np
        DIM = 256
        w = mlp_weight[0]
        w_enc, w_dec = (w[:DIM], w[DIM:])
        enc_proj = encoder_states @ w_enc
        dec_proj = decoder_states @ w_dec
        attn = dec_proj[:, :, None] + enc_proj[:, None, :] + mlp_bias[0]
        return attn

    def _L0_ffn_ref(hidden_states, gate_w, w_gate, w_up, w_down, ws_gate, ws_up, ws_down):
        import jax, jax.numpy as jnp
        import numpy as np
        H = 256
        M = 128
        E = 16
        TOP_K = 2
        SCALE = 2.5
        NORM_TOPK = True
        B, S = (1, 256)

        def _moe(x, gate_w, w_gate, w_up, w_down, ws_gate, ws_up, ws_down):
            T = x.shape[0]
            shared = jax.nn.silu(x @ ws_gate) * (x @ ws_up) @ ws_down
            scores = jax.nn.sigmoid(x.astype(jnp.float32) @ gate_w.T.astype(jnp.float32))
            topk_w, topk_idx = jax.lax.top_k(scores, TOP_K)
            if NORM_TOPK and TOP_K > 1:
                topk_w = topk_w / (topk_w.sum(-1, keepdims=True) + 1e-20)
            topk_w = topk_w * SCALE
            route = jnp.zeros((T, E), topk_w.dtype).at[jnp.arange(T)[:, None], topk_idx].set(topk_w)
            g = jnp.einsum('th,ehm->etm', x, w_gate)
            u = jnp.einsum('th,ehm->etm', x, w_up)
            eo = jnp.einsum('etm,emh->eth', jax.nn.silu(g) * u, w_down)
            routed = jnp.einsum('te,eth->th', route.astype(x.dtype), eo)
            return routed + shared
        b, s, h = hidden_states.shape
        x = hidden_states.reshape(-1, h)
        out = _moe(x, gate_w, w_gate, w_up, w_down, ws_gate, ws_up, ws_down)
        return out.reshape(b, s, h)
    x = x + _L0_attn_ref(_layernorm(x, axis=-1), L0_attn_ln_w, L0_attn_ln_b, L0_attn_w_q, L0_attn_w_kv, L0_attn_w_o, L0_attn_theta)
    x = x + _L0_xattn_ref(_layernorm(x, axis=-1), ctx_1024, 0, L0_xattn_mlp_weight, L0_xattn_mlp_bias)
    x = x + _L0_ffn_ref(_layernorm(x, axis=-1), L0_ffn_gate_w, L0_ffn_w_gate, L0_ffn_w_up, L0_ffn_w_down, L0_ffn_ws_gate, L0_ffn_ws_up, L0_ffn_ws_down)
    return x

_drawn_inputs = setup_inputs


def setup_inputs(seed=0):
    import zlib

    import numpy as np

    out = dict(_drawn_inputs(seed))
    spreads = {'L0_attn_ln_w': (1.0, 0.6), 'L0_attn_ln_b': (0.0, 0.1)}
    factors = {'L0_ffn_gate_w': 3.358,
     'L0_ffn_w_gate': 3.144,
     'L0_ffn_w_up': 3.116,
     'L0_ffn_w_down': 3.112,
     'L0_ffn_ws_gate': 5.612,
     'L0_ffn_ws_up': 5.49,
     'L0_ffn_ws_down': 5.504}
    for name, (base, spread) in spreads.items():
        noise = np.random.default_rng([zlib.crc32(name.encode()), seed]).standard_normal(out[name].shape)
        drawn = base * np.exp(spread * noise) if base else spread * noise
        out[name] = jnp.asarray(drawn.astype(out[name].dtype))
    for name, factor in factors.items():
        out[name] = (out[name] * factor).astype(out[name].dtype)
    return out
```

```python
from contextlib import ExitStack

import numpy as np

import concourse.bass as bass
from concourse import mybir

F32 = mybir.dt.float32
F16 = mybir.dt.float16
BF16 = mybir.dt.bfloat16
I32 = mybir.dt.int32
U32 = mybir.dt.uint32
ALU = mybir.AluOpType
ACT = mybir.ActivationFunctionType
AX = mybir.AxisListType

P = 128
NB, T, D = 16, 256, 256
TT = T // P
KD = D // P
HEADS, HD = 16, 16
GROUPS = 4
HPG = HEADS // GROUPS
E, M, TOPK = 16, 128, 2
NTOK = NB * T
NTILES = NTOK // P
ROUTE_SCALE = 2.5
EPS = 1e-5

ROW = D + 2
EROWS = NTOK + P
SLOTS = (NTOK * TOPK) // P + E
NULLS = SLOTS - (NTOK * TOPK) // P
XROWS = E * EROWS + NULLS * P
YROWS = NTOK * TOPK
SKIP_ROW = 1 << 20

MAGIC = 1.5 * 2.0 ** 23


def mel_base():
    f = np.float32
    top = f(2595.0 * np.log10(1.0 + 4000.0 / 200.0))
    lin = np.array([top * f(i / (HD // 2 - 1)) for i in range(HD // 2)], f)
    mel = np.power(10.0, (lin / f(2595.0)).astype(np.float64)).astype(f) - f(1.0)
    return [float(v) for v in (f(200.0) * mel / f(1000.0)).astype(f)]


def two_pi_parts():
    c1 = 6.28125
    c2 = float(np.round((2 * np.pi - c1) * 2.0 ** 18) / 2.0 ** 18)
    return c1, c2, float(np.float32(2 * np.pi - c1 - c2))


def build(nc, x, ctx_in, ln_w, ln_b, w_q, w_kv, w_o, theta, mlp_w, mlp_b,
          gate_wT, w_gate, w_up, w_down, ws_gate, ws_up, ws_down, out):
    with ExitStack() as ctx:
        def sb(name, shape, dt=F32):
            return ctx.enter_context(nc.sbuf_tensor(name, shape, dt))

        def sem(name):
            return ctx.enter_context(nc.semaphore(name))

        disp = nc.dram_tensor("dispatch", [XROWS, ROW], F32, kind="Internal").ap()
        yexp = nc.dram_tensor("expert_out", [YROWS, D], F32, kind="Internal").ap()

        wqk = sb("wqk", [P, KD, 2 * D])
        wv_w = sb("wv_w", [P, KD, D])
        wo = sb("wo", [P, KD, D])
        wsgu = sb("wsgu", [P, KD, 2 * M])
        wsd = sb("wsd", [P, D])
        gwT = sb("gwT", [P, KD, E])
        wgu = sb("wgu", [P, E * KD * 2 * M])
        wdn = sb("wdn", [P, E * D])
        lnw_c = sb("lnw_c", [P, KD])
        lnb_c = sb("lnb_c", [P, KD])
        wenc = sb("wenc", [P, D])
        wdec = sb("wdec", [P, D])
        mbias = sb("mbias", [P, 1])
        theta_c = sb("theta_c", [P, 1])
        identf = sb("identf", [P, P])
        identh = sb("identh", [P, P], F16)
        tri = sb("tri", [P, P], BF16)
        onesb = sb("onesb", [P, P], BF16)
        onesf = sb("onesf", [P, E])
        iota16 = sb("iota16", [P, E])
        ebase = sb("ebase", [P, E])
        ebase_i = sb("ebase_i", [P, E], I32)
        iota_i = sb("iota_i", [P, E], I32)
        tok_i = sb("tok_i", [P, TT], I32)
        tokf = sb("tokf", [P, TT])
        idi = sb("idi", [P, TOPK, TT], I32)
        idf = sb("idf", [P, TOPK, TT])
        freq = sb("freq", [P, HD // 2])
        ang = sb("ang", [P, TT, HD // 2])
        turns = sb("turns", [P, TT, HD // 2])
        angc = sb("angc", [P, TT, HD // 2])
        wrap = sb("wrap", [P, TT, HD // 2])
        cosr = sb("cosr", [P, TT, HD // 2, 2])
        sinr = sb("sinr", [P, TT, HD // 2, 2])
        halfneg = sb("halfneg", [P, 2])
        filler = sb("filler", [P, ROW])

        xa = sb("xa", [P, 2, TT, D])
        xb = sb("xb", [P, 2, TT, D])
        cx = sb("cx", [P, 2, TT, D])
        xn = sb("xn", [P, TT, D])
        hT = sb("hT", [P, KD, T])
        rt1 = sb("rt1", [P, TT, 2 * D])
        rt2 = sb("rt2", [P, TT, 2 * D])
        rot = sb("rot", [P, TT, 2 * D])
        stack = sb("stack", [P, TT, 2 * HEADS, 4, HD], F16)
        qT = sb("qT", [P, 2, HEADS // 2, T], F16)
        kT = sb("kT", [P, 2, HEADS // 2, T], F16)
        vaug = sb("vaug", [P, 2, TT, HEADS, 32])
        sq = sb("sq", [P, 4, 2, TT, T])
        vsum = sb("vsum", [P, GROUPS])
        oT = sb("oT", [P, GROUPS, T])
        rec = sb("rec", [P, TT, HEADS])
        wv = sb("wv", [P, TT, D])
        wvT = sb("wvT", [P, KD, T])
        x1 = sb("x1", [P, TT, D])
        x2 = sb("x2", [P, TT, D])
        scr = sb("scr", [P, TT, D])
        scr2 = sb("scr2", [P, TT, D])
        enc = sb("enc", [P, TT])
        dec = sb("dec", [P, TT])
        h3T = sb("h3T", [P, KD, T])
        rows = [sb(f"rows{k}", [P, 2, TT, ROW]) for k in range(TOPK)]
        sgT = sb("sgT", [P, T])
        hidT = sb("hidT", [P, T])
        stats = sb("stats", [P, 3, TT, 6])
        mv = sb("mv", [P, 3, TT, 2])
        vtmp = sb("vtmp", [P, 3, TT])
        rstd = sb("rstd", [P, 3, TT])
        score = sb("score", [P, TT, E])
        topv = sb("topv", [P, TT, 8])
        topi = sb("topi", [P, TT, 8], U32)
        topf = sb("topf", [P, TT * TOPK])
        ssum = sb("ssum", [P, TT])
        onehot = sb("onehot", [P, TT * TOPK, E])
        chosen = sb("chosen", [P, TT, E], BF16)
        seen = sb("seen", [P, E], BF16)
        pose = sb("pose", [P, TT, E])
        posp = sb("posp", [P, TT * TOPK, E])
        posf = sb("posf", [P, TT * TOPK])
        posi = sb("posi", [P, 2, TT * TOPK], I32)
        acc = sb("acc", [P, NTILES * D])

        sidx_i = sb("sidx_i", [P, 1], I32)
        sidx = sb("sidx", [P, 1])
        cnt = sb("cnt", [P, E])
        cnt_i = sb("cnt_i", [P, 2, E], I32)
        ntl = sb("ntl", [P, E])
        cum = sb("cum", [P, E])
        le = sb("le", [P, E])
        lep = sb("lep", [P, E])
        plan = sb("plan", [P, 8])
        plan_i = sb("plan_i", [1, 2 * P + E], I32)

        XRING, YRING = 8, 4
        sq_flat = sq[:, :, :, :, :].rearrange("p a b c d -> p (a b c d)")
        vaug_flat = vaug[:, :, :, :, :].rearrange("p a b c d -> p (a b c d)")
        at = XRING * ROW
        xs = sq_flat[:, 0:at].rearrange("p (r w) -> p r w", r=XRING)
        exT = sq_flat[:, at:at + 2 * D].rearrange("p (r k t) -> p r k t", r=2, k=KD)
        at += 2 * D
        esg = sq_flat[:, at:at + 2 * M].rearrange("p (r m) -> p r m", r=2)
        at += 2 * M
        ehd = sq_flat[:, at:at + 2 * M].rearrange("p (r m) -> p r m", r=2)
        at += 2 * M
        ehT = sq_flat[:, at:at + 2 * P].rearrange("p (r m) -> p r m", r=2)
        ys = vaug_flat[:, 0:YRING * D].rearrange("p (r d) -> p r d", r=YRING)
        CRING = 4
        ypair = stack[:, :, :, :, :].rearrange("p a b c d -> p (a b c d)").bitcast(F32)\
            .rearrange("p (r w) -> p r w", r=CRING)

        bank = [ctx.enter_context(nc.psum_tensor(f"bank{i}", [P, 512], F32)) for i in range(8)]
        PVB, FB, B6, B7 = 4, 5, 6, 7

        w_in = sem("w_in")
        wE_in = sem("wE_in")
        c_pool = sem("c_pool")
        c_dve = sem("c_dve")
        c_act = sem("c_act")
        null_in = sem("null_in")
        xa_in = [sem(f"xa_in{p}") for p in range(2)]
        xb_in = [sem(f"xb_in{p}") for p in range(2)]
        cx_in = [sem(f"cx_in{p}") for p in range(2)]
        ln_mv = [sem(f"ln_mv{n}") for n in range(3)]
        rr = [sem(f"rr{n}") for n in range(3)]
        xn_ok = sem("xn_ok")
        tx_ps = sem("tx_ps")
        hT_ok = sem("hT_ok")
        qk_ps = sem("qk_ps")
        ro_ok = sem("ro_ok")
        rot_ok = sem("rot_ok")
        hi_ok = sem("hi_ok")
        stk_ok = sem("stk_ok")
        v_ps = sem("v_ps")
        v_ok = sem("v_ok")
        tqk_ps = sem("tqk_ps")
        qkT_ok = sem("qkT_ok")
        c_ps = sem("c_ps")
        c_ok = sem("c_ok")
        s_ps = sem("s_ps")
        sq_ok = sem("sq_ok")
        pv_ps = sem("pv_ps")
        o_ok = sem("o_ok")
        to_ps = sem("to_ps")
        rec_ok = sem("rec_ok")
        wv_ok = sem("wv_ok")
        tw_ps = sem("tw_ps")
        wvT_ok = sem("wvT_ok")
        wo_ps = sem("wo_ps")
        x1_ok = sem("x1_ok")
        enc_ok = sem("enc_ok")
        e_ps = sem("e_ps")
        dec_ok = sem("dec_ok")
        x2_ok = sem("x2_ok")
        h3_ok = sem("h3_ok")
        th_ps = sem("th_ps")
        h3T_ok = sem("h3T_ok")
        ga_ps = sem("ga_ps")
        sco_ok = sem("sco_ok")
        sh_ps = sem("sh_ps")
        sg_ok = sem("sg_ok")
        hid_ok = sem("hid_ok")
        ra_ok = sem("ra_ok")
        rk_ps = sem("rk_ps")
        rb_ok = sem("rb_ok")
        dn_ps = sem("dn_ps")
        acc_ok = sem("acc_ok")
        copy_ok = sem("copy_ok")
        sent = [sem(f"sent{p}") for p in range(2)]
        cnt_ps = sem("cnt_ps")
        pl_ok = sem("pl_ok")
        plan_ps = sem("plan_ps")
        plan_ok = sem("plan_ok")
        fill_in = sem("fill_in")
        xs_in = [sem(f"xs_in{r}") for r in range(XRING)]
        etx_ps = sem("etx_ps")
        exT_ok = sem("exT_ok")
        gu_ps = sem("gu_ps")
        esg_ok = sem("esg_ok")
        ehd_ok = sem("ehd_ok")
        etd_ps = sem("etd_ps")
        ehT_ok = sem("ehT_ok")
        edn_ps = sem("edn_ps")
        ys_ok = sem("ys_ok")
        ys_out = [sem(f"ys_out{r}") for r in range(YRING)]
        yp_in = [sem(f"yp_in{r}") for r in range(CRING)]
        f1_ok = sem("f1_ok")
        fin_ok = sem("fin_ok")
        out_done = sem("out_done")
        passed = {nc.vector.engine: sem("passed_dve"), nc.gpsimd.engine: sem("passed_pool")}

        block = ctx.enter_context(nc.Block())

        def wait(eng, s, value):
            if not (isinstance(value, int) and value <= 0):
                eng.wait_ge(s, value)

        def wait_first(eng, s, value):
            wait(eng, s, value)
            if not isinstance(value, int):
                eng.sem_inc(passed[eng.engine], 1)

        def num(b):
            return b[0] * 2 + b[1]

        def pipeline(eng, step):
            step(None, None, (0, 0))
            step((0, 0), None, (0, 1))
            step((0, 1), (0, 0), (1, 0))
            with eng.Fori(0, NB // 2 - 2) as m:
                step((m + 1, 0), (m, 1), (m + 1, 1))
                step((m + 1, 1), (m + 1, 0), (m + 2, 0))
            u = NB // 2 - 1
            step((u, 0), (u - 1, 1), (u, 1))
            step((u, 1), (u, 0), None)
            step(None, (u, 1), None)

        def slots(eng, step):
            for n in range(XRING):
                step(n, n, None)
            with eng.Fori(1, SLOTS // XRING) as m:
                for c in range(XRING):
                    step(m * XRING + c, c, m)
            for n in range(SLOTS, SLOTS + 3):
                step(n, n - SLOTS, None)

        xv = x.rearrange("b (t p) d -> b p t d", p=P)
        cv = ctx_in.rearrange("b (t p) d -> b p t d", p=P)
        NWLOADS = 15

        @block.sync
        def _(sp):
            def load_x(j, b):
                wait(sp, xn_ok, j - 1)
                sp.dma_start(xa[:, b[1], :, :], xv[bass.ds(j, 1), :, :, :].rearrange("o p t d -> p (o t) d")).then_inc(xa_in[b[1]], 16)

            def load_back(j, b):
                wait(sp, x1_ok, j - 1)
                sp.dma_start(xb[:, b[1], :, :], xv[bass.ds(j, 1), :, :, :].rearrange("o p t d -> p (o t) d")).then_inc(xb_in[b[1]], 16)
                sp.dma_start(cx[:, b[1], :, :], cv[bass.ds(j, 1), :, :, :].rearrange("o p t d -> p (o t) d")).then_inc(cx_in[b[1]], 16)

            load_x(0, (0, 0))
            load_x(1, (0, 1))
            for i in range(2):
                load_back(i, (0, i))
                load_x(i + 2, (1, i))
            with sp.Fori(0, NB // 2 - 2) as m:
                for p in range(2):
                    load_x(m * 2 + p + 4, (m + 2, p))
                    load_back(m * 2 + p + 2, (m + 1, p))
            for p in range(2):
                load_back(NB - 2 + p, (NB // 2 - 1, p))

            sp.wait_ge(plan_ok, 2)
            sp.wait_ge(c_pool, 11)
            with sp.Fori(0, E) as e:
                r = sp.value_load(plan_i[0:1, bass.ds(e + 2 * P, 1)], min_val=0, max_val=XROWS - P)
                sp.dma_start(disp[bass.ds(r, P), :], filler[:, :]).then_inc(fill_in, 16)
            sp.wait_ge(fill_in, 16 * E)
            sp.wait_ge(null_in, 16 * NULLS)
            for p in range(2):
                sp.wait_ge(sent[p], 16 * TT * TOPK * (NB // 2))
            sp.wait_ge(pv_ps, GROUPS * NB)

            def load_slot(n, c, m):
                if isinstance(n, int) and n >= SLOTS:
                    return
                q = n // YRING if isinstance(n, int) else m * 2 + c // YRING
                wait(sp, ys_out[c % YRING], (q - 1) * 16)
                r = sp.value_load(plan_i[0:1, bass.ds(n, 1)], min_val=0, max_val=XROWS - P)
                sp.dma_start(xs[:, c, :], disp[bass.ds(r, P), :]).then_inc(xs_in[c], 16)

            slots(sp, load_slot)

            for r in range(YRING):
                sp.wait_ge(ys_out[r], 16 * SLOTS // YRING)
            yv = yexp.rearrange("(n k) d -> n (k d)", k=TOPK)
            for r in range(CRING):
                sp.dma_start(ypair[:, r, :], yv[r * P:(r + 1) * P, :]).then_inc(yp_in[r], 16)
            with sp.Fori(0, NTILES // CRING - 1) as m:
                for r in range(CRING):
                    sp.wait_ge(fin_ok, m * CRING + r + 1)
                    sp.dma_start(ypair[:, r, :], yv[bass.ds((m * CRING + r + CRING) * P, P), :]).then_inc(yp_in[r], 16)
            sp.wait_ge(out_done, 16 * NTILES)

        @block.gpsimd
        def _(pool):
            pool.memset(identf[:, :], 0.0).then_inc(c_pool, 1)
            pool.memset(identh[:, :], 0.0).then_inc(c_pool, 1)
            pool.memset(tri[:, :], 1.0).then_inc(c_pool, 1)
            pool.wait_ge(c_pool, 3)
            pool.affine_select(out=identf[:, :], in_=identf[:, :], compare_op=ALU.not_equal, fill=1.0,
                               base=0, pattern=[[-1, P]], channel_multiplier=1).then_inc(c_pool, 1)
            pool.affine_select(out=identh[:, :], in_=identh[:, :], compare_op=ALU.not_equal, fill=1.0,
                               base=0, pattern=[[-1, P]], channel_multiplier=1).then_inc(c_pool, 1)
            pool.affine_select(out=tri[:, :], in_=tri[:, :], compare_op=ALU.is_gt, fill=0.0,
                               base=0, pattern=[[1, P]], channel_multiplier=-1).then_inc(c_pool, 1)
            pool.iota(iota_i[:, :], [[1, E]], base=0, channel_multiplier=0).then_inc(c_pool, 1)
            pool.iota(ebase_i[:, :], [[EROWS, E]], base=0, channel_multiplier=0).then_inc(c_pool, 1)
            pool.iota(tok_i[:, :], [[P, TT]], base=0, channel_multiplier=1).then_inc(c_pool, 1)
            pool.iota(idi[:, :, :], [[1, TOPK], [P * TOPK, TT]], base=0, channel_multiplier=TOPK).then_inc(c_pool, 1)
            pool.iota(filler[:, D:D + 1].bitcast(I32), [[0, 1]], base=SKIP_ROW, channel_multiplier=0).then_inc(c_pool, 1)
            pool.iota(sidx_i[:, :], [[0, 1]], base=0, channel_multiplier=1).then_inc(c_pool, 1)

            def power(n, j, a, b):
                wait_first(pool, ln_mv[n], 4 * j + 4)
                pool.tensor_scalar(vtmp[:, n, :], mv[:, n, :, 1], a, b, ALU.mult, ALU.add).then_inc(rr[n], 1)
                pool.wait_ge(rr[n], 2 * j + 1)
                pool.tensor_tensor(rstd[:, n, :], vtmp[:, n, :], halfneg[:, :], ALU.pow).then_inc(rr[n], 1)

            def rotate(j, t):
                pool.wait_ge(ro_ok, 2 * j + t + 1)
                wait(pool, stk_ok, 6 * j + 3 * t - 5)
                pool.tensor_tensor(rot[:, t, :], rt1[:, t, :], rt2[:, t, :], ALU.add).then_inc(rot_ok, 1)

            pool.wait_ge(c_dve, 1)

            def step(att, back, front):
                if front:
                    power(0, num(front), 1.0 + EPS, EPS * EPS)
                if back:
                    power(1, num(back), 1.0, EPS)
                if front:
                    rotate(num(front), 0)
                if back:
                    power(2, num(back), 1.0, EPS)
                if front:
                    rotate(num(front), 1)
                if back:
                    j, p = num(back), back[1]
                    wait_first(pool, h3_ok, j + 1)
                    for t in range(TT):
                        last = pool.tensor_scalar(rows[1][:, p, t, 0:D], rows[0][:, p, t, 0:D], 1.0, 0.0, ALU.mult, ALU.add)
                    last.then_inc(copy_ok, 1)
                    pool.wait_ge(copy_ok, j + 1)
                    pool.wait_ge(ra_ok, 15 * j + 15)
                    wait_first(pool, rb_ok, 6 * j + 6)
                    for t in range(TT):
                        for k in range(TOPK):
                            i = t * TOPK + k
                            pool.indirect_dma_start(
                                disp, bass.IndirectOffsetOnAxis(ap=posi[:, p, i:i + 1].bitcast(U32), axis=0),
                                rows[k][:, p, t, :], None).then_inc(sent[p], 16)

            pipeline(pool, step)

            def send(n, c, m):
                if isinstance(n, int) and n < 3:
                    return
                wait_first(pool, ys_ok, n - 2)
                r, y = (c - 3) % XRING, (c - 3) % YRING
                pool.indirect_dma_start(
                    yexp, bass.IndirectOffsetOnAxis(ap=xs[:, r, D:D + 1].bitcast(U32), axis=0),
                    ys[:, y, :], None, bounds_check=YROWS - 1, oob_is_err=False).then_inc(ys_out[y], 16)

            slots(pool, send)

        @block.scalar
        def _(act):
            act.dma_start(theta_c[:, :], theta.partition_broadcast(P)).then_inc(w_in, 16)
            act.dma_start(lnw_c[:, :], ln_w).then_inc(w_in, 16)
            act.dma_start(lnb_c[:, :], ln_b).then_inc(w_in, 16)
            act.dma_start(wqk[:, :, 0:D], w_q.rearrange("(k p) n -> p k n", p=P)).then_inc(w_in, 16)
            act.dma_start(wqk[:, :, D:2 * D], w_kv[:, 0:D].rearrange("(k p) n -> p k n", p=P)).then_inc(w_in, 16)
            act.dma_start(wv_w[:, :, :], w_kv[:, D:2 * D].rearrange("(k p) n -> p k n", p=P)).then_inc(w_in, 16)
            act.dma_start(wo[:, :, :], w_o.rearrange("(k p) n -> p k n", p=P)).then_inc(w_in, 16)
            act.dma_start(wenc[:, :], mlp_w[0, 0:D].partition_broadcast(P)).then_inc(w_in, 16)
            act.dma_start(wdec[:, :], mlp_w[0, D:2 * D].partition_broadcast(P)).then_inc(w_in, 16)
            act.dma_start(mbias[:, :], mlp_b.partition_broadcast(P)).then_inc(w_in, 16)
            act.dma_start(gwT[:, :, :], gate_wT.rearrange("(k p) e -> p k e", p=P)).then_inc(w_in, 16)
            act.dma_start(wsgu[:, :, 0:M], ws_gate.rearrange("(k p) m -> p k m", p=P)).then_inc(w_in, 16)
            act.dma_start(wsgu[:, :, M:2 * M], ws_up.rearrange("(k p) m -> p k m", p=P)).then_inc(w_in, 16)
            act.dma_start(wsd[:, :], ws_down).then_inc(w_in, 16)
            wg4 = wgu[:, :].rearrange("p (e k n) -> p e k n", e=E, k=KD)
            for k in range(KD):
                act.dma_start(wg4[:, :, k, 0:M], w_gate[:, k * P:(k + 1) * P, :].rearrange("e p m -> p e m")).then_inc(wE_in, 16)
                act.dma_start(wg4[:, :, k, M:2 * M], w_up[:, k * P:(k + 1) * P, :].rearrange("e p m -> p e m")).then_inc(wE_in, 16)
            act.dma_start(wdn[:, :].rearrange("p (e n) -> p e n", e=E), w_down.rearrange("e p n -> p e n")).then_inc(wE_in, 16)
            act.wait_ge(c_pool, 11)
            act.wait_ge(c_dve, 1)
            with act.Fori(0, NULLS) as n:
                act.dma_start(disp[bass.ds(n * P + E * EROWS, P), :], filler[:, :]).then_inc(null_in, 16)
            act.wait_ge(c_dve, 17)
            act.activation(sinr[:, :, :, 1], ang[:, :, :], ACT.Sin).then_inc(c_act, 1)
            act.activation(cosr[:, :, :, 0], angc[:, :, :], ACT.Sin).then_inc(c_act, 1)
            act.activation(cosr[:, :, :, 1], angc[:, :, :], ACT.Sin).then_inc(c_act, 1)
            act.activation(sinr[:, :, :, 0], ang[:, :, :], ACT.Sin, scale=-1.0).then_inc(c_act, 1)
            act.preload_act_table_set("sigmoid_and_others")

            def squares(j, a):
                act.wait_ge(s_ps, 8 * j + a + 1)
                g = a // 2
                wait(act, pv_ps, GROUPS * j + g - 1)
                for b in range(2):
                    src = bank[2 * (a % 2) + b]
                    last = act.activation(sq[:, a % 4, b, :, :].rearrange("p a b -> p (a b)"), src[:, :],
                                          ACT.Square, scale=HD ** -0.5, bias=1.0)
                last.then_inc(sq_ok, 1)

            def attended(j, b, h):
                act.wait_ge(pv_ps, GROUPS * j + 2 * h + 2)
                if h == 0:
                    act.wait_ge(c_ok, j + 1)
                    wait(act, to_ps, TT * j)
                for g in range(2):
                    last = act.activation(oT[:, 2 * h + g, :], bank[PVB][:, g * T:(g + 1) * T], ACT.Identity,
                                          bias=vsum[:, 2 * h + g:2 * h + g + 1])
                last.then_inc(o_ok, 1)

            def high_part(j, t):
                act.wait_ge(rot_ok, 2 * j + t + 1)
                wait(act, tqk_ps, 4 * j + 2 * t - 2)
                act.activation(stack[:, t, :, 0, :], rot[:, t, :].rearrange("p (h d) -> p h d", d=HD),
                               ACT.Copy).then_inc(hi_ok, 1)

            def step(att, back, front):
                if att:
                    j = num(att)
                    squares(j, 0)
                    squares(j, 1)
                if back:
                    jb = num(back)
                    act.wait_ge(tw_ps, jb + 1)
                    wait(act, wo_ps, jb)
                    act.activation(wvT[:, :, :].rearrange("p k (t c) -> p t k c", t=TT),
                                   bank[B6][:, :].rearrange("p (t k c) -> p t k c", t=TT, k=KD), ACT.Copy).then_inc(wvT_ok, 1)
                if att:
                    squares(j, 2)
                    squares(j, 3)
                if front:
                    jf = num(front)
                    act.wait_ge(tx_ps, jf + 1)
                    wait(act, v_ps, jf)
                    for k in range(KD):
                        last = act.activation(hT[:, k, :].rearrange("p (t c) -> p t c", t=TT),
                                              bank[FB][:, :].rearrange("p (t k c) -> p k t c", t=TT, k=KD)[:, k, :, :],
                                              ACT.Identity, scale=lnw_c[:, k:k + 1], bias=lnb_c[:, k:k + 1])
                    last.then_inc(hT_ok, 1)
                if att:
                    squares(j, 4)
                    squares(j, 5)
                    attended(j, att, 0)
                    squares(j, 6)
                    squares(j, 7)
                if front:
                    high_part(jf, 0)
                    act.wait_ge(v_ps, jf + 1)
                    wait(act, pv_ps, GROUPS * (jf - 1))
                    act.activation(vaug[:, front[1], :, :, 0:HD].rearrange("p t h d -> p (t h) d"),
                                   bank[FB][:, :].rearrange("p (a d) -> p a d", d=HD), ACT.Copy).then_inc(v_ok, 1)
                    high_part(jf, 1)
                if back:
                    act.wait_ge(th_ps, jb + 1)
                    wait(act, sh_ps, jb)
                    act.activation(h3T[:, :, :].rearrange("p k (t c) -> p t k c", t=TT),
                                   bank[B7][:, :].rearrange("p (t k c) -> p t k c", t=TT, k=KD), ACT.Copy).then_inc(h3T_ok, 1)
                    act.wait_ge(ga_ps, jb + 1)
                    wait(act, ra_ok, 15 * jb)
                    act.activation(score[:, :, :].rearrange("p t e -> p (t e)"), bank[B6][:, 0:TT * E], ACT.Sigmoid).then_inc(sco_ok, 1)
                    act.wait_ge(sh_ps, jb + 1)
                    wait(act, hid_ok, 2 * jb)
                    act.activation(sgT[:, :], bank[B7][:, 0:T], ACT.Sigmoid).then_inc(sg_ok, 1)
                if att:
                    attended(j, att, 1)

            pipeline(act, step)

            def expert(n, c, m):
                small = isinstance(n, int)
                if not small or n < SLOTS:
                    act.wait_ge(etx_ps, n + 1)
                    if not small or n >= 2:
                        act.wait_ge(gu_ps, n - 1)
                    act.activation(exT[:, c % 2, :, :].rearrange("p k t -> p (k t)"), bank[c % 2][:, 0:D], ACT.Copy).then_inc(exT_ok, 1)
                if not small or 1 <= n <= SLOTS:
                    r = (c - 1) % 2
                    act.wait_ge(gu_ps, n)
                    if not small or n >= 3:
                        act.wait_ge(ehd_ok, n - 2)
                    act.activation(esg[:, r, :], bank[2 + r][:, 0:M], ACT.Silu).then_inc(esg_ok, 1)

            act.wait_ge(pv_ps, GROUPS * NB)
            slots(act, expert)

            with act.Fori(0, NTILES) as m:
                act.wait_ge(fin_ok, m + 1)
                act.dma_start(out.rearrange("b t d -> (b t) d")[bass.ds(m * P, P), :],
                              acc[:, bass.ds(m * D, D)]).then_inc(out_done, 16)

        @block.vector
        def _(dve):
            dve.memset(filler[:, 0:D], 0.0)
            dve.memset(filler[:, D + 1:D + 2], 0.0)
            dve.memset(seen[:, :], 0.0)
            dve.memset(onesb[:, :], 1.0)
            dve.memset(onesf[:, :], 1.0)
            dve.memset(vaug[:, :, :, :, HD + 1:32].rearrange("p a t h d -> p (a t h) d"), 0.0)
            dve.memset(vaug[:, :, :, :, HD:HD + 1].rearrange("p a t h d -> p (a t h) d"), 1.0)
            dve.memset(halfneg[:, :], -0.5).then_inc(c_dve, 1)
            dve.wait_ge(c_pool, 12)
            dve.tensor_copy(iota16[:, :], iota_i[:, :])
            dve.tensor_copy(ebase[:, :], ebase_i[:, :])
            dve.tensor_copy(idf[:, :, :], idi[:, :, :])
            dve.tensor_copy(sidx[:, :], sidx_i[:, :])
            dve.tensor_copy(tokf[:, :], tok_i[:, :])
            for i, v in enumerate(mel_base()):
                last = dve.memset(freq[:, i:i + 1], v)
            last.then_inc(c_dve, 1)
            dve.wait_ge(w_in, 16 * 14)
            dve.tensor_scalar(theta_c[:, :], theta_c[:, :], float(np.float32(1.0) / np.float32(220.0)), None, ALU.mult).then_inc(c_dve, 1)
            dve.wait_ge(c_dve, 3)
            dve.tensor_scalar(freq[:, :], freq[:, :], theta_c[:, 0:1], None, ALU.mult).then_inc(c_dve, 1)
            dve.wait_ge(c_dve, 4)
            for t in range(TT):
                last = dve.tensor_scalar(ang[:, t, :], freq[:, :], tokf[:, t:t + 1], None, ALU.mult)
            last.then_inc(c_dve, 1)
            dve.wait_ge(c_dve, 5)
            dve.tensor_scalar(turns[:, :, :], ang[:, :, :], float(1.0 / (2 * np.pi)), MAGIC, ALU.mult, ALU.add).then_inc(c_dve, 1)
            dve.wait_ge(c_dve, 6)
            dve.tensor_scalar(turns[:, :, :], turns[:, :, :], -MAGIC, None, ALU.add).then_inc(c_dve, 1)
            n = 7
            for c in two_pi_parts():
                dve.wait_ge(c_dve, n)
                dve.scalar_tensor_tensor(ang[:, :, :], turns[:, :, :], -c, ang[:, :, :], ALU.mult, ALU.add).then_inc(c_dve, 1)
                n += 1
            dve.wait_ge(c_dve, n)
            dve.tensor_scalar(angc[:, :, :], ang[:, :, :], float(np.pi / 2), None, ALU.add).then_inc(c_dve, 1)
            dve.wait_ge(c_dve, n + 1)
            dve.tensor_scalar(wrap[:, :, :], angc[:, :, :], float(np.pi), None, ALU.is_gt).then_inc(c_dve, 1)
            dve.wait_ge(c_dve, n + 2)
            dve.scalar_tensor_tensor(angc[:, :, :], wrap[:, :, :], float(-2 * np.pi), angc[:, :, :], ALU.mult, ALU.add).then_inc(c_dve, 1)
            dve.wait_ge(c_dve, n + 3)
            lim = 3.1415925
            dve.tensor_scalar(angc[:, :, :], angc[:, :, :], lim, -lim, ALU.min, ALU.max).then_inc(c_dve, 1)
            dve.tensor_scalar(ang[:, :, :], ang[:, :, :], lim, -lim, ALU.min, ALU.max).then_inc(c_dve, 1)
            assert n + 5 == 15
            dve.wait_ge(c_dve, 15)
            dve.engine_nop().then_inc(c_dve, 2)
            dve.wait_ge(c_act, 4)

            def norm_stats(n, j, src):
                for t in range(TT):
                    dve.bn_stats(stats[:, n, t, :], src[:, t, :]).then_inc(ln_mv[n], 1)
                for t in range(TT):
                    wait_first(dve, ln_mv[n], 4 * j + t + 1)
                    dve.bn_aggr(mv[:, n, t, :], stats[:, n, t, :]).then_inc(ln_mv[n], 1)

            def rope(j, t):
                dve.wait_ge(qk_ps, 2 * j + t + 1)
                wait(dve, rot_ok, 2 * j + t - 1)
                src = bank[FB][:, :].rearrange("p (h d c) -> p h d c", d=HD // 2, c=2)
                swapped = bass.AP(src.tensor, src.offset + 1, [list(src.ap[0]), [HD, 2 * HEADS], [2, HD // 2], [-1, 2]])
                shape = [P, 2 * HEADS, HD // 2, 2]
                dst = [r[:, t, :].rearrange("p (h d c) -> p h d c", d=HD // 2, c=2) for r in (rt1, rt2)]
                dve.tensor_tensor(dst[0], src, cosr[:, t, :, :].unsqueeze(1).to_broadcast(shape), ALU.mult)
                dve.tensor_tensor(dst[1], swapped, sinr[:, t, :, :].unsqueeze(1).to_broadcast(shape), ALU.mult).then_inc(ro_ok, 1)

            def low_part(j, t):
                dve.wait_ge(hi_ok, 2 * j + t + 1)
                wait(dve, tqk_ps, 4 * j + 2 * t - 2)
                st = stack[:, t, :, :, :]
                dve.tensor_tensor(st[:, :, 2, :], rot[:, t, :].rearrange("p (h d) -> p h d", d=HD), st[:, :, 0, :], ALU.subtract).then_inc(stk_ok, 1)
                dve.wait_ge(stk_ok, 6 * j + 3 * t + 1)
                dve.tensor_copy(st[:, 0:HEADS, 1:4:2, :], st[:, 0:HEADS, 0:4:2, :]).then_inc(stk_ok, 1)
                kk = st[:, HEADS:2 * HEADS, :, :]
                back_to_front = bass.AP(kk.tensor, kk.offset + 3 * HD, [list(kk.ap[0]), [4 * HD, HEADS], [-2 * HD, 2], [1, HD]])
                dve.tensor_copy(back_to_front, kk[:, :, 0:4:2, :]).then_inc(stk_ok, 1)

            def keep_T(j, b, t, which):
                dve.wait_ge(tqk_ps, 4 * j + 2 * t + which + 1)
                if t == 0:
                    wait(dve, s_ps, 8 * (j - 1))
                dst = (qT, kT)[which]
                dve.tensor_copy(dst[:, b[1], :, t * P:(t + 1) * P],
                                bank[FB][:, :].bitcast(F16).rearrange("p (a c) -> p a c", c=P)).then_inc(qkT_ok, 1)

            def step(att, back, front):
                if back:
                    jb, pb = num(back), back[1]
                    for t in range(TT):
                        dve.wait_ge(to_ps, TT * jb + t + 1)
                        o = bank[(B6, B7)[t]][:, :].rearrange("p (h c) -> p h c", c=32)
                        dve.reciprocal(rec[:, t, :].unsqueeze(2), o[:, :, HD:HD + 1]).then_inc(rec_ok, 1)
                        dve.wait_ge(rec_ok, TT * jb + t + 1)
                        wait(dve, tw_ps, jb)
                        dve.tensor_tensor(wv[:, t, :].rearrange("p (h d) -> p h d", d=HD), o[:, :, 0:HD],
                                          rec[:, t, :].unsqueeze(2).to_broadcast([P, HEADS, HD]), ALU.mult).then_inc(wv_ok, 1)
                if front:
                    jf, pf = num(front), front[1]
                    dve.wait_ge(xa_in[pf], front[0] * 16 + 16)
                    norm_stats(0, jf, xa[:, pf, :, :])
                if back:
                    dve.wait_ge(cx_in[pb], back[0] * 16 + 16)
                    wait(dve, e_ps, jb)
                    for t in range(TT):
                        dve.scalar_tensor_tensor(scr[:, t, :], cx[:, pb, t, :], 1.0, wenc[:, :], ALU.mult, ALU.mult,
                                                 accum_out=enc[:, t:t + 1]).then_inc(enc_ok, 1)
                if front:
                    dve.wait_ge(rr[0], 2 * jf + 2)
                    wait(dve, tx_ps, jf)
                    for t in range(TT):
                        last = dve.tensor_scalar(xn[:, t, :], xa[:, pf, t, :], mv[:, 0, t, 0:1], rstd[:, 0, t:t + 1],
                                                 ALU.subtract, ALU.mult)
                    last.then_inc(xn_ok, 1)
                if back:
                    dve.wait_ge(wo_ps, jb + 1)
                    dve.wait_ge(xb_in[pb], back[0] * 16 + 16)
                    dve.tensor_tensor(x1[:, :, :].rearrange("p t d -> p (t d)"), bank[B7][:, :],
                                      xb[:, pb, :, :].rearrange("p t d -> p (t d)"), ALU.add).then_inc(x1_ok, 1)
                    dve.wait_ge(x1_ok, jb + 1)
                    norm_stats(1, jb, x1)
                    dve.wait_ge(ln_mv[1], 4 * jb + 4)
                    for t in range(TT):
                        dve.scalar_tensor_tensor(scr2[:, t, :], x1[:, t, :], mv[:, 1, t, 0:1], wdec[:, :], ALU.subtract, ALU.mult,
                                                 accum_out=dec[:, t:t + 1]).then_inc(dec_ok, 1)
                if front:
                    rope(jf, 0)
                if back:
                    dve.wait_ge(rr[1], 2 * jb + 2)
                    dve.wait_ge(dec_ok, 4 * jb + 2)
                    dve.tensor_tensor(dec[:, :], dec[:, :], rstd[:, 1, :], ALU.mult).then_inc(dec_ok, 1)
                    dve.wait_ge(dec_ok, 4 * jb + 3)
                    dve.tensor_scalar(dec[:, :], dec[:, :], mbias[:, 0:1], None, ALU.add).then_inc(dec_ok, 1)
                    dve.wait_ge(dec_ok, 4 * jb + 4)
                    dve.wait_ge(e_ps, jb + 1)
                    for t in range(TT):
                        last = dve.scalar_tensor_tensor(x2[:, t, :], x1[:, t, :], dec[:, t:t + 1], bank[B6][:, 0:D], ALU.add, ALU.add)
                    last.then_inc(x2_ok, 1)
                    dve.wait_ge(x2_ok, jb + 1)
                    norm_stats(2, jb, x2)
                if front:
                    rope(jf, 1)
                    low_part(jf, 0)
                if back:
                    dve.wait_ge(rr[2], 2 * jb + 2)
                    wait(dve, sent[pb], back[0] * (16 * TT * TOPK))
                    for t in range(TT):
                        last = dve.tensor_scalar(rows[0][:, pb, t, 0:D], x2[:, t, :], mv[:, 2, t, 0:1], rstd[:, 2, t:t + 1],
                                                 ALU.subtract, ALU.mult)
                    last.then_inc(h3_ok, 1)
                if front:
                    keep_T(jf, front, 0, 0)
                    keep_T(jf, front, 0, 1)
                    low_part(jf, 1)
                if back:
                    wait_first(dve, sco_ok, jb + 1)
                    for t in range(TT):
                        dve.max(topv[:, t, :], score[:, t, :]).then_inc(ra_ok, 1)
                    wait_first(dve, ra_ok, 15 * jb + 2)
                    for t in range(TT):
                        dve.max_index(topi[:, t, :], topv[:, t, :], score[:, t, :]).then_inc(ra_ok, 1)
                    dve.tensor_tensor(ssum[:, :], topv[:, :, 0], topv[:, :, 1], ALU.add).then_inc(ra_ok, 1)
                    dve.wait_ge(ra_ok, 15 * jb + 4)
                    dve.tensor_copy(topf[:, :].rearrange("p (t k) -> p t k", k=TOPK), topi[:, :, 0:TOPK]).then_inc(ra_ok, 1)
                    dve.wait_ge(ra_ok, 15 * jb + 5)
                    dve.tensor_scalar(ssum[:, :], ssum[:, :], 1e-20, None, ALU.add).then_inc(ra_ok, 1)
                    dve.wait_ge(ra_ok, 15 * jb + 6)
                    dve.tensor_tensor(onehot[:, :, :], iota16[:, :].unsqueeze(1).to_broadcast([P, TT * TOPK, E]),
                                      topf[:, :].unsqueeze(2).to_broadcast([P, TT * TOPK, E]), ALU.is_equal).then_inc(ra_ok, 1)
                    dve.wait_ge(ra_ok, 15 * jb + 7)
                    dve.reciprocal(ssum[:, :], ssum[:, :]).then_inc(ra_ok, 1)
                    dve.wait_ge(ra_ok, 15 * jb + 8)
                    oh = onehot[:, :, :].rearrange("p (t k) e -> p t k e", k=TOPK)
                    dve.tensor_tensor(chosen[:, :, :], oh[:, :, 0, :], oh[:, :, 1, :], ALU.add).then_inc(ra_ok, 1)
                    dve.wait_ge(ra_ok, 15 * jb + 9)
                    for k in range(TOPK):
                        dve.scalar_tensor_tensor(rows[k][:, pb, :, D + 1], topv[:, :, k], ROUTE_SCALE, ssum[:, :],
                                                 ALU.mult, ALU.mult).then_inc(ra_ok, 1)
                    for k in range(TOPK):
                        dve.tensor_copy(rows[k][:, pb, :, D].bitcast(I32), idf[:, k, :]).then_inc(ra_ok, 1)
                    dve.wait_ge(ra_ok, 15 * jb + 14)
                    dve.tensor_scalar(idf[:, :, :], idf[:, :, :], float(T * TOPK), None, ALU.add).then_inc(ra_ok, 1)
                    dve.wait_ge(sg_ok, jb + 1)
                    dve.tensor_tensor(sgT[:, :], bank[B7][:, 0:T], sgT[:, :], ALU.mult).then_inc(hid_ok, 1)
                    dve.wait_ge(hid_ok, 2 * jb + 1)
                    dve.tensor_tensor(hidT[:, :], bank[B7][:, T:2 * T], sgT[:, :], ALU.mult).then_inc(hid_ok, 1)
                if front:
                    keep_T(jf, front, 1, 0)
                    keep_T(jf, front, 1, 1)
                    dve.wait_ge(c_ps, jf + 1)
                    wait(dve, o_ok, 2 * jf)
                    dve.tensor_copy(vsum[:, :], bank[FB][:, 0:GROUPS]).then_inc(c_ok, 1)
                if back:
                    dve.wait_ge(rk_ps, jb + 1)
                    dve.wait_ge(ra_ok, 15 * jb + 15)
                    dve.tensor_tensor(pose[:, :, :], bank[B6][:, 0:TT * E].rearrange("p (t e) -> p t e", t=TT),
                                      ebase[:, :].unsqueeze(1).to_broadcast([P, TT, E]), ALU.add).then_inc(rb_ok, 1)
                    dve.tensor_tensor(seen[:, :], seen[:, :], chosen[:, 0, :], ALU.add).then_inc(rb_ok, 1)
                    dve.wait_ge(rb_ok, 6 * jb + 2)
                    dve.tensor_tensor(seen[:, :], seen[:, :], chosen[:, 1, :], ALU.add).then_inc(rb_ok, 1)
                    pk = posp[:, :, :].rearrange("p (t k) e -> p t k e", k=TOPK)
                    for k in range(TOPK):
                        last = dve.tensor_tensor(pk[:, :, k, :], oh[:, :, k, :], pose[:, :, :], ALU.mult)
                    last.then_inc(rb_ok, 1)
                    dve.wait_ge(rb_ok, 6 * jb + 4)
                    dve.reduce_sum(posf[:, :], posp[:, :, :], AX.X).then_inc(rb_ok, 1)
                    dve.wait_ge(rb_ok, 6 * jb + 5)
                    dve.tensor_copy(posi[:, pb, :], posf[:, :]).then_inc(rb_ok, 1)
                    dve.wait_ge(dn_ps, jb + 1)
                    dve.tensor_tensor(acc[:, bass.ds(jb * (TT * D), TT * D)], bank[B7][:, :],
                                      x2[:, :, :].rearrange("p t d -> p (t d)"), ALU.add).then_inc(acc_ok, 1)

            pipeline(dve, step)

            dve.wait_ge(cnt_ps, 1)
            dve.tensor_copy(cnt[:, :], bank[B6][:, 0:E]).then_inc(pl_ok, 1)
            dve.wait_ge(pl_ok, 1)
            dve.tensor_scalar(cnt_i[:, 0, :], cnt[:, :], float(P - 1), None, ALU.add).then_inc(pl_ok, 1)
            dve.tensor_tensor(plan_i[0:1, 2 * P:2 * P + E], cnt[0:1, :], ebase[0:1, :], ALU.add).then_inc(plan_ok, 1)
            dve.wait_ge(pl_ok, 2)
            dve.tensor_single_scalar(cnt_i[:, 1, :], cnt_i[:, 0, :], 7, op=ALU.arith_shift_right).then_inc(pl_ok, 1)
            dve.wait_ge(pl_ok, 3)
            dve.tensor_copy(ntl[:, :], cnt_i[:, 1, :]).then_inc(pl_ok, 1)
            dve.wait_ge(pl_ok, 4)
            dve.tensor_tensor_scan(cum[:, :], onesf[:, :], ntl[:, :], 0.0, ALU.mult, ALU.add).then_inc(pl_ok, 1)
            dve.wait_ge(pl_ok, 5)
            dve.tensor_scalar(le[:, :], cum[:, :], sidx[:, 0:1], None, ALU.is_le).then_inc(pl_ok, 1)
            dve.wait_ge(pl_ok, 6)
            dve.reduce_sum(plan[:, 0:1], le[:, :], AX.X).then_inc(pl_ok, 1)
            dve.tensor_tensor(lep[:, :], le[:, :], ntl[:, :], ALU.mult).then_inc(pl_ok, 1)
            dve.wait_ge(pl_ok, 8)
            dve.reduce_sum(plan[:, 1:2], lep[:, :], AX.X).then_inc(pl_ok, 1)
            dve.wait_ge(pl_ok, 9)
            dve.tensor_tensor(plan[:, 2:3], sidx[:, :], plan[:, 1:2], ALU.subtract).then_inc(pl_ok, 1)
            dve.tensor_scalar(plan[:, 3:4], plan[:, 0:1], float(EROWS), None, ALU.mult).then_inc(pl_ok, 1)
            dve.tensor_scalar(plan[:, 5:6], plan[:, 0:1], float(E - 1), None, ALU.min).then_inc(pl_ok, 1)
            dve.wait_ge(pl_ok, 12)
            dve.scalar_tensor_tensor(plan[:, 4:5], plan[:, 2:3], float(P), plan[:, 3:4], ALU.mult, ALU.add).then_inc(pl_ok, 1)
            dve.wait_ge(plan_ps, 1)
            dve.tensor_copy(plan_i[0:1, 0:2 * P], bank[B6][0:1, 0:2 * P]).then_inc(plan_ok, 1)

            def expert(n, c, m):
                small = isinstance(n, int)
                if not small or 1 <= n <= SLOTS:
                    r = (c - 1) % 2
                    dve.wait_ge(esg_ok, n)
                    if not small or n >= 3:
                        dve.wait_ge(etd_ps, n - 2)
                    dve.tensor_tensor(ehd[:, r, :], bank[2 + r][:, M:2 * M], esg[:, r, :], ALU.mult).then_inc(ehd_ok, 1)
                if not small or 2 <= n <= SLOTS + 1:
                    r = (c - 2) % 2
                    dve.wait_ge(etd_ps, n - 1)
                    if not small or n >= 4:
                        dve.wait_ge(edn_ps, n - 3)
                    dve.tensor_copy(ehT[:, r, :], bank[4 + r][:, 0:P]).then_inc(ehT_ok, 1)
                if not small or n >= 3:
                    r, y = (c - 3) % XRING, (c - 3) % YRING
                    q = (n - 3) // YRING if small else m * 2 + (c - 3) // YRING
                    dve.wait_ge(edn_ps, n - 2)
                    wait(dve, ys_out[y], q * 16)
                    dve.tensor_scalar(ys[:, y, :], bank[6 + r % 2][:, 0:D], xs[:, r, D + 1:D + 2], None, ALU.mult).then_inc(ys_ok, 1)

            slots(dve, expert)

            with dve.Fori(0, NTILES // CRING) as m:
                for r in range(CRING):
                    dve.wait_ge(yp_in[r], m * 16 + 16)
                    a = acc[:, bass.ds((m * CRING + r) * D, D)]
                    dve.tensor_tensor(a, a, ypair[:, r, 0:D], ALU.add).then_inc(f1_ok, 1)
                    dve.wait_ge(f1_ok, m * CRING + r + 1)
                    dve.tensor_tensor(a, a, ypair[:, r, D:2 * D], ALU.add).then_inc(fin_ok, 1)

        @block.tensor
        def _(pe):
            pe.wait_ge(w_in, 16 * 14)
            pe.wait_ge(c_pool, 6)
            pe.wait_ge(c_dve, 2)

            def scores(j, b, a):
                wait(pe, sq_ok, 8 * j + a - 1)
                if a == 0:
                    pe.wait_ge(qkT_ok, 4 * j + 4)
                for h in range(2):
                    for kt in range(TT):
                        lo = 64 * h
                        last = pe.matmul(bank[2 * (a % 2) + h][:, kt * T:(kt + 1) * T],
                                         kT[lo:lo + 64, b[1], a, kt * P:(kt + 1) * P],
                                         qT[lo:lo + 64, b[1], a, :], start=True, stop=True)
                last.then_inc(s_ps, 1)

            def weighted(j, b, g):
                pe.wait_ge(sq_ok, 8 * j + 2 * g + 2)
                if g % 2 == 0:
                    wait(pe, o_ok, 2 * j + g // 2)
                for kt in range(TT):
                    for h in range(HPG):
                        head = HPG * g + h
                        last = pe.matmul(bank[PVB][32 * h:32 * h + 32, (g % 2) * T:(g % 2 + 1) * T],
                                         vaug[:, b[1], kt, head, :], sq[:, (head // 2) % 4, head % 2, kt, :],
                                         start=(kt == 0), stop=(kt == TT - 1))
                last.then_inc(pv_ps, 1)

            def project_qk(j, t):
                if t == 0:
                    pe.wait_ge(hT_ok, j + 1)
                else:
                    pe.wait_ge(ro_ok, 2 * j + 1)
                for k in range(KD):
                    last = pe.matmul(bank[FB][:, :], hT[:, k, t * P:(t + 1) * P], wqk[:, k, :], start=(k == 0), stop=(k == KD - 1))
                last.then_inc(qk_ps, 1)

            def transpose_qk(j, t, which):
                if which == 0:
                    pe.wait_ge(stk_ok, 6 * j + 3 * t + 3)
                if t == 0 and which == 0:
                    pe.wait_ge(v_ok, j + 1)
                else:
                    pe.wait_ge(qkT_ok, 4 * j + 2 * t + which)
                dst = bank[FB][:, :].bitcast(F16)
                for a in range(HEADS // 2):
                    h = which * HEADS + 2 * a
                    last = pe.transpose(dst[:, a * P:(a + 1) * P],
                                        stack[:, t, h:h + 2, :, :].rearrange("p h s d -> p (h s d)"), identh[:, :])
                last.then_inc(tqk_ps, 1)

            def step(att, back, front):
                if back:
                    jb, pb = num(back), back[1]
                    for t in range(TT):
                        pe.wait_ge(o_ok, 2 * jb + 2)
                        if t == 0:
                            wait(pe, rb_ok, 6 * jb)
                        else:
                            wait(pe, acc_ok, jb)
                        for g in range(GROUPS):
                            last = pe.transpose(bank[(B6, B7)[t]][:, g * P:(g + 1) * P], oT[:, g, t * P:(t + 1) * P], identf[:, :])
                        last.then_inc(to_ps, 1)
                if att:
                    ja = num(att)
                    scores(ja, att, 0)
                    scores(ja, att, 1)
                if back:
                    pe.wait_ge(wv_ok, TT * jb + TT)
                    for t in range(TT):
                        for k in range(KD):
                            last = pe.transpose(bank[B6][:, (t * KD + k) * P:(t * KD + k + 1) * P], wv[:, t, k * P:(k + 1) * P], identf[:, :])
                    last.then_inc(tw_ps, 1)
                if att:
                    scores(ja, att, 2)
                    scores(ja, att, 3)
                if front:
                    jf, pf = num(front), front[1]
                    pe.wait_ge(xn_ok, jf + 1)
                    wait(pe, c_ok, jf)
                    for t in range(TT):
                        for k in range(KD):
                            last = pe.transpose(bank[FB][:, (t * KD + k) * P:(t * KD + k + 1) * P], xn[:, t, k * P:(k + 1) * P], identf[:, :])
                    last.then_inc(tx_ps, 1)
                if back:
                    pe.wait_ge(wvT_ok, jb + 1)
                    for t in range(TT):
                        for k in range(KD):
                            last = pe.matmul(bank[B7][:, t * D:(t + 1) * D], wvT[:, k, t * P:(t + 1) * P], wo[:, k, :],
                                             start=(k == 0), stop=(k == KD - 1))
                    last.then_inc(wo_ps, 1)
                if att:
                    weighted(ja, att, 0)
                    scores(ja, att, 4)
                    scores(ja, att, 5)
                if front:
                    project_qk(jf, 0)
                if back:
                    pe.wait_ge(enc_ok, 2 * jb + 2)
                    for t in range(TT):
                        last = pe.matmul(bank[B6][:, t * P:(t + 1) * P], enc[:, t:t + 1].to_broadcast([P, P]), identf[:, :],
                                         start=True, stop=True)
                    last.then_inc(e_ps, 1)
                if att:
                    weighted(ja, att, 1)
                if front:
                    project_qk(jf, 1)
                if att:
                    scores(ja, att, 6)
                    scores(ja, att, 7)
                if front:
                    pe.wait_ge(ro_ok, 2 * jf + 2)
                    for t in range(TT):
                        for k in range(KD):
                            last = pe.matmul(bank[FB][:, t * D:(t + 1) * D], hT[:, k, t * P:(t + 1) * P], wv_w[:, k, :],
                                             start=(k == 0), stop=(k == KD - 1))
                    last.then_inc(v_ps, 1)
                if att:
                    weighted(ja, att, 2)
                if front:
                    transpose_qk(jf, 0, 0)
                    transpose_qk(jf, 0, 1)
                if back:
                    pe.wait_ge(h3_ok, jb + 1)
                    for t in range(TT):
                        for k in range(KD):
                            last = pe.transpose(bank[B7][:, (t * KD + k) * P:(t * KD + k + 1) * P],
                                                rows[0][:, pb, t, k * P:(k + 1) * P], identf[:, :])
                    last.then_inc(th_ps, 1)
                    pe.wait_ge(h3T_ok, jb + 1)
                    for t in range(TT):
                        for k in range(KD):
                            last = pe.matmul(bank[B6][:, t * E:(t + 1) * E], h3T[:, k, t * P:(t + 1) * P], gwT[:, k, :],
                                             start=(k == 0), stop=(k == KD - 1))
                    last.then_inc(ga_ps, 1)
                    for s in range(2):
                        for k in range(KD):
                            last = pe.matmul(bank[B7][:, s * T:(s + 1) * T], wsgu[:, k, s * M:(s + 1) * M], h3T[:, k, :],
                                             start=(k == 0), stop=(k == KD - 1))
                    last.then_inc(sh_ps, 1)
                if att:
                    weighted(ja, att, 3)
                if front:
                    transpose_qk(jf, 1, 0)
                    transpose_qk(jf, 1, 1)
                    pe.wait_ge(qkT_ok, 4 * jf + 4)
                    for g in range(GROUPS):
                        for kt in range(TT):
                            last = pe.matmul(bank[FB][:, g:g + 1],
                                             vaug[:, pf, kt, HPG * g:HPG * g + HPG, :].rearrange("p h d -> p (h d)"),
                                             onesf[:, 0:1], start=(kt == 0), stop=(kt == TT - 1))
                    last.then_inc(c_ps, 1)
                if back:
                    pe.wait_ge(ra_ok, 15 * jb + 10)
                    pe.wait_ge(sco_ok, jb + 1)
                    for t in range(TT):
                        dst = bank[B6][:, t * E:(t + 1) * E]
                        pe.matmul(dst, tri[:, :], chosen[:, t, :], start=True, stop=False)
                        for s in range(t):
                            pe.matmul(dst, onesb[:, :], chosen[:, s, :], start=False, stop=False)
                        last = pe.matmul(dst, onesb[:, :], seen[:, :], start=False, stop=True)
                    last.then_inc(rk_ps, 1)
                    pe.wait_ge(hid_ok, 2 * jb + 2)
                    for t in range(TT):
                        last = pe.matmul(bank[B7][:, t * D:(t + 1) * D], hidT[:, t * P:(t + 1) * P], wsd[:, :], start=True, stop=True)
                    last.then_inc(dn_ps, 1)

            pipeline(pe, step)

            pe.wait_ge(rb_ok, 6 * NB)
            pe.matmul(bank[B6][:, 0:E], onesb[:, :], seen[:, :], start=True, stop=True).then_inc(cnt_ps, 1)
            pe.wait_ge(pl_ok, 13)
            for i in range(2):
                last = pe.matmul(bank[B6][0:1, i * P:(i + 1) * P], plan[:, 4 + i:5 + i], identf[:, :], start=True, stop=True)
            last.then_inc(plan_ps, 1)
            pe.wait_ge(plan_ok, 2)
            pe.wait_ge(wE_in, 16 * 5)
            pe.wait_ge(acc_ok, NB)

            def expert_of(n):
                return pe.value_load(plan_i[0:1, bass.ds(n + P, 1)], min_val=0, max_val=E - 1)

            def expert(n, c, m):
                small = isinstance(n, int)
                if not small or n < SLOTS:
                    q = 1 if small else m + 1
                    pe.wait_ge(xs_in[c], q * 16)
                    if not small or n >= 2:
                        pe.wait_ge(exT_ok, n - 1)
                    for k in range(KD):
                        last = pe.transpose(bank[c % 2][:, k * P:(k + 1) * P], xs[:, c, k * P:(k + 1) * P], identf[:, :])
                    last.then_inc(etx_ps, 1)
                if not small or 1 <= n <= SLOTS:
                    r = (c - 1) % 2
                    e = expert_of(n - 1)
                    pe.wait_ge(exT_ok, n)
                    if not small or n >= 3:
                        pe.wait_ge(ehd_ok, n - 2)
                    for k in range(KD):
                        last = pe.matmul(bank[2 + r][:, 0:2 * M], exT[:, r, k, :], wgu[:, bass.ds(e * (KD * 2 * M) + k * 2 * M, 2 * M)],
                                         start=(k == 0), stop=(k == KD - 1))
                    last.then_inc(gu_ps, 1)
                if not small or 2 <= n <= SLOTS + 1:
                    r = (c - 2) % 2
                    pe.wait_ge(ehd_ok, n - 1)
                    if not small or n >= 4:
                        pe.wait_ge(ehT_ok, n - 3)
                    pe.transpose(bank[4 + r][:, 0:P], ehd[:, r, :], identf[:, :]).then_inc(etd_ps, 1)
                if not small or n >= 3:
                    r = (c - 3) % 2
                    e = expert_of(n - 3)
                    pe.wait_ge(ehT_ok, n - 2)
                    if not small or n >= 5:
                        pe.wait_ge(ys_ok, n - 4)
                    pe.matmul(bank[6 + r][:, 0:D], ehT[:, r, :], wdn[:, bass.ds(e * D, D)], start=True, stop=True).then_inc(edn_ps, 1)

            slots(pe, expert)


_INS = ["x", "ctx_1024", "L0_attn_ln_w", "L0_attn_ln_b", "L0_attn_w_q", "L0_attn_w_kv", "L0_attn_w_o", "L0_attn_theta",
        "L0_xattn_mlp_weight", "L0_xattn_mlp_bias", "L0_ffn_gate_w", "L0_ffn_w_gate", "L0_ffn_w_up", "L0_ffn_w_down",
        "L0_ffn_ws_gate", "L0_ffn_ws_up", "L0_ffn_ws_down"]


def kernel(**inputs):
    import concourse.bacc as bacc
    from concourse.bass_utils import run_bass_kernel_spmd

    nc = bacc.Bacc("TRN2", target_bir_lowering=False, num_devices=1)
    arrays, args = {}, []
    for name in _INS:
        a = np.ascontiguousarray(inputs[name])
        if name == "L0_attn_theta":
            a = a.reshape(1)
        if name == "L0_ffn_gate_w":
            a = np.ascontiguousarray(a.T)
        if name in ("L0_attn_ln_w", "L0_attn_ln_b"):
            a = np.ascontiguousarray(a.reshape(KD, P).T)
        arrays[f"in_{name}"] = a
        args.append(nc.dram_tensor(f"in_{name}", a.shape, mybir.dt.from_np(a.dtype), kind="ExternalInput").ap())
    args.append(nc.dram_tensor("out_0", (NB, T, D), F32, kind="ExternalOutput").ap())
    build(nc, *args)
    r = run_bass_kernel_spmd(nc, [arrays], core_ids=[0])
    return r.results[0]["out_0"]
```

```python
from contextlib import ExitStack

import numpy as np

import concourse.bass as bass
from concourse import mybir

F32 = mybir.dt.float32
F16 = mybir.dt.float16
BF16 = mybir.dt.bfloat16
I32 = mybir.dt.int32
U32 = mybir.dt.uint32
ALU = mybir.AluOpType
ACT = mybir.ActivationFunctionType
AX = mybir.AxisListType

P = 128
NB, T, D = 16, 256, 256
TT = T // P
KD = D // P
HEADS, HD = 16, 16
GROUPS = 4
HPG = HEADS // GROUPS
E, M, TOPK = 16, 128, 2
NTOK = NB * T
NTILES = NTOK // P
ROUTE_SCALE = 2.5
EPS = 1e-5

ROW = D + 2
EROWS = NTOK + P
SLOTS = (NTOK * TOPK) // P + E
NULLS = SLOTS - (NTOK * TOPK) // P
XROWS = E * EROWS + NULLS * P
YROWS = NTOK * TOPK
SKIP_ROW = 1 << 20

WE = KD * 2 * M + D
FROWS = 8
FDMAS = E // FROWS

MAGIC = 1.5 * 2.0 ** 23


def mel_base():
    f = np.float32
    top = f(2595.0 * np.log10(1.0 + 4000.0 / 200.0))
    lin = np.array([top * f(i / (HD // 2 - 1)) for i in range(HD // 2)], f)
    mel = np.power(10.0, (lin / f(2595.0)).astype(np.float64)).astype(f) - f(1.0)
    return [float(v) for v in (f(200.0) * mel / f(1000.0)).astype(f)]


def two_pi_parts():
    c1 = 6.28125
    c2 = float(np.round((2 * np.pi - c1) * 2.0 ** 18) / 2.0 ** 18)
    return c1, c2, float(np.float32(2 * np.pi - c1 - c2))


def build(nc, x, ctx_in, ln_w, ln_b, w_q, w_kv, w_o, theta, mlp_w, mlp_b,
          gate_wT, w_gate, w_up, w_down, ws_gate, ws_up, ws_down, out):
    with ExitStack() as ctx:
        def sb(name, shape, dt=F32):
            return ctx.enter_context(nc.sbuf_tensor(name, shape, dt))

        def sem(name):
            return ctx.enter_context(nc.semaphore(name))

        disp = nc.dram_tensor("dispatch", [XROWS, ROW], F32, kind="Internal").ap()
        yexp = nc.dram_tensor("expert_out", [YROWS, D], F32, kind="Internal").ap()

        wqk = sb("wqk", [P, KD, 2 * D])
        wv_w = sb("wv_w", [P, KD, D])
        wo = sb("wo", [P, KD, D])
        wsgu = sb("wsgu", [P, KD, 2 * M])
        wsd = sb("wsd", [P, D])
        gwT = sb("gwT", [P, KD, E])
        wex = sb("wex", [P, E * WE])
        lnw_c = sb("lnw_c", [P, KD])
        lnb_c = sb("lnb_c", [P, KD])
        wenc = sb("wenc", [P, D])
        wdec = sb("wdec", [P, D])
        mbias = sb("mbias", [P, 1])
        theta_c = sb("theta_c", [P, 1])
        identf = sb("identf", [P, P])
        identh = sb("identh", [P, P], F16)
        tri = sb("tri", [P, P], BF16)
        onesb = sb("onesb", [P, P], BF16)
        onesf = sb("onesf", [P, E])
        iota16 = sb("iota16", [P, E])
        ebase = sb("ebase", [P, E])
        ebase_i = sb("ebase_i", [P, E], I32)
        iota_i = sb("iota_i", [P, E], I32)
        tok_i = sb("tok_i", [P, TT], I32)
        tokf = sb("tokf", [P, TT])
        fidx_i = sb("fidx_i", [P, 2, FDMAS], I32)
        fidx = sb("fidx", [P, 2, FDMAS])
        fmask = sb("fmask", [P, FDMAS, E])
        fprod = sb("fprod", [P, FDMAS, E])
        fbase = sb("fbase", [P, FDMAS])
        fcnt = sb("fcnt", [P, FDMAS])
        frow = sb("frow", [P, FDMAS], I32)
        idi = sb("idi", [P, TOPK, TT], I32)
        idf = sb("idf", [P, TOPK, TT])
        freq = sb("freq", [P, HD // 2])
        ang = sb("ang", [P, TT, HD // 2])
        turns = sb("turns", [P, TT, HD // 2])
        angc = sb("angc", [P, TT, HD // 2])
        wrap = sb("wrap", [P, TT, HD // 2])
        cosr = sb("cosr", [P, TT, HD // 2, 2])
        sinr = sb("sinr", [P, TT, HD // 2, 2])
        halfneg = sb("halfneg", [P, 2])
        filler = sb("filler", [P, ROW])

        xa = sb("xa", [P, 2, TT, D])
        xb = sb("xb", [P, 2, TT, D])
        cx = sb("cx", [P, 2, TT, D])
        xn = sb("xn", [P, TT, D])
        hT = sb("hT", [P, KD, T])
        rt1 = sb("rt1", [P, TT, 2 * D])
        rt2 = sb("rt2", [P, TT, 2 * D])
        rot = sb("rot", [P, TT, 2 * D])
        stack = sb("stack", [P, TT, 2 * HEADS, 4, HD], F16)
        qT = sb("qT", [P, 2, HEADS // 2, T], F16)
        kT = sb("kT", [P, 2, HEADS // 2, T], F16)
        vaug = sb("vaug", [P, 2, TT, HEADS, 32])
        sq = sb("sq", [P, 4, 2, TT, T])
        vpair = sb("vpair", [P, HEADS, 32])
        vsum = sb("vsum", [P, GROUPS])
        oT = sb("oT", [P, GROUPS, T])
        rec = sb("rec", [P, TT, HEADS])
        wv = sb("wv", [P, TT, D])
        wvT = sb("wvT", [P, KD, T])
        x1 = sb("x1", [P, TT, D])
        x2 = sb("x2", [P, TT, D])
        scr = sb("scr", [P, TT, D])
        scr2 = sb("scr2", [P, TT, D])
        enc = sb("enc", [P, TT])
        dec = sb("dec", [P, TT])
        h3T = sb("h3T", [P, KD, T])
        rows = [sb(f"rows{k}", [P, 2, TT, ROW]) for k in range(TOPK)]
        sgT = sb("sgT", [P, T])
        hidT = sb("hidT", [P, T])
        stats = sb("stats", [P, 3, TT, 6])
        mv = sb("mv", [P, 3, TT, 2])
        vtmp = sb("vtmp", [P, 3, TT])
        rstd = sb("rstd", [P, 3, TT])
        score = sb("score", [P, TT, E])
        topv = sb("topv", [P, TT, 8])
        topi = sb("topi", [P, TT, 8], U32)
        topf = sb("topf", [P, TT * TOPK])
        ssum = sb("ssum", [P, TT])
        onehot = sb("onehot", [P, TT * TOPK, E])
        chosen = sb("chosen", [P, TT, E], BF16)
        seen = sb("seen", [P, E], BF16)
        pose = sb("pose", [P, TT, E])
        posp = sb("posp", [P, TT * TOPK, E])
        posf = sb("posf", [P, TT * TOPK])
        posi = sb("posi", [P, 2, TT * TOPK], I32)
        acc = sb("acc", [P, NTILES * D])

        sidx_i = sb("sidx_i", [P, 1], I32)
        sidx = sb("sidx", [P, 1])
        cnt = sb("cnt", [P, E])
        cnt_i = sb("cnt_i", [P, 2, E], I32)
        ntl = sb("ntl", [P, E])
        cum = sb("cum", [P, E])
        le = sb("le", [P, E])
        lep = sb("lep", [P, E])
        plan = sb("plan", [P, 8])
        plan_i = sb("plan_i", [1, 2 * P + 4], I32)

        WLOADS = 7
        ANGLES = 15
        FILL_AT = 4
        XRING, YRING = 8, 4
        sq_flat = sq[:, :, :, :, :].rearrange("p a b c d -> p (a b c d)")
        vaug_flat = vaug[:, :, :, :, :].rearrange("p a b c d -> p (a b c d)")
        at = XRING * ROW
        xs = sq_flat[:, 0:at].rearrange("p (r w) -> p r w", r=XRING)
        exT = sq_flat[:, at:at + 2 * D].rearrange("p (r k t) -> p r k t", r=2, k=KD)
        at += 2 * D
        esg = sq_flat[:, at:at + 2 * M].rearrange("p (r m) -> p r m", r=2)
        at += 2 * M
        ehd = sq_flat[:, at:at + 2 * M].rearrange("p (r m) -> p r m", r=2)
        at += 2 * M
        ehT = sq_flat[:, at:at + 2 * P].rearrange("p (r m) -> p r m", r=2)
        fzero = sq_flat[:, 0:FROWS * ROW].rearrange("p (r w) -> p r w", r=FROWS)
        ys = vaug_flat[:, 0:YRING * D].rearrange("p (r d) -> p r d", r=YRING)
        CRING = 4
        ypair = stack[:, :, :, :, :].rearrange("p a b c d -> p (a b c d)").bitcast(F32)\
            .rearrange("p (r w) -> p r w", r=CRING)

        bank = [ctx.enter_context(nc.psum_tensor(f"bank{i}", [P, 512], F32)) for i in range(8)]
        PVB, FB, B6, B7 = 4, 5, 6, 7

        th_in = sem("th_in")
        ln_in = sem("ln_in")
        wqk_in = sem("wqk_in")
        wv_in = sem("wv_in")
        wo_in = sem("wo_in")
        ws_in = sem("ws_in")
        fz_ok = sem("fz_ok")
        wE_in = sem("wE_in")
        c_pool = sem("c_pool")
        c_dve = sem("c_dve")
        c_act = sem("c_act")
        f_dve = sem("f_dve")
        null_in = sem("null_in")
        xa_in = [sem(f"xa_in{p}") for p in range(2)]
        xb_in = [sem(f"xb_in{p}") for p in range(2)]
        cx_in = [sem(f"cx_in{p}") for p in range(2)]
        ln_mv = [sem(f"ln_mv{n}") for n in range(3)]
        rr = [sem(f"rr{n}") for n in range(3)]
        xn_ok = sem("xn_ok")
        tx_ps = sem("tx_ps")
        hT_ok = sem("hT_ok")
        qk_ps = sem("qk_ps")
        ro_ok = sem("ro_ok")
        rot_ok = sem("rot_ok")
        hi_ok = sem("hi_ok")
        stk_ok = sem("stk_ok")
        v_ps = sem("v_ps")
        v_ok = sem("v_ok")
        tqk_ps = sem("tqk_ps")
        qkT_ok = sem("qkT_ok")
        vp_ok = sem("vp_ok")
        c_ps = sem("c_ps")
        c_ok = sem("c_ok")
        s_ps = sem("s_ps")
        sq_ok = sem("sq_ok")
        pv_ps = sem("pv_ps")
        o_ok = sem("o_ok")
        to_ps = sem("to_ps")
        rec_ok = sem("rec_ok")
        wv_ok = sem("wv_ok")
        tw_ps = sem("tw_ps")
        wvT_ok = sem("wvT_ok")
        wo_ps = sem("wo_ps")
        x1_ok = sem("x1_ok")
        enc_ok = sem("enc_ok")
        e_ps = sem("e_ps")
        dec_ok = sem("dec_ok")
        x2_ok = sem("x2_ok")
        h3_ok = sem("h3_ok")
        th_ps = sem("th_ps")
        h3T_ok = sem("h3T_ok")
        ga_ps = sem("ga_ps")
        sco_ok = sem("sco_ok")
        sh_ps = sem("sh_ps")
        sg_ok = sem("sg_ok")
        hid_ok = sem("hid_ok")
        ra_ok = sem("ra_ok")
        rk_ps = sem("rk_ps")
        rb_ok = sem("rb_ok")
        dn_ps = sem("dn_ps")
        acc_ok = sem("acc_ok")
        copy_ok = sem("copy_ok")
        sent = [sem(f"sent{p}") for p in range(2)]
        cnt_ps = sem("cnt_ps")
        pl_ok = sem("pl_ok")
        plan_ps = sem("plan_ps")
        plan_ok = sem("plan_ok")
        fill_in = sem("fill_in")
        xs_in = [sem(f"xs_in{r}") for r in range(XRING)]
        etx_ps = sem("etx_ps")
        exT_ok = sem("exT_ok")
        gu_ps = sem("gu_ps")
        esg_ok = sem("esg_ok")
        ehd_ok = sem("ehd_ok")
        etd_ps = sem("etd_ps")
        ehT_ok = sem("ehT_ok")
        edn_ps = sem("edn_ps")
        ys_ok = sem("ys_ok")
        ys_out = [sem(f"ys_out{r}") for r in range(YRING)]
        yp_in = [sem(f"yp_in{r}") for r in range(CRING)]
        f1_ok = sem("f1_ok")
        fin_ok = sem("fin_ok")
        out_done = sem("out_done")
        passed = {nc.vector.engine: sem("passed_dve"), nc.gpsimd.engine: sem("passed_pool")}

        block = ctx.enter_context(nc.Block())

        def wait(eng, s, value):
            if not (isinstance(value, int) and value <= 0):
                eng.wait_ge(s, value)

        def wait_first(eng, s, value):
            wait(eng, s, value)
            if not isinstance(value, int):
                eng.sem_inc(passed[eng.engine], 1)

        def num(b):
            return b[0] * 2 + b[1]

        def pipeline(eng, step):
            step(None, None, None, (0, 0))
            step(None, None, (0, 0), (0, 1))
            step((0, 0), None, (0, 1), (1, 0))
            step((0, 1), (0, 0), (1, 0), (1, 1))
            with eng.Fori(0, NB // 2 - 2) as m:
                step((m + 1, 0), (m, 1), (m + 1, 1), (m + 2, 0))
                step((m + 1, 1), (m + 1, 0), (m + 2, 0), (m + 2, 1))
            u = NB // 2 - 1
            step((u, 0), (u - 1, 1), (u, 1), None)
            step((u, 1), (u, 0), None, None)
            step(None, (u, 1), None, None)

        def slots(eng, step):
            for n in range(XRING):
                step(n, n, None)
            with eng.Fori(1, SLOTS // XRING) as m:
                for c in range(XRING):
                    step(m * XRING + c, c, m)
            for n in range(SLOTS, SLOTS + 3):
                step(n, n - SLOTS, None)

        def read_plan(eng, at, count, top):
            return nc.values_load_multi_w_load_instructions(
                plan_i[0:1, bass.ds(at, count)], engines=[eng.engine], min_val=0, max_val=top,
                skip_runtime_bounds_check_because="the plan clamps the expert, and an expert's tiles end within its rows")[1]

        xv = x.rearrange("b (t p) d -> b p t d", p=P)
        cv = ctx_in.rearrange("b (t p) d -> b p t d", p=P)
        
        def first(b):
            return b is not None and isinstance(b[0], int) and b == (0, 0)

        @block.sync
        def _(sp):
            def load_x(j, b):
                wait(sp, xn_ok, j - 1)
                sp.dma_start(xa[:, b[1], :, :], xv[bass.ds(j, 1), :, :, :].rearrange("o p t d -> p (o t) d")).then_inc(xa_in[b[1]], 16)

            def load_back(j, b):
                wait(sp, x1_ok, j - 1)
                sp.dma_start(xb[:, b[1], :, :], xv[bass.ds(j, 1), :, :, :].rearrange("o p t d -> p (o t) d")).then_inc(xb_in[b[1]], 16)
                sp.dma_start(cx[:, b[1], :, :], cv[bass.ds(j, 1), :, :, :].rearrange("o p t d -> p (o t) d")).then_inc(cx_in[b[1]], 16)

            load_x(0, (0, 0))
            sp.dma_start(wqk[:, :, 0:D], w_q.rearrange("(k p) n -> p k n", p=P)).then_inc(wqk_in, 16)
            sp.dma_start(wqk[:, :, D:2 * D], w_kv[:, 0:D].rearrange("(k p) n -> p k n", p=P)).then_inc(wqk_in, 16)
            load_x(1, (0, 1))
            sp.dma_start(wo[:, :, :], w_o.rearrange("(k p) n -> p k n", p=P)).then_inc(wo_in, 16)
            sp.dma_start(wenc[:, :], mlp_w[0, 0:D].partition_broadcast(P)).then_inc(ws_in, 16)
            sp.dma_start(wdec[:, :], mlp_w[0, D:2 * D].partition_broadcast(P)).then_inc(ws_in, 16)
            sp.dma_start(mbias[:, :], mlp_b.partition_broadcast(P)).then_inc(ws_in, 16)
            sp.dma_start(gwT[:, :, :], gate_wT.rearrange("(k p) e -> p k e", p=P)).then_inc(ws_in, 16)
            sp.dma_start(wsgu[:, :, 0:M], ws_gate.rearrange("(k p) m -> p k m", p=P)).then_inc(ws_in, 16)
            sp.dma_start(wsgu[:, :, M:2 * M], ws_up.rearrange("(k p) m -> p k m", p=P)).then_inc(ws_in, 16)
            sp.dma_start(wsd[:, :], ws_down).then_inc(ws_in, 16)
            for i in range(2):
                load_back(i, (0, i))
                load_x(i + 2, (1, i))
            with sp.Fori(0, NB // 2 - 2) as m:
                for p in range(2):
                    load_x(m * 2 + p + 4, (m + 2, p))
                    load_back(m * 2 + p + 2, (m + 1, p))
            for p in range(2):
                load_back(NB - 2 + p, (NB // 2 - 1, p))

            sp.wait_ge(plan_ok, 2)
            sp.wait_ge(fill_in, 16 * FDMAS)
            sp.wait_ge(null_in, 16)
            for p in range(2):
                sp.wait_ge(sent[p], 16 * TT * TOPK * (NB // 2))
            sp.wait_ge(pv_ps, GROUPS * NB)

            first_rows = []

            def load_slot(n, c, m):
                if isinstance(n, int) and n >= SLOTS:
                    return
                if c == 0:
                    first_rows[:] = read_plan(sp, n, XRING, XROWS - P)
                q = n // YRING if isinstance(n, int) else m * 2 + c // YRING
                wait(sp, ys_out[c % YRING], (q - 1) * 16)
                sp.dma_start(xs[:, c, :], disp[bass.ds(first_rows[c], P), :]).then_inc(xs_in[c], 16)

            slots(sp, load_slot)

            for r in range(YRING):
                sp.wait_ge(ys_out[r], 16 * SLOTS // YRING)
            yv = yexp.rearrange("(n k) d -> n (k d)", k=TOPK)
            for r in range(CRING):
                sp.dma_start(ypair[:, r, :], yv[r * P:(r + 1) * P, :]).then_inc(yp_in[r], 16)
            with sp.Fori(0, NTILES // CRING - 1) as m:
                for r in range(CRING):
                    sp.wait_ge(fin_ok, m * CRING + r + 1)
                    sp.dma_start(ypair[:, r, :], yv[bass.ds((m * CRING + r + CRING) * P, P), :]).then_inc(yp_in[r], 16)
            sp.wait_ge(out_done, 16 * NTILES)

        @block.gpsimd
        def _(pool):
            pool.memset(identf[:, :], 0.0).then_inc(c_pool, 1)
            pool.memset(identh[:, :], 0.0).then_inc(c_pool, 1)
            pool.memset(tri[:, :], 1.0).then_inc(c_pool, 1)
            pool.wait_ge(c_pool, 3)
            pool.affine_select(out=identf[:, :], in_=identf[:, :], compare_op=ALU.not_equal, fill=1.0,
                               base=0, pattern=[[-1, P]], channel_multiplier=1).then_inc(c_pool, 1)
            pool.affine_select(out=identh[:, :], in_=identh[:, :], compare_op=ALU.not_equal, fill=1.0,
                               base=0, pattern=[[-1, P]], channel_multiplier=1).then_inc(c_pool, 1)
            pool.affine_select(out=tri[:, :], in_=tri[:, :], compare_op=ALU.is_gt, fill=0.0,
                               base=0, pattern=[[1, P]], channel_multiplier=-1).then_inc(c_pool, 1)
            pool.iota(iota_i[:, :], [[1, E]], base=0, channel_multiplier=0).then_inc(c_pool, 1)
            pool.iota(ebase_i[:, :], [[EROWS, E]], base=0, channel_multiplier=0).then_inc(c_pool, 1)
            pool.iota(tok_i[:, :], [[P, TT]], base=0, channel_multiplier=1).then_inc(c_pool, 1)
            pool.iota(idi[:, :, :], [[1, TOPK], [P * TOPK, TT]], base=0, channel_multiplier=TOPK).then_inc(c_pool, 1)
            pool.iota(filler[:, D:D + 1].bitcast(I32), [[0, 1]], base=SKIP_ROW, channel_multiplier=0).then_inc(c_pool, 1)
            pool.iota(sidx_i[:, :], [[0, 1]], base=0, channel_multiplier=1).then_inc(c_pool, 1)
            pool.iota(fidx_i[:, 0, :], [[P, FDMAS]], base=0, channel_multiplier=1).then_inc(c_pool, 1)

            def power(n, j, a, b):
                wait_first(pool, ln_mv[n], 4 * j + 4)
                pool.tensor_scalar(vtmp[:, n, :], mv[:, n, :, 1], a, b, ALU.mult, ALU.add).then_inc(rr[n], 1)
                pool.wait_ge(rr[n], 2 * j + 1)
                pool.tensor_tensor(rstd[:, n, :], vtmp[:, n, :], halfneg[:, :], ALU.pow).then_inc(rr[n], 1)

            def rotate(j, t):
                pool.wait_ge(ro_ok, 2 * j + t + 1)
                wait(pool, stk_ok, 6 * j + 3 * t - 5)
                pool.tensor_tensor(rot[:, t, :], rt1[:, t, :], rt2[:, t, :], ALU.add).then_inc(rot_ok, 1)

            pool.wait_ge(c_dve, 1)

            def step(att, back, front, nxt):
                if att is None and front is None and nxt is None:
                    pool.wait_ge(pv_ps, GROUPS * NB)
                    pool.memset(fzero[:, :, :], 0.0).then_inc(fz_ok, 1)
                    pool.wait_ge(fz_ok, 1)
                    pool.iota(fzero[:, :, D].bitcast(I32), [[0, FROWS]], base=SKIP_ROW, channel_multiplier=0).then_inc(fz_ok, 1)
                if front:
                    rotate(num(front), 0)
                if back:
                    power(1, num(back), 1.0, EPS)
                if front:
                    rotate(num(front), 1)
                if back:
                    power(2, num(back), 1.0, EPS)
                if front:
                    j, p = num(front), front[1]
                    pool.wait_ge(v_ok, j + 1)
                    wait(pool, c_ps, j)
                    pool.tensor_tensor(vpair[:, :, 0:HD], vaug[:, p, 0, :, 0:HD], vaug[:, p, 1, :, 0:HD], ALU.add).then_inc(vp_ok, 1)
                if nxt:
                    power(0, num(nxt), 1.0 + EPS, EPS * EPS)
                if back:
                    j, p = num(back), back[1]
                    wait_first(pool, h3_ok, j + 1)
                    for t in range(TT):
                        last = pool.tensor_scalar(rows[1][:, p, t, 0:D], rows[0][:, p, t, 0:D], 1.0, 0.0, ALU.mult, ALU.add)
                    last.then_inc(copy_ok, 1)
                    pool.wait_ge(copy_ok, j + 1)
                    pool.wait_ge(ra_ok, 15 * j + 15)
                    wait_first(pool, rb_ok, 6 * j + 6)
                    for t in range(TT):
                        for k in range(TOPK):
                            i = t * TOPK + k
                            pool.indirect_dma_start(
                                disp, bass.IndirectOffsetOnAxis(ap=posi[:, p, i:i + 1].bitcast(U32), axis=0),
                                rows[k][:, p, t, :], None).then_inc(sent[p], 16)

            pipeline(pool, step)

            pool.wait_ge(fz_ok, 2)
            pool.wait_ge(pl_ok, FILL_AT)
            words = disp.rearrange("r (w o) -> (r w) o", o=1)
            for i in range(FDMAS):
                pool.indirect_dma_start(
                    words, bass.IndirectOffsetOnAxis(ap=frow[:, i:i + 1].bitcast(U32), axis=0),
                    fzero[:, :, :].rearrange("p r w -> p (r w)"), None).then_inc(fill_in, 16)

            def send(n, c, m):
                if isinstance(n, int) and n < 3:
                    return
                wait_first(pool, ys_ok, n - 2)
                r, y = (c - 3) % XRING, (c - 3) % YRING
                pool.indirect_dma_start(
                    yexp, bass.IndirectOffsetOnAxis(ap=xs[:, r, D:D + 1].bitcast(U32), axis=0),
                    ys[:, y, :], None, bounds_check=YROWS - 1, oob_is_err=False).then_inc(ys_out[y], 16)

            slots(pool, send)

        @block.scalar
        def _(act):
            act.dma_start(theta_c[:, :], theta.partition_broadcast(P)).then_inc(th_in, 16)
            act.dma_start(lnw_c[:, :], ln_w).then_inc(ln_in, 16)
            act.dma_start(lnb_c[:, :], ln_b).then_inc(ln_in, 16)
            act.dma_start(wv_w[:, :, :], w_kv[:, D:2 * D].rearrange("(k p) n -> p k n", p=P)).then_inc(wv_in, 16)
            act.wait_ge(c_dve, ANGLES)
            act.activation(sinr[:, :, :, 1], ang[:, :, :], ACT.Sin).then_inc(c_act, 1)
            act.activation(cosr[:, :, :, 0], angc[:, :, :], ACT.Sin).then_inc(c_act, 1)
            act.activation(cosr[:, :, :, 1], angc[:, :, :], ACT.Sin).then_inc(c_act, 1)
            act.activation(sinr[:, :, :, 0], ang[:, :, :], ACT.Sin, scale=-1.0).then_inc(c_act, 1)
            act.preload_act_table_set("sigmoid_and_others")

            def load_experts():
                we = wex[:, :].rearrange("p (e n) -> p e n", e=E)
                for k in range(KD):
                    at = k * 2 * M
                    act.dma_start(we[:, :, at:at + M], w_gate[:, k * P:(k + 1) * P, :].rearrange("e p m -> p e m")).then_inc(wE_in, 16)
                    act.dma_start(we[:, :, at + M:at + 2 * M], w_up[:, k * P:(k + 1) * P, :].rearrange("e p m -> p e m")).then_inc(wE_in, 16)
                act.dma_start(we[:, :, KD * 2 * M:WE], w_down.rearrange("e p n -> p e n")).then_inc(wE_in, 16)
                act.wait_ge(c_pool, 11)
                act.wait_ge(c_dve, 1)
                act.dma_start(disp[E * EROWS:XROWS, :].rearrange("(n p) w -> p n w", p=P),
                              filler[:, :].unsqueeze(1).to_broadcast([P, NULLS, ROW])).then_inc(null_in, 16)

            def squares(j, a):
                act.wait_ge(s_ps, 8 * j + a + 1)
                g = a // 2
                wait(act, pv_ps, GROUPS * j + g - 1)
                for b in range(2):
                    src = bank[2 * (a % 2) + b]
                    last = act.activation(sq[:, a % 4, b, :, :].rearrange("p a b -> p (a b)"), src[:, :],
                                          ACT.Square, scale=HD ** -0.5, bias=1.0)
                last.then_inc(sq_ok, 1)

            def attended(j, b, h):
                act.wait_ge(pv_ps, GROUPS * j + 2 * h + 2)
                if h == 0:
                    act.wait_ge(c_ok, j + 1)
                    wait(act, to_ps, TT * j)
                for g in range(2):
                    last = act.activation(oT[:, 2 * h + g, :], bank[PVB][:, g * T:(g + 1) * T], ACT.Identity,
                                          bias=vsum[:, 2 * h + g:2 * h + g + 1])
                last.then_inc(o_ok, 1)

            def high_part(j, t):
                act.wait_ge(rot_ok, 2 * j + t + 1)
                wait(act, tqk_ps, 4 * j + 2 * t - 2)
                act.activation(stack[:, t, :, 0, :], rot[:, t, :].rearrange("p (h d) -> p h d", d=HD),
                               ACT.Copy).then_inc(hi_ok, 1)

            def step(att, back, front, nxt):
                ja = num(att) if att else None
                if front:
                    jf = num(front)
                    if first(front):
                        act.wait_ge(ln_in, 32)
                    act.wait_ge(tx_ps, jf + 1)
                    wait(act, v_ps, jf)
                    for k in range(KD):
                        last = act.activation(hT[:, k, :].rearrange("p (t c) -> p t c", t=TT),
                                              bank[FB][:, :].rearrange("p (t k c) -> p k t c", t=TT, k=KD)[:, k, :, :],
                                              ACT.Identity, scale=lnw_c[:, k:k + 1], bias=lnb_c[:, k:k + 1])
                    last.then_inc(hT_ok, 1)
                if first(att):
                    load_experts()
                if att:
                    squares(ja, 0)
                if back:
                    jb = num(back)
                    act.wait_ge(tw_ps, jb + 1)
                    wait(act, wo_ps, jb)
                    act.activation(wvT[:, :, :].rearrange("p k (t c) -> p t k c", t=TT),
                                   bank[B6][:, :].rearrange("p (t k c) -> p t k c", t=TT, k=KD), ACT.Copy).then_inc(wvT_ok, 1)
                if att:
                    squares(ja, 1)
                if front:
                    high_part(jf, 0)
                if att:
                    squares(ja, 2)
                    squares(ja, 3)
                if front:
                    high_part(jf, 1)
                    act.wait_ge(v_ps, jf + 1)
                    wait(act, pv_ps, GROUPS * (jf - 1))
                    act.activation(vaug[:, front[1], :, :, 0:HD].rearrange("p t h d -> p (t h) d"),
                                   bank[FB][:, :].rearrange("p (a d) -> p a d", d=HD), ACT.Copy).then_inc(v_ok, 1)
                if att:
                    squares(ja, 4)
                    squares(ja, 5)
                    attended(ja, att, 0)
                    squares(ja, 6)
                if back:
                    act.wait_ge(th_ps, jb + 1)
                    wait(act, sh_ps, jb)
                    act.activation(h3T[:, :, :].rearrange("p k (t c) -> p t k c", t=TT),
                                   bank[B7][:, :].rearrange("p (t k c) -> p t k c", t=TT, k=KD), ACT.Copy).then_inc(h3T_ok, 1)
                if att:
                    squares(ja, 7)
                if back:
                    act.wait_ge(ga_ps, jb + 1)
                    wait(act, ra_ok, 15 * jb)
                    act.activation(score[:, :, :].rearrange("p t e -> p (t e)"), bank[B6][:, 0:TT * E], ACT.Sigmoid).then_inc(sco_ok, 1)
                    act.wait_ge(sh_ps, jb + 1)
                    wait(act, hid_ok, 2 * jb)
                    act.activation(sgT[:, :], bank[B7][:, 0:T], ACT.Sigmoid).then_inc(sg_ok, 1)
                if att:
                    attended(ja, att, 1)

            pipeline(act, step)

            def expert(n, c, m):
                small = isinstance(n, int)
                if not small or n < SLOTS:
                    act.wait_ge(etx_ps, n + 1)
                    if not small or n >= 2:
                        act.wait_ge(gu_ps, n - 1)
                    act.activation(exT[:, c % 2, :, :].rearrange("p k t -> p (k t)"), bank[c % 2][:, 0:D], ACT.Copy).then_inc(exT_ok, 1)
                if not small or 1 <= n <= SLOTS:
                    r = (c - 1) % 2
                    act.wait_ge(gu_ps, n)
                    if not small or n >= 3:
                        act.wait_ge(ehd_ok, n - 2)
                    act.activation(esg[:, r, :], bank[2 + r][:, 0:M], ACT.Silu).then_inc(esg_ok, 1)

            act.wait_ge(pv_ps, GROUPS * NB)
            slots(act, expert)

            with act.Fori(0, NTILES) as m:
                act.wait_ge(fin_ok, m + 1)
                act.dma_start(out.rearrange("b t d -> (b t) d")[bass.ds(m * P, P), :],
                              acc[:, bass.ds(m * D, D)]).then_inc(out_done, 16)

        @block.vector
        def _(dve):
            dve.memset(filler[:, 0:D], 0.0)
            dve.memset(filler[:, D + 1:D + 2], 0.0)
            dve.memset(seen[:, :], 0.0)
            dve.memset(onesb[:, :], 1.0)
            dve.memset(onesf[:, :], 1.0)
            dve.memset(vaug[:, :, :, :, HD + 1:32].rearrange("p a t h d -> p (a t h) d"), 0.0)
            dve.memset(vaug[:, :, :, :, HD:HD + 1].rearrange("p a t h d -> p (a t h) d"), 1.0)
            dve.memset(vpair[:, :, HD + 1:32], 0.0)
            dve.memset(vpair[:, :, HD:HD + 1], float(TT))
            dve.memset(halfneg[:, :], -0.5).then_inc(c_dve, 1)
            dve.wait_ge(c_pool, 13)
            dve.tensor_copy(iota16[:, :], iota_i[:, :])
            dve.tensor_copy(ebase[:, :], ebase_i[:, :])
            dve.tensor_copy(idf[:, :, :], idi[:, :, :])
            dve.tensor_copy(sidx[:, :], sidx_i[:, :])
            dve.tensor_single_scalar(fidx_i[:, 1, :], fidx_i[:, 0, :], 4, op=ALU.arith_shift_right).then_inc(f_dve, 1)
            dve.tensor_copy(tokf[:, :], tok_i[:, :])
            for i, v in enumerate(mel_base()):
                last = dve.memset(freq[:, i:i + 1], v)
            last.then_inc(c_dve, 1)
            dve.wait_ge(th_in, 16)
            dve.tensor_scalar(theta_c[:, :], theta_c[:, :], float(np.float32(1.0) / np.float32(220.0)), None, ALU.mult).then_inc(c_dve, 1)
            dve.wait_ge(c_dve, 3)
            dve.tensor_scalar(freq[:, :], freq[:, :], theta_c[:, 0:1], None, ALU.mult).then_inc(c_dve, 1)
            dve.wait_ge(c_dve, 4)
            for t in range(TT):
                last = dve.tensor_scalar(ang[:, t, :], freq[:, :], tokf[:, t:t + 1], None, ALU.mult)
            last.then_inc(c_dve, 1)
            dve.wait_ge(c_dve, 5)
            dve.tensor_scalar(turns[:, :, :], ang[:, :, :], float(1.0 / (2 * np.pi)), MAGIC, ALU.mult, ALU.add).then_inc(c_dve, 1)
            dve.wait_ge(c_dve, 6)
            dve.tensor_scalar(turns[:, :, :], turns[:, :, :], -MAGIC, None, ALU.add).then_inc(c_dve, 1)
            n = 7
            for c in two_pi_parts():
                dve.wait_ge(c_dve, n)
                dve.scalar_tensor_tensor(ang[:, :, :], turns[:, :, :], -c, ang[:, :, :], ALU.mult, ALU.add).then_inc(c_dve, 1)
                n += 1
            dve.wait_ge(c_dve, n)
            dve.tensor_scalar(angc[:, :, :], ang[:, :, :], float(np.pi / 2), None, ALU.add).then_inc(c_dve, 1)
            dve.wait_ge(c_dve, n + 1)
            dve.tensor_scalar(wrap[:, :, :], angc[:, :, :], float(np.pi), None, ALU.is_gt).then_inc(c_dve, 1)
            dve.wait_ge(c_dve, n + 2)
            dve.scalar_tensor_tensor(angc[:, :, :], wrap[:, :, :], float(-2 * np.pi), angc[:, :, :], ALU.mult, ALU.add).then_inc(c_dve, 1)
            dve.wait_ge(c_dve, n + 3)
            lim = 3.1415925
            dve.tensor_scalar(angc[:, :, :], angc[:, :, :], lim, -lim, ALU.min, ALU.max).then_inc(c_dve, 1)
            dve.tensor_scalar(ang[:, :, :], ang[:, :, :], lim, -lim, ALU.min, ALU.max).then_inc(c_dve, 1)
            assert n + 5 == ANGLES
            dve.wait_ge(f_dve, 1)
            dve.tensor_copy(fidx[:, :, :], fidx_i[:, :, :]).then_inc(f_dve, 1)
            dve.wait_ge(f_dve, 2)
            dve.tensor_tensor(fmask[:, :, :], iota16[:, :].unsqueeze(1).to_broadcast([P, FDMAS, E]),
                              fidx[:, 1, :].unsqueeze(2).to_broadcast([P, FDMAS, E]), ALU.is_equal).then_inc(f_dve, 1)
            dve.tensor_scalar(fbase[:, :], fidx[:, 1, :], float(EROWS - P), None, ALU.mult).then_inc(f_dve, 1)
            dve.wait_ge(f_dve, 4)
            dve.scalar_tensor_tensor(fbase[:, :], fidx[:, 0, :], float(FROWS), fbase[:, :], ALU.mult, ALU.add).then_inc(f_dve, 1)
            dve.wait_ge(f_dve, 5)
            dve.tensor_scalar(fbase[:, :], fbase[:, :], float(ROW), None, ALU.mult).then_inc(f_dve, 1)
            dve.memset(plan_i[0:1, P:P + 4], 0).then_inc(f_dve, 1)

            def norm_stats(n, j, src):
                for t in range(TT):
                    dve.bn_stats(stats[:, n, t, :], src[:, t, :]).then_inc(ln_mv[n], 1)
                for t in range(TT):
                    wait_first(dve, ln_mv[n], 4 * j + t + 1)
                    dve.bn_aggr(mv[:, n, t, :], stats[:, n, t, :]).then_inc(ln_mv[n], 1)

            def rope(j, t):
                dve.wait_ge(qk_ps, 2 * j + t + 1)
                if t == 0 and isinstance(j, int) and j == 0:
                    dve.wait_ge(c_act, 4)
                wait(dve, rot_ok, 2 * j + t - 1)
                src = bank[FB][:, :].rearrange("p (h d c) -> p h d c", d=HD // 2, c=2)
                swapped = bass.AP(src.tensor, src.offset + 1, [list(src.ap[0]), [HD, 2 * HEADS], [2, HD // 2], [-1, 2]])
                shape = [P, 2 * HEADS, HD // 2, 2]
                dst = [r[:, t, :].rearrange("p (h d c) -> p h d c", d=HD // 2, c=2) for r in (rt1, rt2)]
                dve.tensor_tensor(dst[0], src, cosr[:, t, :, :].unsqueeze(1).to_broadcast(shape), ALU.mult)
                dve.tensor_tensor(dst[1], swapped, sinr[:, t, :, :].unsqueeze(1).to_broadcast(shape), ALU.mult).then_inc(ro_ok, 1)

            def low_part(j, t):
                dve.wait_ge(hi_ok, 2 * j + t + 1)
                wait(dve, tqk_ps, 4 * j + 2 * t - 2)
                st = stack[:, t, :, :, :]
                dve.tensor_tensor(st[:, :, 2, :], rot[:, t, :].rearrange("p (h d) -> p h d", d=HD), st[:, :, 0, :], ALU.subtract).then_inc(stk_ok, 1)
                dve.wait_ge(stk_ok, 6 * j + 3 * t + 1)
                dve.tensor_copy(st[:, 0:HEADS, 1:4:2, :], st[:, 0:HEADS, 0:4:2, :]).then_inc(stk_ok, 1)
                kk = st[:, HEADS:2 * HEADS, :, :]
                back_to_front = bass.AP(kk.tensor, kk.offset + 3 * HD, [list(kk.ap[0]), [4 * HD, HEADS], [-2 * HD, 2], [1, HD]])
                dve.tensor_copy(back_to_front, kk[:, :, 0:4:2, :]).then_inc(stk_ok, 1)

            def keep_T(j, b, t, which):
                dve.wait_ge(tqk_ps, 4 * j + 2 * t + which + 1)
                if t == 0:
                    wait(dve, s_ps, 8 * (j - 1))
                dst = (qT, kT)[which]
                dve.tensor_copy(dst[:, b[1], :, t * P:(t + 1) * P],
                                bank[FB][:, :].bitcast(F16).rearrange("p (a c) -> p a c", c=P)).then_inc(qkT_ok, 1)

            def step(att, back, front, nxt):
                if back:
                    jb, pb = num(back), back[1]
                    for t in range(TT):
                        dve.wait_ge(to_ps, TT * jb + t + 1)
                        o = bank[(B6, B7)[t]][:, :].rearrange("p (h c) -> p h c", c=32)
                        dve.reciprocal(rec[:, t, :].unsqueeze(2), o[:, :, HD:HD + 1]).then_inc(rec_ok, 1)
                        dve.wait_ge(rec_ok, TT * jb + t + 1)
                        wait(dve, tw_ps, jb)
                        dve.tensor_tensor(wv[:, t, :].rearrange("p (h d) -> p h d", d=HD), o[:, :, 0:HD],
                                          rec[:, t, :].unsqueeze(2).to_broadcast([P, HEADS, HD]), ALU.mult).then_inc(wv_ok, 1)
                    if first(back):
                        dve.wait_ge(ws_in, 16 * WLOADS)
                    dve.wait_ge(cx_in[pb], back[0] * 16 + 16)
                    wait(dve, e_ps, jb)
                    for t in range(TT):
                        dve.scalar_tensor_tensor(scr[:, t, :], cx[:, pb, t, :], 1.0, wenc[:, :], ALU.mult, ALU.mult,
                                                 accum_out=enc[:, t:t + 1]).then_inc(enc_ok, 1)
                if front:
                    jf, pf = num(front), front[1]
                    rope(jf, 0)
                if back:
                    dve.wait_ge(wo_ps, jb + 1)
                    dve.wait_ge(xb_in[pb], back[0] * 16 + 16)
                    dve.tensor_tensor(x1[:, :, :].rearrange("p t d -> p (t d)"), bank[B7][:, :],
                                      xb[:, pb, :, :].rearrange("p t d -> p (t d)"), ALU.add).then_inc(x1_ok, 1)
                    dve.wait_ge(x1_ok, jb + 1)
                    norm_stats(1, jb, x1)
                    dve.wait_ge(ln_mv[1], 4 * jb + 4)
                    for t in range(TT):
                        dve.scalar_tensor_tensor(scr2[:, t, :], x1[:, t, :], mv[:, 1, t, 0:1], wdec[:, :], ALU.subtract, ALU.mult,
                                                 accum_out=dec[:, t:t + 1]).then_inc(dec_ok, 1)
                if front:
                    rope(jf, 1)
                if back:
                    dve.wait_ge(rr[1], 2 * jb + 2)
                    dve.wait_ge(dec_ok, 4 * jb + 2)
                    dve.tensor_tensor(dec[:, :], dec[:, :], rstd[:, 1, :], ALU.mult).then_inc(dec_ok, 1)
                    dve.wait_ge(dec_ok, 4 * jb + 3)
                    dve.tensor_scalar(dec[:, :], dec[:, :], mbias[:, 0:1], None, ALU.add).then_inc(dec_ok, 1)
                    dve.wait_ge(dec_ok, 4 * jb + 4)
                    dve.wait_ge(e_ps, jb + 1)
                    for t in range(TT):
                        last = dve.scalar_tensor_tensor(x2[:, t, :], x1[:, t, :], dec[:, t:t + 1], bank[B6][:, 0:D], ALU.add, ALU.add)
                    last.then_inc(x2_ok, 1)
                    dve.wait_ge(x2_ok, jb + 1)
                    norm_stats(2, jb, x2)
                if front:
                    low_part(jf, 0)
                if back:
                    dve.wait_ge(rr[2], 2 * jb + 2)
                    wait(dve, sent[pb], back[0] * (16 * TT * TOPK))
                    for t in range(TT):
                        last = dve.tensor_scalar(rows[0][:, pb, t, 0:D], x2[:, t, :], mv[:, 2, t, 0:1], rstd[:, 2, t:t + 1],
                                                 ALU.subtract, ALU.mult)
                    last.then_inc(h3_ok, 1)
                if front:
                    low_part(jf, 1)
                    keep_T(jf, front, 0, 0)
                    keep_T(jf, front, 0, 1)
                if nxt:
                    jn, pn = num(nxt), nxt[1]
                    dve.wait_ge(xa_in[pn], nxt[0] * 16 + 16)
                    norm_stats(0, jn, xa[:, pn, :, :])
                if back:
                    wait_first(dve, sco_ok, jb + 1)
                    for t in range(TT):
                        dve.max(topv[:, t, :], score[:, t, :]).then_inc(ra_ok, 1)
                    wait_first(dve, ra_ok, 15 * jb + 2)
                    for t in range(TT):
                        dve.max_index(topi[:, t, :], topv[:, t, :], score[:, t, :]).then_inc(ra_ok, 1)
                    dve.tensor_tensor(ssum[:, :], topv[:, :, 0], topv[:, :, 1], ALU.add).then_inc(ra_ok, 1)
                    dve.wait_ge(ra_ok, 15 * jb + 4)
                    dve.tensor_copy(topf[:, :].rearrange("p (t k) -> p t k", k=TOPK), topi[:, :, 0:TOPK]).then_inc(ra_ok, 1)
                    dve.wait_ge(ra_ok, 15 * jb + 5)
                    dve.tensor_scalar(ssum[:, :], ssum[:, :], 1e-20, None, ALU.add).then_inc(ra_ok, 1)
                    dve.wait_ge(ra_ok, 15 * jb + 6)
                    dve.tensor_tensor(onehot[:, :, :], iota16[:, :].unsqueeze(1).to_broadcast([P, TT * TOPK, E]),
                                      topf[:, :].unsqueeze(2).to_broadcast([P, TT * TOPK, E]), ALU.is_equal).then_inc(ra_ok, 1)
                    dve.wait_ge(ra_ok, 15 * jb + 7)
                    dve.reciprocal(ssum[:, :], ssum[:, :]).then_inc(ra_ok, 1)
                    dve.wait_ge(ra_ok, 15 * jb + 8)
                    oh = onehot[:, :, :].rearrange("p (t k) e -> p t k e", k=TOPK)
                    dve.tensor_tensor(chosen[:, :, :], oh[:, :, 0, :], oh[:, :, 1, :], ALU.add).then_inc(ra_ok, 1)
                    dve.wait_ge(ra_ok, 15 * jb + 9)
                    for k in range(TOPK):
                        dve.scalar_tensor_tensor(rows[k][:, pb, :, D + 1], topv[:, :, k], ROUTE_SCALE, ssum[:, :],
                                                 ALU.mult, ALU.mult).then_inc(ra_ok, 1)
                    for k in range(TOPK):
                        dve.tensor_copy(rows[k][:, pb, :, D].bitcast(I32), idf[:, k, :]).then_inc(ra_ok, 1)
                    dve.wait_ge(ra_ok, 15 * jb + 14)
                    dve.tensor_scalar(idf[:, :, :], idf[:, :, :], float(T * TOPK), None, ALU.add).then_inc(ra_ok, 1)
                if front:
                    keep_T(jf, front, 1, 0)
                if back:
                    dve.wait_ge(sg_ok, jb + 1)
                    dve.tensor_tensor(sgT[:, :], bank[B7][:, 0:T], sgT[:, :], ALU.mult).then_inc(hid_ok, 1)
                    dve.wait_ge(hid_ok, 2 * jb + 1)
                    dve.tensor_tensor(hidT[:, :], bank[B7][:, T:2 * T], sgT[:, :], ALU.mult).then_inc(hid_ok, 1)
                if nxt:
                    dve.wait_ge(rr[0], 2 * jn + 2)
                    wait(dve, tx_ps, jn)
                    for t in range(TT):
                        last = dve.tensor_scalar(xn[:, t, :], xa[:, pn, t, :], mv[:, 0, t, 0:1], rstd[:, 0, t:t + 1],
                                                 ALU.subtract, ALU.mult)
                    last.then_inc(xn_ok, 1)
                if front:
                    keep_T(jf, front, 1, 1)
                if back:
                    dve.wait_ge(rk_ps, jb + 1)
                    dve.wait_ge(ra_ok, 15 * jb + 15)
                    dve.tensor_tensor(pose[:, :, :], bank[B6][:, 0:TT * E].rearrange("p (t e) -> p t e", t=TT),
                                      ebase[:, :].unsqueeze(1).to_broadcast([P, TT, E]), ALU.add).then_inc(rb_ok, 1)
                    dve.tensor_tensor(seen[:, :], seen[:, :], chosen[:, 0, :], ALU.add).then_inc(rb_ok, 1)
                    dve.wait_ge(rb_ok, 6 * jb + 2)
                    dve.tensor_tensor(seen[:, :], seen[:, :], chosen[:, 1, :], ALU.add).then_inc(rb_ok, 1)
                    pk = posp[:, :, :].rearrange("p (t k) e -> p t k e", k=TOPK)
                    for k in range(TOPK):
                        last = dve.tensor_tensor(pk[:, :, k, :], oh[:, :, k, :], pose[:, :, :], ALU.mult)
                    last.then_inc(rb_ok, 1)
                    dve.wait_ge(rb_ok, 6 * jb + 4)
                    dve.reduce_sum(posf[:, :], posp[:, :, :], AX.X).then_inc(rb_ok, 1)
                    dve.wait_ge(rb_ok, 6 * jb + 5)
                    dve.tensor_copy(posi[:, pb, :], posf[:, :]).then_inc(rb_ok, 1)
                    dve.wait_ge(dn_ps, jb + 1)
                    dve.tensor_tensor(acc[:, bass.ds(jb * (TT * D), TT * D)], bank[B7][:, :],
                                      x2[:, :, :].rearrange("p t d -> p (t d)"), ALU.add).then_inc(acc_ok, 1)
                if front:
                    dve.wait_ge(c_ps, jf + 1)
                    wait(dve, o_ok, 2 * jf)
                    dve.tensor_copy(vsum[:, :], bank[FB][:, 0:GROUPS]).then_inc(c_ok, 1)

            pipeline(dve, step)

            dve.wait_ge(cnt_ps, 1)
            dve.tensor_copy(cnt[:, :], bank[B6][:, 0:E]).then_inc(pl_ok, 1)
            dve.wait_ge(pl_ok, 1)
            dve.wait_ge(f_dve, 7)
            dve.tensor_tensor(fprod[:, :, :], fmask[:, :, :], cnt[:, :].unsqueeze(1).to_broadcast([P, FDMAS, E]), ALU.mult).then_inc(pl_ok, 1)
            dve.wait_ge(pl_ok, 2)
            dve.reduce_sum(fcnt[:, :], fprod[:, :, :], AX.X).then_inc(pl_ok, 1)
            dve.wait_ge(pl_ok, 3)
            dve.scalar_tensor_tensor(frow[:, :], fcnt[:, :], float(ROW), fbase[:, :], ALU.mult, ALU.add).then_inc(pl_ok, 1)
            dve.tensor_scalar(cnt_i[:, 0, :], cnt[:, :], float(P - 1), None, ALU.add).then_inc(pl_ok, 1)
            dve.wait_ge(pl_ok, 5)
            dve.tensor_single_scalar(cnt_i[:, 1, :], cnt_i[:, 0, :], 7, op=ALU.arith_shift_right).then_inc(pl_ok, 1)
            dve.wait_ge(pl_ok, 6)
            dve.tensor_copy(ntl[:, :], cnt_i[:, 1, :]).then_inc(pl_ok, 1)
            dve.wait_ge(pl_ok, 7)
            dve.tensor_tensor_scan(cum[:, :], onesf[:, :], ntl[:, :], 0.0, ALU.mult, ALU.add).then_inc(pl_ok, 1)
            dve.wait_ge(pl_ok, 8)
            dve.tensor_scalar(le[:, :], cum[:, :], sidx[:, 0:1], None, ALU.is_le).then_inc(pl_ok, 1)
            dve.wait_ge(pl_ok, 9)
            dve.reduce_sum(plan[:, 0:1], le[:, :], AX.X).then_inc(pl_ok, 1)
            dve.tensor_tensor(lep[:, :], le[:, :], ntl[:, :], ALU.mult).then_inc(pl_ok, 1)
            dve.wait_ge(pl_ok, 11)
            dve.reduce_sum(plan[:, 1:2], lep[:, :], AX.X).then_inc(pl_ok, 1)
            dve.wait_ge(pl_ok, 12)
            dve.tensor_tensor(plan[:, 2:3], sidx[:, :], plan[:, 1:2], ALU.subtract).then_inc(pl_ok, 1)
            dve.tensor_scalar(plan[:, 3:4], plan[:, 0:1], float(EROWS), None, ALU.mult).then_inc(pl_ok, 1)
            dve.tensor_scalar(plan[:, 5:6], plan[:, 0:1], float(E - 1), float(WE), ALU.min, ALU.mult).then_inc(pl_ok, 1)
            dve.wait_ge(pl_ok, 15)
            dve.scalar_tensor_tensor(plan[:, 4:5], plan[:, 2:3], float(P), plan[:, 3:4], ALU.mult, ALU.add).then_inc(pl_ok, 1)
            dve.wait_ge(plan_ps, 1)
            dve.tensor_copy(plan_i[0:1, 0:P], bank[B6][0:1, 0:P]).then_inc(plan_ok, 1)
            dve.tensor_copy(plan_i[0:1, P + 4:2 * P + 4], bank[B6][0:1, P:2 * P]).then_inc(plan_ok, 1)

            def expert(n, c, m):
                small = isinstance(n, int)
                if not small or 1 <= n <= SLOTS:
                    r = (c - 1) % 2
                    dve.wait_ge(esg_ok, n)
                    if not small or n >= 3:
                        dve.wait_ge(etd_ps, n - 2)
                    dve.tensor_tensor(ehd[:, r, :], bank[2 + r][:, M:2 * M], esg[:, r, :], ALU.mult).then_inc(ehd_ok, 1)
                if not small or 2 <= n <= SLOTS + 1:
                    r = (c - 2) % 2
                    dve.wait_ge(etd_ps, n - 1)
                    if not small or n >= 4:
                        dve.wait_ge(edn_ps, n - 3)
                    dve.tensor_copy(ehT[:, r, :], bank[4 + r][:, 0:P]).then_inc(ehT_ok, 1)
                if not small or n >= 3:
                    r, y = (c - 3) % XRING, (c - 3) % YRING
                    q = (n - 3) // YRING if small else m * 2 + (c - 3) // YRING
                    dve.wait_ge(edn_ps, n - 2)
                    wait(dve, ys_out[y], q * 16)
                    dve.tensor_scalar(ys[:, y, :], bank[6 + r % 2][:, 0:D], xs[:, r, D + 1:D + 2], None, ALU.mult).then_inc(ys_ok, 1)

            slots(dve, expert)

            with dve.Fori(0, NTILES // CRING) as m:
                for r in range(CRING):
                    dve.wait_ge(yp_in[r], m * 16 + 16)
                    a = acc[:, bass.ds((m * CRING + r) * D, D)]
                    dve.tensor_tensor(a, a, ypair[:, r, 0:D], ALU.add).then_inc(f1_ok, 1)
                    dve.wait_ge(f1_ok, m * CRING + r + 1)
                    dve.tensor_tensor(a, a, ypair[:, r, D:2 * D], ALU.add).then_inc(fin_ok, 1)

        @block.tensor
        def _(pe):
            pe.wait_ge(c_pool, 6)
            pe.wait_ge(c_dve, 2)

            def scores(j, b, a):
                wait(pe, sq_ok, 8 * j + a - 1)
                if a == 0:
                    pe.wait_ge(qkT_ok, 4 * j + 4)
                for h in range(2):
                    for kt in range(TT):
                        lo = 64 * h
                        last = pe.matmul(bank[2 * (a % 2) + h][:, kt * T:(kt + 1) * T],
                                         kT[lo:lo + 64, b[1], a, kt * P:(kt + 1) * P],
                                         qT[lo:lo + 64, b[1], a, :], start=True, stop=True)
                last.then_inc(s_ps, 1)

            def weighted(j, b, g):
                pe.wait_ge(sq_ok, 8 * j + 2 * g + 2)
                if g % 2 == 0:
                    wait(pe, o_ok, 2 * j + g // 2)
                for kt in range(TT):
                    for h in range(HPG):
                        head = HPG * g + h
                        last = pe.matmul(bank[PVB][32 * h:32 * h + 32, (g % 2) * T:(g % 2 + 1) * T],
                                         vaug[:, b[1], kt, head, :], sq[:, (head // 2) % 4, head % 2, kt, :],
                                         start=(kt == 0), stop=(kt == TT - 1))
                last.then_inc(pv_ps, 1)

            def project_qk(j, t):
                if t == 0:
                    if isinstance(j, int) and j == 0:
                        pe.wait_ge(wqk_in, 32)
                    pe.wait_ge(hT_ok, j + 1)
                else:
                    pe.wait_ge(ro_ok, 2 * j + 1)
                for k in range(KD):
                    last = pe.matmul(bank[FB][:, :], hT[:, k, t * P:(t + 1) * P], wqk[:, k, :], start=(k == 0), stop=(k == KD - 1))
                last.then_inc(qk_ps, 1)

            def transpose_qk(j, t, which):
                if which == 0:
                    pe.wait_ge(stk_ok, 6 * j + 3 * t + 3)
                if t == 0 and which == 0:
                    pe.wait_ge(v_ok, j + 1)
                else:
                    pe.wait_ge(qkT_ok, 4 * j + 2 * t + which)
                dst = bank[FB][:, :].bitcast(F16)
                for a in range(HEADS // 2):
                    h = which * HEADS + 2 * a
                    last = pe.transpose(dst[:, a * P:(a + 1) * P],
                                        stack[:, t, h:h + 2, :, :].rearrange("p h s d -> p (h s d)"), identh[:, :])
                last.then_inc(tqk_ps, 1)

            def step(att, back, front, nxt):
                ja = num(att) if att else None
                if back:
                    jb, pb = num(back), back[1]
                    for t in range(TT):
                        pe.wait_ge(o_ok, 2 * jb + 2)
                        if t == 0:
                            wait(pe, rb_ok, 6 * jb)
                        else:
                            wait(pe, acc_ok, jb)
                        for g in range(GROUPS):
                            last = pe.transpose(bank[(B6, B7)[t]][:, g * P:(g + 1) * P], oT[:, g, t * P:(t + 1) * P], identf[:, :])
                        last.then_inc(to_ps, 1)
                if front:
                    jf, pf = num(front), front[1]
                    pe.wait_ge(xn_ok, jf + 1)
                    wait(pe, c_ok, jf)
                    for t in range(TT):
                        for k in range(KD):
                            last = pe.transpose(bank[FB][:, (t * KD + k) * P:(t * KD + k + 1) * P], xn[:, t, k * P:(k + 1) * P], identf[:, :])
                    last.then_inc(tx_ps, 1)
                if att:
                    scores(ja, att, 0)
                    scores(ja, att, 1)
                if back:
                    pe.wait_ge(wv_ok, TT * jb + TT)
                    for t in range(TT):
                        for k in range(KD):
                            last = pe.transpose(bank[B6][:, (t * KD + k) * P:(t * KD + k + 1) * P], wv[:, t, k * P:(k + 1) * P], identf[:, :])
                    last.then_inc(tw_ps, 1)
                if front:
                    project_qk(jf, 0)
                if back:
                    if first(back):
                        pe.wait_ge(wo_in, 16)
                        pe.wait_ge(ws_in, 16 * WLOADS)
                    pe.wait_ge(wvT_ok, jb + 1)
                    for t in range(TT):
                        for k in range(KD):
                            last = pe.matmul(bank[B7][:, t * D:(t + 1) * D], wvT[:, k, t * P:(t + 1) * P], wo[:, k, :],
                                             start=(k == 0), stop=(k == KD - 1))
                    last.then_inc(wo_ps, 1)
                    pe.wait_ge(enc_ok, 2 * jb + 2)
                    for t in range(TT):
                        last = pe.matmul(bank[B6][:, t * P:(t + 1) * P], enc[:, t:t + 1].to_broadcast([P, P]), identf[:, :],
                                         start=True, stop=True)
                    last.then_inc(e_ps, 1)
                if front:
                    project_qk(jf, 1)
                if att:
                    scores(ja, att, 2)
                    scores(ja, att, 3)
                if att:
                    weighted(ja, att, 0)
                if front:
                    if first(front):
                        pe.wait_ge(wv_in, 16)
                    pe.wait_ge(ro_ok, 2 * jf + 2)
                    for t in range(TT):
                        for k in range(KD):
                            last = pe.matmul(bank[FB][:, t * D:(t + 1) * D], hT[:, k, t * P:(t + 1) * P], wv_w[:, k, :],
                                             start=(k == 0), stop=(k == KD - 1))
                    last.then_inc(v_ps, 1)
                if att:
                    scores(ja, att, 4)
                    scores(ja, att, 5)
                if att:
                    weighted(ja, att, 1)
                if front:
                    transpose_qk(jf, 0, 0)
                if att:
                    scores(ja, att, 6)
                if back:
                    pe.wait_ge(h3_ok, jb + 1)
                    for t in range(TT):
                        for k in range(KD):
                            last = pe.transpose(bank[B7][:, (t * KD + k) * P:(t * KD + k + 1) * P],
                                                rows[0][:, pb, t, k * P:(k + 1) * P], identf[:, :])
                    last.then_inc(th_ps, 1)
                if front:
                    transpose_qk(jf, 0, 1)
                if att:
                    scores(ja, att, 7)
                if back:
                    pe.wait_ge(h3T_ok, jb + 1)
                    for t in range(TT):
                        for k in range(KD):
                            last = pe.matmul(bank[B6][:, t * E:(t + 1) * E], h3T[:, k, t * P:(t + 1) * P], gwT[:, k, :],
                                             start=(k == 0), stop=(k == KD - 1))
                    last.then_inc(ga_ps, 1)
                    for s in range(2):
                        for k in range(KD):
                            last = pe.matmul(bank[B7][:, s * T:(s + 1) * T], wsgu[:, k, s * M:(s + 1) * M], h3T[:, k, :],
                                             start=(k == 0), stop=(k == KD - 1))
                    last.then_inc(sh_ps, 1)
                if att:
                    weighted(ja, att, 2)
                if front:
                    transpose_qk(jf, 1, 0)
                if att:
                    weighted(ja, att, 3)
                if front:
                    transpose_qk(jf, 1, 1)
                if back:
                    pe.wait_ge(ra_ok, 15 * jb + 10)
                    pe.wait_ge(sco_ok, jb + 1)
                    for t in range(TT):
                        dst = bank[B6][:, t * E:(t + 1) * E]
                        pe.matmul(dst, tri[:, :], chosen[:, t, :], start=True, stop=False)
                        for s in range(t):
                            pe.matmul(dst, onesb[:, :], chosen[:, s, :], start=False, stop=False)
                        last = pe.matmul(dst, onesb[:, :], seen[:, :], start=False, stop=True)
                    last.then_inc(rk_ps, 1)
                    pe.wait_ge(hid_ok, 2 * jb + 2)
                    for t in range(TT):
                        last = pe.matmul(bank[B7][:, t * D:(t + 1) * D], hidT[:, t * P:(t + 1) * P], wsd[:, :], start=True, stop=True)
                    last.then_inc(dn_ps, 1)
                if front:
                    pe.wait_ge(qkT_ok, 4 * jf + 4)
                    pe.wait_ge(vp_ok, jf + 1)
                    for g in range(GROUPS):
                        last = pe.matmul(bank[FB][:, g:g + 1],
                                         vpair[:, HPG * g:HPG * g + HPG, :].rearrange("p h d -> p (h d)"),
                                         onesf[:, 0:1], start=True, stop=True)
                    last.then_inc(c_ps, 1)

            pipeline(pe, step)

            pe.wait_ge(rb_ok, 6 * NB)
            pe.matmul(bank[B6][:, 0:E], onesb[:, :], seen[:, :], start=True, stop=True).then_inc(cnt_ps, 1)
            pe.wait_ge(pl_ok, 16)
            for i in range(2):
                last = pe.matmul(bank[B6][0:1, i * P:(i + 1) * P], plan[:, 4 + i:5 + i], identf[:, :], start=True, stop=True)
            last.then_inc(plan_ps, 1)
            pe.wait_ge(plan_ok, 2)
            pe.wait_ge(wE_in, 16 * 5)
            pe.wait_ge(acc_ok, NB)

            columns = []

            def expert(n, c, m):
                small = isinstance(n, int)
                if c == 0:
                    columns[:] = read_plan(pe, n + P, 4 + XRING if not small or n < SLOTS else 4, (E - 1) * WE)
                if not small or n < SLOTS:
                    q = 1 if small else m + 1
                    pe.wait_ge(xs_in[c], q * 16)
                    if not small or n >= 2:
                        pe.wait_ge(exT_ok, n - 1)
                    for k in range(KD):
                        last = pe.transpose(bank[c % 2][:, k * P:(k + 1) * P], xs[:, c, k * P:(k + 1) * P], identf[:, :])
                    last.then_inc(etx_ps, 1)
                if not small or 1 <= n <= SLOTS:
                    r = (c - 1) % 2
                    w = columns[c + 3]
                    pe.wait_ge(exT_ok, n)
                    if not small or n >= 3:
                        pe.wait_ge(ehd_ok, n - 2)
                    for k in range(KD):
                        last = pe.matmul(bank[2 + r][:, 0:2 * M], exT[:, r, k, :], wex[:, bass.ds(w + k * 2 * M, 2 * M)],
                                         start=(k == 0), stop=(k == KD - 1))
                    last.then_inc(gu_ps, 1)
                if not small or 2 <= n <= SLOTS + 1:
                    r = (c - 2) % 2
                    pe.wait_ge(ehd_ok, n - 1)
                    if not small or n >= 4:
                        pe.wait_ge(ehT_ok, n - 3)
                    pe.transpose(bank[4 + r][:, 0:P], ehd[:, r, :], identf[:, :]).then_inc(etd_ps, 1)
                if not small or n >= 3:
                    r = (c - 3) % 2
                    w = columns[c + 1]
                    pe.wait_ge(ehT_ok, n - 2)
                    if not small or n >= 5:
                        pe.wait_ge(ys_ok, n - 4)
                    pe.matmul(bank[6 + r][:, 0:D], ehT[:, r, :], wex[:, bass.ds(w + KD * 2 * M, D)], start=True, stop=True).then_inc(edn_ps, 1)

            slots(pe, expert)


_INS = ["x", "ctx_1024", "L0_attn_ln_w", "L0_attn_ln_b", "L0_attn_w_q", "L0_attn_w_kv", "L0_attn_w_o", "L0_attn_theta",
        "L0_xattn_mlp_weight", "L0_xattn_mlp_bias", "L0_ffn_gate_w", "L0_ffn_w_gate", "L0_ffn_w_up", "L0_ffn_w_down",
        "L0_ffn_ws_gate", "L0_ffn_ws_up", "L0_ffn_ws_down"]


def kernel(**inputs):
    import concourse.bacc as bacc
    from concourse.bass_utils import run_bass_kernel_spmd

    nc = bacc.Bacc("TRN2", target_bir_lowering=False, num_devices=1)
    arrays, args = {}, []
    for name in _INS:
        a = np.ascontiguousarray(inputs[name])
        if name == "L0_attn_theta":
            a = a.reshape(1)
        if name == "L0_ffn_gate_w":
            a = np.ascontiguousarray(a.T)
        if name in ("L0_attn_ln_w", "L0_attn_ln_b"):
            a = np.ascontiguousarray(a.reshape(KD, P).T)
        arrays[f"in_{name}"] = a
        args.append(nc.dram_tensor(f"in_{name}", a.shape, mybir.dt.from_np(a.dtype), kind="ExternalInput").ap())
    args.append(nc.dram_tensor("out_0", (NB, T, D), F32, kind="ExternalOutput").ap())
    build(nc, *args)
    r = run_bass_kernel_spmd(nc, [arrays], core_ids=[0])
    return r.results[0]["out_0"]
```

```python
from contextlib import ExitStack

import numpy as np

import concourse.bass as bass
from concourse import mybir

F32 = mybir.dt.float32
F16 = mybir.dt.float16
BF16 = mybir.dt.bfloat16
I32 = mybir.dt.int32
U32 = mybir.dt.uint32
ALU = mybir.AluOpType
ACT = mybir.ActivationFunctionType
AX = mybir.AxisListType

P = 128
NB, T, D = 16, 256, 256
TT = T // P
KD = D // P
HEADS, HD = 16, 16
GROUPS = 4
HPG = HEADS // GROUPS
E, M, TOPK = 16, 128, 2
NTOK = NB * T
NTILES = NTOK // P
ROUTE_SCALE = 2.5
EPS = 1e-5

ROW = D + 2
EROWS = NTOK + P
SLOTS = (NTOK * TOPK + E * (P - 1)) // P
NULLS = SLOTS - (NTOK * TOPK) // P
XROWS = E * EROWS + NULLS * P
YROWS = NTOK * TOPK
PLANNED = NB - 2
EARLY = 24
assert EARLY * P <= PLANNED * T * TOPK - E * (P - 1)
SKIP_ROW = 1 << 20

WE = KD * 2 * M + D
FROWS = 8
FDMAS = E // FROWS

MAGIC = 1.5 * 2.0 ** 23


def mel_base():
    f = np.float32
    top = f(2595.0 * np.log10(1.0 + 4000.0 / 200.0))
    lin = np.array([top * f(i / (HD // 2 - 1)) for i in range(HD // 2)], f)
    mel = np.power(10.0, (lin / f(2595.0)).astype(np.float64)).astype(f) - f(1.0)
    return [float(v) for v in (f(200.0) * mel / f(1000.0)).astype(f)]


def two_pi_parts():
    c1 = 6.28125
    c2 = float(np.round((2 * np.pi - c1) * 2.0 ** 18) / 2.0 ** 18)
    return c1, c2, float(np.float32(2 * np.pi - c1 - c2))


def build(nc, x, ctx_in, ln_w, ln_b, w_q, w_kv, w_o, theta, mlp_w, mlp_b,
          gate_wT, w_gate, w_up, w_down, ws_gate, ws_up, ws_down, out):
    with ExitStack() as ctx:
        def sb(name, shape, dt=F32):
            return ctx.enter_context(nc.sbuf_tensor(name, shape, dt))

        def sem(name):
            return ctx.enter_context(nc.semaphore(name))

        disp = nc.dram_tensor("dispatch", [XROWS, ROW], F32, kind="Internal").ap()
        yexp = nc.dram_tensor("expert_out", [YROWS, D], F32, kind="Internal").ap()

        wqk = sb("wqk", [P, KD, 2 * D])
        wv_w = sb("wv_w", [P, KD, D])
        wo = sb("wo", [P, KD, D])
        wsgu = sb("wsgu", [P, KD, 2 * M])
        wsd = sb("wsd", [P, D])
        gwT = sb("gwT", [P, KD, E])
        wex = sb("wex", [P, E * WE])
        lnw_c = sb("lnw_c", [P, KD])
        lnb_c = sb("lnb_c", [P, KD])
        wenc = sb("wenc", [P, D])
        wdec = sb("wdec", [P, D])
        mbias = sb("mbias", [P, 1])
        theta_c = sb("theta_c", [P, 1])
        identf = sb("identf", [P, P])
        identh = sb("identh", [P, P], F16)
        tri = sb("tri", [P, P], BF16)
        onesb = sb("onesb", [P, P], BF16)
        onesf = sb("onesf", [P, E])
        iota16 = sb("iota16", [P, E])
        ebase = sb("ebase", [P, E])
        ebase_i = sb("ebase_i", [P, E], I32)
        iota_i = sb("iota_i", [P, E], I32)
        tok_i = sb("tok_i", [P, TT], I32)
        tokf = sb("tokf", [P, TT])
        fidx_i = sb("fidx_i", [P, 2, FDMAS], I32)
        fidx = sb("fidx", [P, 2, FDMAS])
        fmask = sb("fmask", [P, FDMAS, E])
        fprod = sb("fprod", [P, FDMAS, E])
        fbase = sb("fbase", [P, FDMAS])
        fcnt = sb("fcnt", [P, FDMAS])
        frow = sb("frow", [P, FDMAS], I32)
        idi = sb("idi", [P, TOPK, TT], I32)
        idf = sb("idf", [P, TOPK, TT])
        freq = sb("freq", [P, HD // 2])
        ang = sb("ang", [P, TT, HD // 2])
        turns = sb("turns", [P, TT, HD // 2])
        angc = sb("angc", [P, TT, HD // 2])
        wrap = sb("wrap", [P, TT, HD // 2])
        cosr = sb("cosr", [P, TT, HD // 2, 2])
        sinr = sb("sinr", [P, TT, HD // 2, 2])
        halfneg = sb("halfneg", [P, 2])
        filler = sb("filler", [P, ROW])

        xa = sb("xa", [P, 2, TT, D])
        xb = sb("xb", [P, 2, TT, D])
        cx = sb("cx", [P, 2, TT, D])
        xn = sb("xn", [P, TT, D])
        hT = sb("hT", [P, KD, T])
        rotary = sb("rotary", [P, 3 * TT * 2 * D])
        rt1, rt2, rot = (rotary[:, i * TT * 2 * D:(i + 1) * TT * 2 * D].rearrange("p (t n) -> p t n", t=TT)
                         for i in range(3))
        stack = sb("stack", [P, TT, 2 * HEADS, 4, HD], F16)
        qT = sb("qT", [P, 2, HEADS // 2, T], F16)
        kT = sb("kT", [P, 2, HEADS // 2, T], F16)
        vaug = sb("vaug", [P, 2, TT, HEADS, 32])
        sq = sb("sq", [P, 4, 2, TT, T])
        vpair = sb("vpair", [P, HEADS, 32])
        vsum = sb("vsum", [P, GROUPS])
        oT = sb("oT", [P, GROUPS, T])
        rec = sb("rec", [P, TT, HEADS])
        wv = sb("wv", [P, TT, D])
        wvT = sb("wvT", [P, KD, T])
        x1 = sb("x1", [P, TT, D])
        x2 = sb("x2", [P, TT, D])
        scr = sb("scr", [P, TT, D])
        scr2 = sb("scr2", [P, TT, D])
        enc = sb("enc", [P, TT])
        dec = sb("dec", [P, TT])
        h3T = sb("h3T", [P, KD, T])
        rows = [sb(f"rows{k}", [P, 2, TT, ROW]) for k in range(TOPK)]
        sgT = sb("sgT", [P, T])
        hidT = sb("hidT", [P, T])
        stats = sb("stats", [P, 3, TT, 6])
        mv = sb("mv", [P, 3, TT, 2])
        vtmp = sb("vtmp", [P, 3, TT])
        rstd = sb("rstd", [P, 3, TT])
        score = sb("score", [P, TT, E])
        topv = sb("topv", [P, TT, 8])
        topi = sb("topi", [P, TT, 8], U32)
        topf = sb("topf", [P, TT * TOPK])
        ssum = sb("ssum", [P, TT])
        onehot = sb("onehot", [P, TT * TOPK, E])
        chosen = sb("chosen", [P, TT, E], BF16)
        seen = sb("seen", [P, E], BF16)
        pose = sb("pose", [P, TT, E])
        posp = sb("posp", [P, TT * TOPK, E])
        posf = sb("posf", [P, TT * TOPK])
        posi = sb("posi", [P, 2, TT * TOPK], I32)
        acc = sb("acc", [P, NTILES * D])

        sidx_i = sb("sidx_i", [P, 1], I32)
        sidx = sb("sidx", [P, 1])
        cnt = sb("cnt", [P, E])
        cnt_i = sb("cnt_i", [P, 2, E], I32)
        ntl = sb("ntl", [P, E])
        cum = sb("cum", [P, E])
        le = sb("le", [P, E])
        before = sb("before", [P, E])
        taken = sb("taken", [P, E])
        at_expert = sb("at_expert", [P, E])
        lep = sb("lep", [P, E])
        plan = sb("plan", [P, 8])
        plan_i = sb("plan_i", [1, 2 * P + 4], I32)

        LAST = (NB // 2 - 1, 1)
        WLOADS = 7
        ANGLES = 15
        XRING, YRING = 8, 4
        assert SLOTS % XRING + 3 > XRING + 1 and SLOTS + 1 <= P
        sq_flat = sq[:, :, :, :, :].rearrange("p a b c d -> p (a b c d)")
        vaug_flat = vaug[:, :, :, :, :].rearrange("p a b c d -> p (a b c d)")
        at = XRING * ROW
        xs = sq_flat[:, 0:at].rearrange("p (r w) -> p r w", r=XRING)
        exT = sq_flat[:, at:at + 2 * D].rearrange("p (r k t) -> p r k t", r=2, k=KD)
        at += 2 * D
        esg = sq_flat[:, at:at + 2 * M].rearrange("p (r m) -> p r m", r=2)
        at += 2 * M
        ehd = sq_flat[:, at:at + 2 * M].rearrange("p (r m) -> p r m", r=2)
        at += 2 * M
        ehT = sq_flat[:, at:at + 2 * P].rearrange("p (r m) -> p r m", r=2)
        fzero = rotary[:, 0:FROWS * ROW].rearrange("p (r w) -> p r w", r=FROWS)
        ys = vaug_flat[:, 0:YRING * D].rearrange("p (r d) -> p r d", r=YRING)
        CRING = 4
        ypair = stack[:, :, :, :, :].rearrange("p a b c d -> p (a b c d)").bitcast(F32)\
            .rearrange("p (r w) -> p r w", r=CRING)

        bank = [ctx.enter_context(nc.psum_tensor(f"bank{i}", [P, 512], F32)) for i in range(8)]
        PVB, FB, B6, B7 = 4, 5, 6, 7

        th_in = sem("th_in")
        ln_in = sem("ln_in")
        wqk_in = sem("wqk_in")
        wv_in = sem("wv_in")
        wo_in = sem("wo_in")
        ws_in = sem("ws_in")
        fz_ok = sem("fz_ok")
        wex_in = sem("wex_in")
        c_pool = sem("c_pool")
        c_dve = sem("c_dve")
        c_act = sem("c_act")
        f_dve = sem("f_dve")
        null_in = sem("null_in")
        xa_in = [sem(f"xa_in{p}") for p in range(2)]
        xb_in = [sem(f"xb_in{p}") for p in range(2)]
        cx_in = [sem(f"cx_in{p}") for p in range(2)]
        ln_mv = [sem(f"ln_mv{n}") for n in range(3)]
        rr = [sem(f"rr{n}") for n in range(3)]
        xn_ok = sem("xn_ok")
        tx_ps = sem("tx_ps")
        hT_ok = sem("hT_ok")
        qk_ps = sem("qk_ps")
        ro_ok = sem("ro_ok")
        rot_ok = sem("rot_ok")
        hi_ok = sem("hi_ok")
        stk_ok = sem("stk_ok")
        v_ps = sem("v_ps")
        v_ok = sem("v_ok")
        tqk_ps = sem("tqk_ps")
        qkT_ok = sem("qkT_ok")
        vp_ok = sem("vp_ok")
        c_ps = sem("c_ps")
        c_ok = sem("c_ok")
        s_ps = sem("s_ps")
        sq_ok = sem("sq_ok")
        pv_ps = sem("pv_ps")
        o_ok = sem("o_ok")
        to_ps = sem("to_ps")
        rec_ok = sem("rec_ok")
        wv_ok = sem("wv_ok")
        tw_ps = sem("tw_ps")
        wvT_ok = sem("wvT_ok")
        wo_ps = sem("wo_ps")
        x1_ok = sem("x1_ok")
        enc_ok = sem("enc_ok")
        e_ps = sem("e_ps")
        dec_ok = sem("dec_ok")
        x2_ok = sem("x2_ok")
        h3_ok = sem("h3_ok")
        th_ps = sem("th_ps")
        h3T_ok = sem("h3T_ok")
        ga_ps = sem("ga_ps")
        sco_ok = sem("sco_ok")
        sh_ps = sem("sh_ps")
        sg_ok = sem("sg_ok")
        hid_ok = sem("hid_ok")
        ra_ok = sem("ra_ok")
        rk_ps = sem("rk_ps")
        rb_ok = sem("rb_ok")
        dn_ps = sem("dn_ps")
        acc_ok = sem("acc_ok")
        copy_ok = sem("copy_ok")
        sent = [sem(f"sent{p}") for p in range(2)]
        cnt_ps = sem("cnt_ps")
        pl_ok = sem("pl_ok")
        pcol_ok = sem("pcol_ok")
        frow_ok = sem("frow_ok")
        plan_ps = sem("plan_ps")
        plan_ok = sem("plan_ok")
        fill_in = sem("fill_in")
        xs_in = [sem(f"xs_in{r}") for r in range(XRING)]
        etx_ps = sem("etx_ps")
        exT_ok = sem("exT_ok")
        gu_ps = sem("gu_ps")
        esg_ok = sem("esg_ok")
        ehd_ok = sem("ehd_ok")
        etd_ps = sem("etd_ps")
        ehT_ok = sem("ehT_ok")
        edn_ps = sem("edn_ps")
        ys_ok = sem("ys_ok")
        ys_out = [sem(f"ys_out{r}") for r in range(YRING)]
        yp_in = [sem(f"yp_in{r}") for r in range(CRING)]
        f1_ok = sem("f1_ok")
        fin_ok = sem("fin_ok")
        out_done = sem("out_done")
        passed = {nc.vector.engine: sem("passed_dve"), nc.gpsimd.engine: sem("passed_pool")}

        block = ctx.enter_context(nc.Block())

        def wait(eng, s, value):
            if not (isinstance(value, int) and value <= 0):
                eng.wait_ge(s, value)

        def wait_first(eng, s, value):
            wait(eng, s, value)
            if not isinstance(value, int):
                eng.sem_inc(passed[eng.engine], 1)

        def num(b):
            return b[0] * 2 + b[1]

        def pipeline(eng, step):
            step(None, None, None, (0, 0))
            step(None, None, (0, 0), (0, 1))
            step((0, 0), None, (0, 1), (1, 0))
            step((0, 1), (0, 0), (1, 0), (1, 1))
            with eng.Fori(0, NB // 2 - 2) as m:
                step((m + 1, 0), (m, 1), (m + 1, 1), (m + 2, 0))
                step((m + 1, 1), (m + 1, 0), (m + 2, 0), (m + 2, 1))
            u = NB // 2 - 1
            step((u, 0), (u - 1, 1), (u, 1), None)

        def early(step, lo, hi):
            for n in range(lo, hi):
                step(n, n % XRING, None)

        def late(eng, step):
            rounds = SLOTS // XRING
            with eng.Fori(EARLY // XRING, rounds) as m:
                for c in range(XRING):
                    step(m * XRING + c, c, m)
            for n in range(rounds * XRING, SLOTS + 3):
                step(n, n - rounds * XRING, None)

        def read_plan(eng, at, count, top):
            return nc.values_load_multi_w_load_instructions(
                plan_i[0:1, bass.ds(at, count)], engines=[eng.engine], min_val=0, max_val=top,
                skip_runtime_bounds_check_because="the plan clamps the expert, and an expert's tiles end within its rows")[1]

        def keep_T(eng, copy, j, b, t, which):
            eng.wait_ge(tqk_ps, 4 * j + 2 * t + which + 1)
            wait(eng, s_ps, 8 * (j - 1))
            copy((qT, kT)[which][:, b[1], :, t * P:(t + 1) * P],
                 bank[FB][:, :].bitcast(F16).rearrange("p (a c) -> p a c", c=P)).then_inc(qkT_ok, 1)

        xv = x.rearrange("b (t p) d -> b p t d", p=P)
        cv = ctx_in.rearrange("b (t p) d -> b p t d", p=P)

        def first(b):
            return b is not None and isinstance(b[0], int) and b == (0, 0)

        @block.sync
        def _(sp):
            def load_x(j, b):
                wait(sp, xn_ok, j - 1)
                sp.dma_start(xa[:, b[1], :, :], xv[bass.ds(j, 1), :, :, :].rearrange("o p t d -> p (o t) d")).then_inc(xa_in[b[1]], 16)

            def load_back(j, b):
                wait(sp, x1_ok, j - 1)
                sp.dma_start(xb[:, b[1], :, :], xv[bass.ds(j, 1), :, :, :].rearrange("o p t d -> p (o t) d")).then_inc(xb_in[b[1]], 16)
                sp.dma_start(cx[:, b[1], :, :], cv[bass.ds(j, 1), :, :, :].rearrange("o p t d -> p (o t) d")).then_inc(cx_in[b[1]], 16)

            load_x(0, (0, 0))
            sp.dma_start(wqk[:, :, 0:D], w_q.rearrange("(k p) n -> p k n", p=P)).then_inc(wqk_in, 16)
            sp.dma_start(wqk[:, :, D:2 * D], w_kv[:, 0:D].rearrange("(k p) n -> p k n", p=P)).then_inc(wqk_in, 16)
            load_x(1, (0, 1))
            sp.dma_start(wo[:, :, :], w_o.rearrange("(k p) n -> p k n", p=P)).then_inc(wo_in, 16)
            sp.dma_start(wenc[:, :], mlp_w[0, 0:D].partition_broadcast(P)).then_inc(ws_in, 16)
            sp.dma_start(wdec[:, :], mlp_w[0, D:2 * D].partition_broadcast(P)).then_inc(ws_in, 16)
            sp.dma_start(mbias[:, :], mlp_b.partition_broadcast(P)).then_inc(ws_in, 16)
            sp.dma_start(gwT[:, :, :], gate_wT.rearrange("(k p) e -> p k e", p=P)).then_inc(ws_in, 16)
            sp.dma_start(wsgu[:, :, 0:M], ws_gate.rearrange("(k p) m -> p k m", p=P)).then_inc(ws_in, 16)
            sp.dma_start(wsgu[:, :, M:2 * M], ws_up.rearrange("(k p) m -> p k m", p=P)).then_inc(ws_in, 16)
            sp.dma_start(wsd[:, :], ws_down).then_inc(ws_in, 16)
            for i in range(2):
                load_back(i, (0, i))
                load_x(i + 2, (1, i))
            with sp.Fori(0, NB // 2 - 2) as m:
                for p in range(2):
                    load_x(m * 2 + p + 4, (m + 2, p))
                    load_back(m * 2 + p + 2, (m + 1, p))
            for p in range(2):
                load_back(NB - 2 + p, (NB // 2 - 1, p))

            first_rows = []

            def load_slot(n, c, m):
                if isinstance(n, int) and n >= SLOTS:
                    return
                if c == 0:
                    first_rows[:] = read_plan(sp, n, XRING, XROWS - P)
                q = n // YRING if isinstance(n, int) else m * 2 + c // YRING
                wait(sp, ys_out[c % YRING], (q - 1) * 16)
                sp.dma_start(xs[:, c, :], disp[bass.ds(first_rows[c], P), :]).then_inc(xs_in[c], 16)

            sp.wait_ge(plan_ok, 2)
            for p in range(2):
                sp.wait_ge(sent[p], 16 * TT * TOPK * (PLANNED // 2))
            sp.wait_ge(pv_ps, GROUPS * NB)
            early(load_slot, 0, EARLY)
            sp.wait_ge(plan_ok, 4)
            sp.wait_ge(fill_in, 16 * FDMAS)
            sp.wait_ge(null_in, 16)
            for p in range(2):
                sp.wait_ge(sent[p], 16 * TT * TOPK * (NB // 2))
            late(sp, load_slot)

            for r in range(YRING):
                sp.wait_ge(ys_out[r], 16 * len(range(r, SLOTS, YRING)))
            yv = yexp.rearrange("(n k) d -> n (k d)", k=TOPK)
            for r in range(CRING):
                sp.dma_start(ypair[:, r, :], yv[r * P:(r + 1) * P, :]).then_inc(yp_in[r], 16)
            with sp.Fori(0, NTILES // CRING - 1) as m:
                for r in range(CRING):
                    sp.wait_ge(fin_ok, m * CRING + r + 1)
                    sp.dma_start(ypair[:, r, :], yv[bass.ds((m * CRING + r + CRING) * P, P), :]).then_inc(yp_in[r], 16)
            sp.wait_ge(out_done, 16 * NTILES)

        @block.gpsimd
        def _(pool):
            pool.memset(identf[:, :], 0.0).then_inc(c_pool, 1)
            pool.memset(identh[:, :], 0.0).then_inc(c_pool, 1)
            pool.memset(tri[:, :], 1.0).then_inc(c_pool, 1)
            pool.wait_ge(c_pool, 3)
            pool.affine_select(out=identf[:, :], in_=identf[:, :], compare_op=ALU.not_equal, fill=1.0,
                               base=0, pattern=[[-1, P]], channel_multiplier=1).then_inc(c_pool, 1)
            pool.affine_select(out=identh[:, :], in_=identh[:, :], compare_op=ALU.not_equal, fill=1.0,
                               base=0, pattern=[[-1, P]], channel_multiplier=1).then_inc(c_pool, 1)
            pool.affine_select(out=tri[:, :], in_=tri[:, :], compare_op=ALU.is_gt, fill=0.0,
                               base=0, pattern=[[1, P]], channel_multiplier=-1).then_inc(c_pool, 1)
            pool.iota(iota_i[:, :], [[1, E]], base=0, channel_multiplier=0).then_inc(c_pool, 1)
            pool.iota(ebase_i[:, :], [[EROWS, E]], base=0, channel_multiplier=0).then_inc(c_pool, 1)
            pool.iota(tok_i[:, :], [[P, TT]], base=0, channel_multiplier=1).then_inc(c_pool, 1)
            pool.iota(idi[:, :, :], [[1, TOPK], [P * TOPK, TT]], base=0, channel_multiplier=TOPK).then_inc(c_pool, 1)
            pool.iota(filler[:, D:D + 1].bitcast(I32), [[0, 1]], base=SKIP_ROW, channel_multiplier=0).then_inc(c_pool, 1)
            pool.iota(sidx_i[:, :], [[0, 1]], base=0, channel_multiplier=1).then_inc(c_pool, 1)
            pool.iota(fidx_i[:, 0, :], [[P, FDMAS]], base=0, channel_multiplier=1).then_inc(c_pool, 1)

            def power(n, j, a, b):
                wait_first(pool, ln_mv[n], 4 * j + 4)
                pool.tensor_scalar(vtmp[:, n, :], mv[:, n, :, 1], a, b, ALU.mult, ALU.add).then_inc(rr[n], 1)
                pool.wait_ge(rr[n], 2 * j + 1)
                pool.tensor_tensor(rstd[:, n, :], vtmp[:, n, :], halfneg[:, :], ALU.pow).then_inc(rr[n], 1)

            def rotate(j, t):
                pool.wait_ge(ro_ok, 2 * j + t + 1)
                wait(pool, stk_ok, 6 * j + 3 * t - 5)
                pool.tensor_tensor(rot[:, t, :], rt1[:, t, :], rt2[:, t, :], ALU.add).then_inc(rot_ok, 1)

            pool.wait_ge(c_dve, 1)

            def copy_rows(j, p):
                wait_first(pool, h3_ok, j + 1)
                for t in range(TT):
                    last = pool.tensor_scalar(rows[1][:, p, t, 0:D], rows[0][:, p, t, 0:D], 1.0, 0.0, ALU.mult, ALU.add)
                last.then_inc(copy_ok, 1)

            def scatter(j, p, t):
                if t == 0:
                    pool.wait_ge(copy_ok, j + 1)
                    pool.wait_ge(ra_ok, 15 * j + 15)
                    wait_first(pool, rb_ok, 6 * j + 6)
                for k in range(TOPK):
                    i = t * TOPK + k
                    pool.indirect_dma_start(
                        disp, bass.IndirectOffsetOnAxis(ap=posi[:, p, i:i + 1].bitcast(U32), axis=0),
                        rows[k][:, p, t, :], None).then_inc(sent[p], 16)

            def sum_tiles(j, p):
                pool.wait_ge(v_ok, j + 1)
                wait(pool, c_ps, j)
                pool.tensor_tensor(vpair[:, :, 0:HD], vaug[:, p, 0, :, 0:HD], vaug[:, p, 1, :, 0:HD], ALU.add).then_inc(vp_ok, 1)

            def step(att, back, front, nxt):
                jb = num(back) if back else None
                jf = num(front) if front else None
                jn = num(nxt) if nxt else None
                if front:
                    rotate(jf, 0)
                if back:
                    power(1, jb, 1.0, EPS)
                if front:
                    rotate(jf, 1)
                if back:
                    power(2, jb, 1.0, EPS)
                if front:
                    sum_tiles(jf, front[1])
                if nxt:
                    power(0, jn, 1.0 + EPS, EPS * EPS)
                if back:
                    copy_rows(jb, back[1])
                    scatter(jb, back[1], 0)
                    scatter(jb, back[1], 1)

            def send(n, c, m):
                if isinstance(n, int) and n < 3:
                    return
                wait_first(pool, ys_ok, n - 2)
                r, y = (c - 3) % XRING, (c - 3) % YRING
                pool.indirect_dma_start(
                    yexp, bass.IndirectOffsetOnAxis(ap=xs[:, r, D:D + 1].bitcast(U32), axis=0),
                    ys[:, y, :], None, bounds_check=YROWS - 1, oob_is_err=False).then_inc(ys_out[y], 16)

            pipeline(pool, step)

            def fill(i):
                if i == 0:
                    pool.wait_ge(fz_ok, 2)
                    pool.wait_ge(frow_ok, 1)
                pool.indirect_dma_start(
                    disp.rearrange("r (w o) -> (r w) o", o=1), bass.IndirectOffsetOnAxis(ap=frow[:, i:i + 1].bitcast(U32), axis=0),
                    fzero[:, :, :].rearrange("p r w -> p (r w)"), None).then_inc(fill_in, 16)

            assert FDMAS == 2
            pool.wait_ge(stk_ok, 6 * NB)
            pool.memset(fzero[:, :, :], 0.0).then_inc(fz_ok, 1)
            pool.wait_ge(fz_ok, 1)
            pool.iota(fzero[:, :, D].bitcast(I32), [[0, FROWS]], base=SKIP_ROW, channel_multiplier=0).then_inc(fz_ok, 1)
            power(1, NB - 2, 1.0, EPS)
            power(2, NB - 2, 1.0, EPS)
            copy_rows(NB - 2, 0)
            early(send, 0, 2)
            scatter(NB - 2, 0, 0)
            scatter(NB - 2, 0, 1)
            early(send, 2, 3)
            power(1, NB - 1, 1.0, EPS)
            early(send, 3, 6)
            power(2, NB - 1, 1.0, EPS)
            early(send, 6, 8)
            copy_rows(NB - 1, 1)
            early(send, 8, 12)
            scatter(NB - 1, 1, 0)
            early(send, 12, 14)
            scatter(NB - 1, 1, 1)
            early(send, 14, 16)
            fill(0)
            fill(1)
            early(send, 16, EARLY)
            late(pool, send)

        @block.scalar
        def _(act):
            act.dma_start(theta_c[:, :], theta.partition_broadcast(P)).then_inc(th_in, 16)
            act.dma_start(lnw_c[:, :], ln_w).then_inc(ln_in, 16)
            act.dma_start(lnb_c[:, :], ln_b).then_inc(ln_in, 16)
            act.dma_start(wv_w[:, :, :], w_kv[:, D:2 * D].rearrange("(k p) n -> p k n", p=P)).then_inc(wv_in, 16)
            act.preload_act_table_set("silu_and_others")

            def rotary_tables():
                act.wait_ge(c_dve, ANGLES)
                act.activation(sinr[:, :, :, 1], ang[:, :, :], ACT.Sin).then_inc(c_act, 1)
                act.activation(cosr[:, :, :, 0], angc[:, :, :], ACT.Sin).then_inc(c_act, 1)
                act.activation(cosr[:, :, :, 1], angc[:, :, :], ACT.Sin).then_inc(c_act, 1)
                act.activation(sinr[:, :, :, 0], ang[:, :, :], ACT.Sin, scale=-1.0).then_inc(c_act, 1)
                act.preload_act_table_set("sigmoid_and_others")

            def load_experts():
                we = wex[:, :].rearrange("p (e n) -> p e n", e=E)
                for k in range(KD):
                    at = k * 2 * M
                    act.dma_start(we[:, :, at:at + M], w_gate[:, k * P:(k + 1) * P, :].rearrange("e p m -> p e m")).then_inc(wex_in, 16)
                    act.dma_start(we[:, :, at + M:at + 2 * M], w_up[:, k * P:(k + 1) * P, :].rearrange("e p m -> p e m")).then_inc(wex_in, 16)
                act.dma_start(we[:, :, KD * 2 * M:WE], w_down.rearrange("e p n -> p e n")).then_inc(wex_in, 16)
                act.wait_ge(c_pool, 11)
                act.wait_ge(c_dve, 1)
                act.dma_start(disp[E * EROWS:XROWS, :].rearrange("(n p) w -> p n w", p=P),
                              filler[:, :].unsqueeze(1).to_broadcast([P, NULLS, ROW])).then_inc(null_in, 16)

            def squares(j, a):
                act.wait_ge(s_ps, 8 * j + a + 1)
                g = a // 2
                wait(act, pv_ps, GROUPS * j + g - 1)
                for b in range(2):
                    src = bank[2 * (a % 2) + b]
                    last = act.activation(sq[:, a % 4, b, :, :].rearrange("p a b -> p (a b)"), src[:, :],
                                          ACT.Square, scale=HD ** -0.5, bias=1.0)
                last.then_inc(sq_ok, 1)

            def attended(j, b, h):
                act.wait_ge(pv_ps, GROUPS * j + 2 * h + 2)
                if h == 0:
                    act.wait_ge(c_ok, j + 1)
                    wait(act, to_ps, TT * j)
                for g in range(2):
                    last = act.activation(oT[:, 2 * h + g, :], bank[PVB][:, g * T:(g + 1) * T], ACT.Identity,
                                          bias=vsum[:, 2 * h + g:2 * h + g + 1])
                last.then_inc(o_ok, 1)

            def high_part(j, t):
                act.wait_ge(rot_ok, 2 * j + t + 1)
                wait(act, tqk_ps, 4 * j + 2 * t - 2)
                act.activation(stack[:, t, :, 0, :], rot[:, t, :].rearrange("p (h d) -> p h d", d=HD),
                               ACT.Copy).then_inc(hi_ok, 1)

            def keep_wvT(jb):
                act.wait_ge(tw_ps, jb + 1)
                wait(act, wo_ps, jb)
                act.activation(wvT[:, :, :].rearrange("p k (t c) -> p t k c", t=TT),
                               bank[B6][:, :].rearrange("p (t k c) -> p t k c", t=TT, k=KD), ACT.Copy).then_inc(wvT_ok, 1)

            def keep_h3T(jb):
                act.wait_ge(th_ps, jb + 1)
                wait(act, sh_ps, jb)
                act.activation(h3T[:, :, :].rearrange("p k (t c) -> p t k c", t=TT),
                               bank[B7][:, :].rearrange("p (t k c) -> p t k c", t=TT, k=KD), ACT.Copy).then_inc(h3T_ok, 1)

            def sigmoids(jb):
                act.wait_ge(ga_ps, jb + 1)
                wait(act, ra_ok, 15 * jb)
                act.activation(score[:, :, :].rearrange("p t e -> p (t e)"), bank[B6][:, 0:TT * E], ACT.Sigmoid).then_inc(sco_ok, 1)
                act.wait_ge(sh_ps, jb + 1)
                wait(act, hid_ok, 2 * jb)
                act.activation(sgT[:, :], bank[B7][:, 0:T], ACT.Sigmoid).then_inc(sg_ok, 1)

            def copy(out, in_):
                return act.activation(out, in_, ACT.Copy)

            def keep_hT(jf):
                if isinstance(jf, int) and jf == 0:
                    act.wait_ge(ln_in, 32)
                act.wait_ge(tx_ps, jf + 1)
                wait(act, v_ps, jf)
                for k in range(KD):
                    last = act.activation(hT[:, k, :].rearrange("p (t c) -> p t c", t=TT),
                                          bank[FB][:, :].rearrange("p (t k c) -> p k t c", t=TT, k=KD)[:, k, :, :],
                                          ACT.Identity, scale=lnw_c[:, k:k + 1], bias=lnb_c[:, k:k + 1])
                last.then_inc(hT_ok, 1)

            def keep_v(jf, p):
                act.wait_ge(v_ps, jf + 1)
                wait(act, pv_ps, GROUPS * (jf - 1))
                act.activation(vaug[:, p, :, :, 0:HD].rearrange("p t h d -> p (t h) d"),
                               bank[FB][:, :].rearrange("p (a d) -> p a d", d=HD), ACT.Copy).then_inc(v_ok, 1)

            def step(att, back, front, nxt):
                ja = num(att) if att else None
                jb = num(back) if back else None
                jf = num(front) if front else None
                if front:
                    keep_hT(jf)
                if first(front):
                    rotary_tables()
                if first(att):
                    load_experts()
                if att:
                    squares(ja, 0)
                if back:
                    keep_wvT(jb)
                if att:
                    squares(ja, 1)
                if front:
                    high_part(jf, 0)
                if att:
                    squares(ja, 2)
                    squares(ja, 3)
                if front:
                    high_part(jf, 1)
                    keep_v(jf, front[1])
                if att:
                    squares(ja, 4)
                    squares(ja, 5)
                if back:
                    keep_h3T(jb)
                if att:
                    attended(ja, att, 0)
                    squares(ja, 6)
                    squares(ja, 7)
                if back:
                    sigmoids(jb)
                if front:
                    keep_T(act, copy, jf, front, 1, 1)
                if att:
                    attended(ja, att, 1)

            def expert(n, c, m):
                small = isinstance(n, int)
                if not small or n < SLOTS:
                    act.wait_ge(etx_ps, n + 1)
                    if not small or n >= 2:
                        act.wait_ge(gu_ps, n - 1)
                    act.activation(exT[:, c % 2, :, :].rearrange("p k t -> p (k t)"), bank[c % 2][:, 0:D], ACT.Copy).then_inc(exT_ok, 1)
                if not small or 1 <= n <= SLOTS:
                    r = (c - 1) % 2
                    act.wait_ge(gu_ps, n)
                    if not small or n >= 3:
                        act.wait_ge(ehd_ok, n - 2)
                    act.activation(esg[:, r, :], bank[2 + r][:, 0:M], ACT.Silu).then_inc(esg_ok, 1)

            pipeline(act, step)

            keep_wvT(NB - 2)
            squares(NB - 1, 0)
            squares(NB - 1, 1)
            squares(NB - 1, 2)
            squares(NB - 1, 3)
            squares(NB - 1, 4)
            squares(NB - 1, 5)
            attended(NB - 1, LAST, 0)
            squares(NB - 1, 6)
            squares(NB - 1, 7)
            attended(NB - 1, LAST, 1)
            act.wait_ge(pv_ps, GROUPS * NB)
            keep_h3T(NB - 2)
            early(expert, 0, 1)
            sigmoids(NB - 2)
            early(expert, 1, 2)
            keep_wvT(NB - 1)
            early(expert, 2, 8)
            keep_h3T(NB - 1)
            early(expert, 8, 10)
            sigmoids(NB - 1)
            early(expert, 10, EARLY)
            late(act, expert)

            with act.Fori(0, NTILES) as m:
                act.wait_ge(fin_ok, m + 1)
                act.dma_start(out.rearrange("b t d -> (b t) d")[bass.ds(m * P, P), :],
                              acc[:, bass.ds(m * D, D)]).then_inc(out_done, 16)

        @block.vector
        def _(dve):
            dve.memset(filler[:, 0:D], 0.0)
            dve.memset(filler[:, D + 1:D + 2], 0.0)
            dve.memset(seen[:, :], 0.0)
            dve.memset(onesb[:, :], 1.0)
            dve.memset(onesf[:, :], 1.0)
            dve.memset(vaug[:, :, :, :, HD + 1:32].rearrange("p a t h d -> p (a t h) d"), 0.0)
            dve.memset(vaug[:, :, :, :, HD:HD + 1].rearrange("p a t h d -> p (a t h) d"), 1.0)
            dve.memset(vpair[:, :, HD + 1:32], 0.0)
            dve.memset(vpair[:, :, HD:HD + 1], float(TT))
            dve.memset(halfneg[:, :], -0.5).then_inc(c_dve, 1)
            dve.wait_ge(c_pool, 13)
            dve.tensor_copy(iota16[:, :], iota_i[:, :])
            dve.tensor_copy(ebase[:, :], ebase_i[:, :])
            dve.tensor_copy(idf[:, :, :], idi[:, :, :])
            dve.tensor_copy(sidx[:, :], sidx_i[:, :])
            dve.tensor_single_scalar(fidx_i[:, 1, :], fidx_i[:, 0, :], 4, op=ALU.arith_shift_right).then_inc(f_dve, 1)
            dve.tensor_copy(tokf[:, :], tok_i[:, :])
            for i, v in enumerate(mel_base()):
                last = dve.memset(freq[:, i:i + 1], v)
            last.then_inc(c_dve, 1)
            def rotary_angles():
                dve.wait_ge(th_in, 16)
                dve.tensor_scalar(theta_c[:, :], theta_c[:, :], float(np.float32(1.0) / np.float32(220.0)), None, ALU.mult).then_inc(c_dve, 1)
                dve.wait_ge(c_dve, 3)
                dve.tensor_scalar(freq[:, :], freq[:, :], theta_c[:, 0:1], None, ALU.mult).then_inc(c_dve, 1)
                dve.wait_ge(c_dve, 4)
                for t in range(TT):
                    last = dve.tensor_scalar(ang[:, t, :], freq[:, :], tokf[:, t:t + 1], None, ALU.mult)
                last.then_inc(c_dve, 1)
                dve.wait_ge(c_dve, 5)
                dve.tensor_scalar(turns[:, :, :], ang[:, :, :], float(1.0 / (2 * np.pi)), MAGIC, ALU.mult, ALU.add).then_inc(c_dve, 1)
                dve.wait_ge(c_dve, 6)
                dve.tensor_scalar(turns[:, :, :], turns[:, :, :], -MAGIC, None, ALU.add).then_inc(c_dve, 1)
                n = 7
                for c in two_pi_parts():
                    dve.wait_ge(c_dve, n)
                    dve.scalar_tensor_tensor(ang[:, :, :], turns[:, :, :], -c, ang[:, :, :], ALU.mult, ALU.add).then_inc(c_dve, 1)
                    n += 1
                dve.wait_ge(c_dve, n)
                dve.tensor_scalar(angc[:, :, :], ang[:, :, :], float(np.pi / 2), None, ALU.add).then_inc(c_dve, 1)
                dve.wait_ge(c_dve, n + 1)
                dve.tensor_scalar(wrap[:, :, :], angc[:, :, :], float(np.pi), None, ALU.is_gt).then_inc(c_dve, 1)
                dve.wait_ge(c_dve, n + 2)
                dve.scalar_tensor_tensor(angc[:, :, :], wrap[:, :, :], float(-2 * np.pi), angc[:, :, :], ALU.mult, ALU.add).then_inc(c_dve, 1)
                dve.wait_ge(c_dve, n + 3)
                lim = 3.1415925
                dve.tensor_scalar(angc[:, :, :], angc[:, :, :], lim, -lim, ALU.min, ALU.max).then_inc(c_dve, 1)
                dve.tensor_scalar(ang[:, :, :], ang[:, :, :], lim, -lim, ALU.min, ALU.max).then_inc(c_dve, 1)
                assert n + 5 == ANGLES

            def filler_index():
                dve.wait_ge(f_dve, 1)
                dve.tensor_copy(fidx[:, :, :], fidx_i[:, :, :]).then_inc(f_dve, 1)
                dve.wait_ge(f_dve, 2)
                dve.tensor_tensor(fmask[:, :, :], iota16[:, :].unsqueeze(1).to_broadcast([P, FDMAS, E]),
                                  fidx[:, 1, :].unsqueeze(2).to_broadcast([P, FDMAS, E]), ALU.is_equal).then_inc(f_dve, 1)
                dve.tensor_scalar(fbase[:, :], fidx[:, 1, :], float(EROWS - P), None, ALU.mult).then_inc(f_dve, 1)
                dve.wait_ge(f_dve, 4)
                dve.scalar_tensor_tensor(fbase[:, :], fidx[:, 0, :], float(FROWS), fbase[:, :], ALU.mult, ALU.add).then_inc(f_dve, 1)
                dve.wait_ge(f_dve, 5)
                dve.tensor_scalar(fbase[:, :], fbase[:, :], float(ROW), None, ALU.mult).then_inc(f_dve, 1)
                dve.memset(plan_i[0:1, P:P + 4], 0).then_inc(f_dve, 1)

            def norm_stats(n, j, src):
                for t in range(TT):
                    dve.bn_stats(stats[:, n, t, :], src[:, t, :]).then_inc(ln_mv[n], 1)
                for t in range(TT):
                    wait_first(dve, ln_mv[n], 4 * j + t + 1)
                    dve.bn_aggr(mv[:, n, t, :], stats[:, n, t, :]).then_inc(ln_mv[n], 1)

            def rope(j, t):
                dve.wait_ge(qk_ps, 2 * j + t + 1)
                if t == 0 and isinstance(j, int) and j == 0:
                    dve.wait_ge(c_act, 4)
                wait(dve, rot_ok, 2 * j + t - 1)
                src = bank[FB][:, :].rearrange("p (h d c) -> p h d c", d=HD // 2, c=2)
                swapped = bass.AP(src.tensor, src.offset + 1, [list(src.ap[0]), [HD, 2 * HEADS], [2, HD // 2], [-1, 2]])
                shape = [P, 2 * HEADS, HD // 2, 2]
                dst = [r[:, t, :].rearrange("p (h d c) -> p h d c", d=HD // 2, c=2) for r in (rt1, rt2)]
                dve.tensor_tensor(dst[0], src, cosr[:, t, :, :].unsqueeze(1).to_broadcast(shape), ALU.mult)
                dve.tensor_tensor(dst[1], swapped, sinr[:, t, :, :].unsqueeze(1).to_broadcast(shape), ALU.mult).then_inc(ro_ok, 1)

            def low_part(j, t):
                dve.wait_ge(hi_ok, 2 * j + t + 1)
                wait(dve, tqk_ps, 4 * j + 2 * t - 2)
                st = stack[:, t, :, :, :]
                dve.tensor_tensor(st[:, :, 2, :], rot[:, t, :].rearrange("p (h d) -> p h d", d=HD), st[:, :, 0, :], ALU.subtract).then_inc(stk_ok, 1)
                dve.wait_ge(stk_ok, 6 * j + 3 * t + 1)
                dve.tensor_copy(st[:, 0:HEADS, 1:4:2, :], st[:, 0:HEADS, 0:4:2, :]).then_inc(stk_ok, 1)
                kk = st[:, HEADS:2 * HEADS, :, :]
                back_to_front = bass.AP(kk.tensor, kk.offset + 3 * HD, [list(kk.ap[0]), [4 * HD, HEADS], [-2 * HD, 2], [1, HD]])
                dve.tensor_copy(back_to_front, kk[:, :, 0:4:2, :]).then_inc(stk_ok, 1)

            done = [0]

            def then(instruction):
                instruction.then_inc(pl_ok, 1)
                done[0] += 1
                dve.wait_ge(pl_ok, done[0])

            def plan_slots(b, start, slot=None):
                dve.wait_ge(cnt_ps, 2 if start else 1)
                then(dve.tensor_copy(cnt[:, :], bank[b][:, 0:E]))
                if start:
                    dve.wait_ge(f_dve, 7)
                    then(dve.tensor_tensor(fprod[:, :, :], fmask[:, :, :], cnt[:, :].unsqueeze(1).to_broadcast([P, FDMAS, E]), ALU.mult))
                    then(dve.reduce_sum(fcnt[:, :], fprod[:, :, :], AX.X))
                    dve.scalar_tensor_tensor(frow[:, :], fcnt[:, :], float(ROW), fbase[:, :], ALU.mult, ALU.add).then_inc(frow_ok, 1)
                then(dve.tensor_scalar(cnt_i[:, 0, :], cnt[:, :], float(P - 1 if start else 0), None, ALU.add))
                then(dve.tensor_single_scalar(cnt_i[:, 1, :], cnt_i[:, 0, :], 7, op=ALU.arith_shift_right))
                then(dve.tensor_copy(ntl[:, :], cnt_i[:, 1, :]))
                if start:
                    then(dve.tensor_tensor(ntl[:, :], ntl[:, :], taken[:, :], ALU.subtract))
                then(dve.tensor_tensor_scan(cum[:, :], onesf[:, :], ntl[:, :], float(start), ALU.mult, ALU.add))
                then(dve.tensor_scalar(le[:, :], cum[:, :], sidx[:, 0:1], None, ALU.is_le))
                if start:
                    early(expert, slot, slot + 1)
                then(dve.reduce_sum(plan[:, 0:1], le[:, :], AX.X))
                then(dve.tensor_tensor(lep[:, :], le[:, :], ntl[:, :], ALU.mult))
                then(dve.reduce_sum(plan[:, 1:2], lep[:, :], AX.X))
                then(dve.tensor_tensor(plan[:, 2:3], sidx[:, :], plan[:, 1:2], ALU.subtract))
                if start:
                    dve.tensor_scalar(at_expert[:, :], iota16[:, :], plan[:, 0:1], None, ALU.is_equal)
                    then(dve.tensor_scalar(plan[:, 2:3], plan[:, 2:3], float(-start), None, ALU.add))
                    then(dve.tensor_tensor(at_expert[:, :], at_expert[:, :], taken[:, :], ALU.mult))
                    then(dve.reduce_sum(plan[:, 6:7], at_expert[:, :], AX.X))
                    then(dve.tensor_tensor(plan[:, 2:3], plan[:, 2:3], plan[:, 6:7], ALU.add))
                dve.tensor_scalar(plan[:, 5:6], plan[:, 0:1], float(E - 1), float(WE), ALU.min, ALU.mult).then_inc(pcol_ok, 1)
                then(dve.tensor_scalar(plan[:, 3:4], plan[:, 0:1], float(EROWS), None, ALU.mult))
                dve.scalar_tensor_tensor(plan[:, 4:5], plan[:, 2:3], float(P), plan[:, 3:4], ALU.mult, ALU.add).then_inc(pcol_ok, 1)
                if not start:
                    then(dve.tensor_tensor(before[:, :], cum[:, :], ntl[:, :], ALU.subtract))
                    then(dve.tensor_scalar(before[:, :], before[:, :], float(EARLY), None, ALU.min))
                    then(dve.tensor_scalar(taken[:, :], cum[:, :], float(EARLY), None, ALU.min))
                    then(dve.tensor_tensor(taken[:, :], taken[:, :], before[:, :], ALU.subtract))

            def keep_plan(b, lo, hi):
                dve.wait_ge(plan_ps, 2 if lo else 1)
                dve.tensor_copy(plan_i[0:1, lo:hi], bank[b][0:1, lo:hi]).then_inc(plan_ok, 1)
                dve.tensor_copy(plan_i[0:1, P + 4 + lo:P + 4 + hi], bank[b][0:1, P + lo:P + hi]).then_inc(plan_ok, 1)

            halves = [0]

            def divide(jb, pb):
                for t in range(TT):
                    dve.wait_ge(to_ps, TT * jb + t + 1)
                    o = bank[(B6, B7)[t]][:, :].rearrange("p (h c) -> p h c", c=32)
                    dve.reciprocal(rec[:, t, :].unsqueeze(2), o[:, :, HD:HD + 1]).then_inc(rec_ok, 1)
                    dve.wait_ge(rec_ok, TT * jb + t + 1)
                    wait(dve, tw_ps, jb)
                    dve.tensor_tensor(wv[:, t, :].rearrange("p (h d) -> p h d", d=HD), o[:, :, 0:HD],
                                      rec[:, t, :].unsqueeze(2).to_broadcast([P, HEADS, HD]), ALU.mult).then_inc(wv_ok, 1)

            def project_context(jb, pb):
                if isinstance(jb, int) and jb == 0:
                    dve.wait_ge(ws_in, 16 * WLOADS)
                dve.wait_ge(cx_in[pb], halves[0] * 16 + 16)
                wait(dve, e_ps, jb)
                for t in range(TT):
                    dve.scalar_tensor_tensor(scr[:, t, :], cx[:, pb, t, :], 1.0, wenc[:, :], ALU.mult, ALU.mult,
                                             accum_out=enc[:, t:t + 1]).then_inc(enc_ok, 1)

            def residual_one(jb, pb):
                dve.wait_ge(wo_ps, jb + 1)
                dve.wait_ge(xb_in[pb], halves[0] * 16 + 16)
                dve.tensor_tensor(x1[:, :, :].rearrange("p t d -> p (t d)"), bank[B7][:, :],
                                  xb[:, pb, :, :].rearrange("p t d -> p (t d)"), ALU.add).then_inc(x1_ok, 1)
                dve.wait_ge(x1_ok, jb + 1)
                norm_stats(1, jb, x1)
                dve.wait_ge(ln_mv[1], 4 * jb + 4)
                for t in range(TT):
                    dve.scalar_tensor_tensor(scr2[:, t, :], x1[:, t, :], mv[:, 1, t, 0:1], wdec[:, :], ALU.subtract, ALU.mult,
                                             accum_out=dec[:, t:t + 1]).then_inc(dec_ok, 1)

            def residual_two(jb, pb):
                dve.wait_ge(rr[1], 2 * jb + 2)
                dve.wait_ge(dec_ok, 4 * jb + 2)
                dve.tensor_tensor(dec[:, :], dec[:, :], rstd[:, 1, :], ALU.mult).then_inc(dec_ok, 1)
                dve.wait_ge(dec_ok, 4 * jb + 3)
                dve.tensor_scalar(dec[:, :], dec[:, :], mbias[:, 0:1], None, ALU.add).then_inc(dec_ok, 1)
                dve.wait_ge(dec_ok, 4 * jb + 4)
                dve.wait_ge(e_ps, jb + 1)
                for t in range(TT):
                    last = dve.scalar_tensor_tensor(x2[:, t, :], x1[:, t, :], dec[:, t:t + 1], bank[B6][:, 0:D], ALU.add, ALU.add)
                last.then_inc(x2_ok, 1)
                dve.wait_ge(x2_ok, jb + 1)
                norm_stats(2, jb, x2)

            def norm_three(jb, pb):
                dve.wait_ge(rr[2], 2 * jb + 2)
                wait(dve, sent[pb], halves[0] * (16 * TT * TOPK))
                for t in range(TT):
                    last = dve.tensor_scalar(rows[0][:, pb, t, 0:D], x2[:, t, :], mv[:, 2, t, 0:1], rstd[:, 2, t:t + 1],
                                             ALU.subtract, ALU.mult)
                last.then_inc(h3_ok, 1)

            def top_experts(jb, pb):
                wait_first(dve, sco_ok, jb + 1)
                for t in range(TT):
                    dve.max(topv[:, t, :], score[:, t, :]).then_inc(ra_ok, 1)
                wait_first(dve, ra_ok, 15 * jb + 2)
                for t in range(TT):
                    dve.max_index(topi[:, t, :], topv[:, t, :], score[:, t, :]).then_inc(ra_ok, 1)
                dve.tensor_tensor(ssum[:, :], topv[:, :, 0], topv[:, :, 1], ALU.add).then_inc(ra_ok, 1)
                dve.wait_ge(ra_ok, 15 * jb + 4)
                dve.tensor_copy(topf[:, :].rearrange("p (t k) -> p t k", k=TOPK), topi[:, :, 0:TOPK]).then_inc(ra_ok, 1)
                dve.wait_ge(ra_ok, 15 * jb + 5)
                dve.tensor_scalar(ssum[:, :], ssum[:, :], 1e-20, None, ALU.add).then_inc(ra_ok, 1)
                dve.wait_ge(ra_ok, 15 * jb + 6)
                dve.tensor_tensor(onehot[:, :, :], iota16[:, :].unsqueeze(1).to_broadcast([P, TT * TOPK, E]),
                                  topf[:, :].unsqueeze(2).to_broadcast([P, TT * TOPK, E]), ALU.is_equal).then_inc(ra_ok, 1)
                dve.wait_ge(ra_ok, 15 * jb + 7)
                dve.reciprocal(ssum[:, :], ssum[:, :]).then_inc(ra_ok, 1)
                dve.wait_ge(ra_ok, 15 * jb + 8)
                oh = onehot[:, :, :].rearrange("p (t k) e -> p t k e", k=TOPK)
                dve.tensor_tensor(chosen[:, :, :], oh[:, :, 0, :], oh[:, :, 1, :], ALU.add).then_inc(ra_ok, 1)
                dve.wait_ge(ra_ok, 15 * jb + 9)
                for k in range(TOPK):
                    dve.scalar_tensor_tensor(rows[k][:, pb, :, D + 1], topv[:, :, k], ROUTE_SCALE, ssum[:, :],
                                             ALU.mult, ALU.mult).then_inc(ra_ok, 1)
                for k in range(TOPK):
                    dve.tensor_copy(rows[k][:, pb, :, D].bitcast(I32), idf[:, k, :]).then_inc(ra_ok, 1)
                dve.wait_ge(ra_ok, 15 * jb + 14)
                dve.tensor_scalar(idf[:, :, :], idf[:, :, :], float(T * TOPK), None, ALU.add).then_inc(ra_ok, 1)

            def hidden(jb, pb):
                dve.wait_ge(sg_ok, jb + 1)
                dve.tensor_tensor(sgT[:, :], bank[B7][:, 0:T], sgT[:, :], ALU.mult).then_inc(hid_ok, 1)
                dve.wait_ge(hid_ok, 2 * jb + 1)
                dve.tensor_tensor(hidT[:, :], bank[B7][:, T:2 * T], sgT[:, :], ALU.mult).then_inc(hid_ok, 1)

            def positions(jb, pb):
                dve.wait_ge(rk_ps, jb + 1)
                dve.wait_ge(ra_ok, 15 * jb + 15)
                dve.tensor_tensor(pose[:, :, :], bank[B6][:, 0:TT * E].rearrange("p (t e) -> p t e", t=TT),
                                  ebase[:, :].unsqueeze(1).to_broadcast([P, TT, E]), ALU.add).then_inc(rb_ok, 1)
                dve.tensor_tensor(seen[:, :], seen[:, :], chosen[:, 0, :], ALU.add).then_inc(rb_ok, 1)
                dve.wait_ge(rb_ok, 6 * jb + 2)
                dve.tensor_tensor(seen[:, :], seen[:, :], chosen[:, 1, :], ALU.add).then_inc(rb_ok, 1)
                oh = onehot[:, :, :].rearrange("p (t k) e -> p t k e", k=TOPK)
                pk = posp[:, :, :].rearrange("p (t k) e -> p t k e", k=TOPK)
                for k in range(TOPK):
                    last = dve.tensor_tensor(pk[:, :, k, :], oh[:, :, k, :], pose[:, :, :], ALU.mult)
                last.then_inc(rb_ok, 1)
                dve.wait_ge(rb_ok, 6 * jb + 4)
                dve.reduce_sum(posf[:, :], posp[:, :, :], AX.X).then_inc(rb_ok, 1)
                dve.wait_ge(rb_ok, 6 * jb + 5)
                dve.tensor_copy(posi[:, pb, :], posf[:, :]).then_inc(rb_ok, 1)

            def keep_acc(jb, pb):
                dve.wait_ge(dn_ps, jb + 1)
                dve.tensor_tensor(acc[:, bass.ds(jb * (TT * D), TT * D)], bank[B7][:, :],
                                  x2[:, :, :].rearrange("p t d -> p (t d)"), ALU.add).then_inc(acc_ok, 1)

            def stats_x(jn, pn, u):
                dve.wait_ge(xa_in[pn], u * 16 + 16)
                norm_stats(0, jn, xa[:, pn, :, :])

            def normalise_x(jn, pn):
                dve.wait_ge(rr[0], 2 * jn + 2)
                wait(dve, tx_ps, jn)
                for t in range(TT):
                    last = dve.tensor_scalar(xn[:, t, :], xa[:, pn, t, :], mv[:, 0, t, 0:1], rstd[:, 0, t:t + 1],
                                             ALU.subtract, ALU.mult)
                last.then_inc(xn_ok, 1)

            def keep_vsum(jf):
                dve.wait_ge(c_ps, jf + 1)
                wait(dve, o_ok, 2 * jf)
                dve.tensor_copy(vsum[:, :], bank[FB][:, 0:GROUPS]).then_inc(c_ok, 1)

            def step(att, back, front, nxt):
                jn, pn = (num(nxt), nxt[1]) if nxt else (None, None)
                jb, pb = (num(back), back[1]) if back else (None, None)
                jf = num(front) if front else None
                if first(front):
                    rotary_angles()
                if first(att):
                    filler_index()
                if back:
                    halves[0] = back[0]
                if back:
                    divide(jb, pb)
                    project_context(jb, pb)
                if front:
                    rope(jf, 0)
                if back:
                    residual_one(jb, pb)
                if front:
                    rope(jf, 1)
                if back:
                    residual_two(jb, pb)
                if front:
                    low_part(jf, 0)
                if back:
                    norm_three(jb, pb)
                if front:
                    keep_T(dve, dve.tensor_copy, jf, front, 0, 0)
                    low_part(jf, 1)
                    keep_T(dve, dve.tensor_copy, jf, front, 0, 1)
                if nxt:
                    stats_x(jn, pn, nxt[0])
                if front:
                    keep_T(dve, dve.tensor_copy, jf, front, 1, 0)
                if back:
                    top_experts(jb, pb)
                    hidden(jb, pb)
                if nxt:
                    normalise_x(jn, pn)
                if back:
                    positions(jb, pb)
                    keep_acc(jb, pb)
                if front:
                    keep_vsum(jf)

            def expert(n, c, m):
                small = isinstance(n, int)
                if not small or 1 <= n <= SLOTS:
                    r = (c - 1) % 2
                    dve.wait_ge(esg_ok, n)
                    if not small or n >= 3:
                        dve.wait_ge(etd_ps, n - 2)
                    dve.tensor_tensor(ehd[:, r, :], bank[2 + r][:, M:2 * M], esg[:, r, :], ALU.mult).then_inc(ehd_ok, 1)
                if not small or 2 <= n <= SLOTS + 1:
                    r = (c - 2) % 2
                    dve.wait_ge(etd_ps, n - 1)
                    if not small or n >= 4:
                        dve.wait_ge(edn_ps, n - 3)
                    dve.tensor_copy(ehT[:, r, :], bank[4 if small and n < EARLY else 4 + r][:, 0:P]).then_inc(ehT_ok, 1)
                if not small or n >= 3:
                    r, y = (c - 3) % XRING, (c - 3) % YRING
                    q = (n - 3) // YRING if small else m * 2 + (c - 3) // YRING
                    dve.wait_ge(edn_ps, n - 2)
                    wait(dve, ys_out[y], q * 16)
                    dve.tensor_scalar(ys[:, y, :], bank[5 if small and n < EARLY else 6 + r % 2][:, 0:D], xs[:, r, D + 1:D + 2], None, ALU.mult).then_inc(ys_ok, 1)

            pipeline(dve, step)

            halves[0] = NB // 2 - 1
            divide(NB - 2, 0)
            project_context(NB - 2, 0)
            plan_slots(FB, 0)
            residual_one(NB - 2, 0)
            keep_plan(FB, 0, EARLY)
            residual_two(NB - 2, 0)
            dve.wait_ge(pv_ps, GROUPS * NB)
            norm_three(NB - 2, 0)
            early(expert, 0, 1)
            top_experts(NB - 2, 0)
            positions(NB - 2, 0)
            hidden(NB - 2, 0)
            early(expert, 1, 2)
            keep_acc(NB - 2, 0)
            divide(NB - 1, 1)
            project_context(NB - 1, 1)
            early(expert, 2, 3)
            residual_one(NB - 1, 1)
            early(expert, 3, 6)
            residual_two(NB - 1, 1)
            early(expert, 6, 8)
            norm_three(NB - 1, 1)
            early(expert, 8, 10)
            top_experts(NB - 1, 1)
            hidden(NB - 1, 1)
            early(expert, 10, 12)
            positions(NB - 1, 1)
            early(expert, 12, 15)
            plan_slots(B6, EARLY, 15)
            keep_acc(NB - 1, 1)
            keep_plan(B6, EARLY, P)
            early(expert, 16, EARLY)
            late(dve, expert)

            with dve.Fori(0, NTILES // CRING) as m:
                for r in range(CRING):
                    dve.wait_ge(yp_in[r], m * 16 + 16)
                    a = acc[:, bass.ds((m * CRING + r) * D, D)]
                    dve.tensor_tensor(a, a, ypair[:, r, 0:D], ALU.add).then_inc(f1_ok, 1)
                    dve.wait_ge(f1_ok, m * CRING + r + 1)
                    dve.tensor_tensor(a, a, ypair[:, r, D:2 * D], ALU.add).then_inc(fin_ok, 1)

        @block.tensor
        def _(pe):
            pe.wait_ge(c_pool, 6)
            pe.wait_ge(c_dve, 2)

            def scores(j, b, a):
                wait(pe, sq_ok, 8 * j + a - 1)
                if a == 0:
                    pe.wait_ge(qkT_ok, 4 * j + 4)
                for h in range(2):
                    for kt in range(TT):
                        lo = 64 * h
                        last = pe.matmul(bank[2 * (a % 2) + h][:, kt * T:(kt + 1) * T],
                                         kT[lo:lo + 64, b[1], a, kt * P:(kt + 1) * P],
                                         qT[lo:lo + 64, b[1], a, :], start=True, stop=True)
                last.then_inc(s_ps, 1)

            def weighted(j, b, g):
                pe.wait_ge(sq_ok, 8 * j + 2 * g + 2)
                if g % 2 == 0:
                    wait(pe, o_ok, 2 * j + g // 2)
                for kt in range(TT):
                    for h in range(HPG):
                        head = HPG * g + h
                        last = pe.matmul(bank[PVB][32 * h:32 * h + 32, (g % 2) * T:(g % 2 + 1) * T],
                                         vaug[:, b[1], kt, head, :], sq[:, (head // 2) % 4, head % 2, kt, :],
                                         start=(kt == 0), stop=(kt == TT - 1))
                last.then_inc(pv_ps, 1)

            def project_qk(j, t):
                if t == 0:
                    if isinstance(j, int) and j == 0:
                        pe.wait_ge(wqk_in, 32)
                    pe.wait_ge(hT_ok, j + 1)
                else:
                    pe.wait_ge(ro_ok, 2 * j + 1)
                for k in range(KD):
                    last = pe.matmul(bank[FB][:, :], hT[:, k, t * P:(t + 1) * P], wqk[:, k, :], start=(k == 0), stop=(k == KD - 1))
                last.then_inc(qk_ps, 1)

            def transpose_qk(j, t, which):
                if which == 0:
                    pe.wait_ge(stk_ok, 6 * j + 3 * t + 3)
                if t == 0 and which == 0:
                    pe.wait_ge(v_ok, j + 1)
                else:
                    pe.wait_ge(qkT_ok, 4 * j + 2 * t + which)
                dst = bank[FB][:, :].bitcast(F16)
                for a in range(HEADS // 2):
                    h = which * HEADS + 2 * a
                    last = pe.transpose(dst[:, a * P:(a + 1) * P],
                                        stack[:, t, h:h + 2, :, :].rearrange("p h s d -> p (h s d)"), identh[:, :])
                last.then_inc(tqk_ps, 1)

            def transpose_out(jb, pb):
                for t in range(TT):
                    pe.wait_ge(o_ok, 2 * jb + 2)
                    if t == 0:
                        wait(pe, rb_ok, 6 * jb)
                    else:
                        wait(pe, acc_ok, jb)
                    for g in range(GROUPS):
                        last = pe.transpose(bank[(B6, B7)[t]][:, g * P:(g + 1) * P], oT[:, g, t * P:(t + 1) * P], identf[:, :])
                    last.then_inc(to_ps, 1)

            def transpose_wv(jb, pb):
                pe.wait_ge(wv_ok, TT * jb + TT)
                for t in range(TT):
                    for k in range(KD):
                        last = pe.transpose(bank[B6][:, (t * KD + k) * P:(t * KD + k + 1) * P], wv[:, t, k * P:(k + 1) * P], identf[:, :])
                last.then_inc(tw_ps, 1)

            def project_out(jb, pb):
                if isinstance(jb, int) and jb == 0:
                    pe.wait_ge(wo_in, 16)
                    pe.wait_ge(ws_in, 16 * WLOADS)
                pe.wait_ge(wvT_ok, jb + 1)
                for t in range(TT):
                    for k in range(KD):
                        last = pe.matmul(bank[B7][:, t * D:(t + 1) * D], wvT[:, k, t * P:(t + 1) * P], wo[:, k, :],
                                         start=(k == 0), stop=(k == KD - 1))
                last.then_inc(wo_ps, 1)

            def spread_context(jb, pb):
                pe.wait_ge(enc_ok, 2 * jb + 2)
                for t in range(TT):
                    last = pe.matmul(bank[B6][:, t * P:(t + 1) * P], enc[:, t:t + 1].to_broadcast([P, P]), identf[:, :],
                                     start=True, stop=True)
                last.then_inc(e_ps, 1)

            def transpose_rows(jb, pb):
                pe.wait_ge(h3_ok, jb + 1)
                for t in range(TT):
                    for k in range(KD):
                        last = pe.transpose(bank[B7][:, (t * KD + k) * P:(t * KD + k + 1) * P],
                                            rows[0][:, pb, t, k * P:(k + 1) * P], identf[:, :])
                last.then_inc(th_ps, 1)

            def gate(jb, pb):
                pe.wait_ge(h3T_ok, jb + 1)
                for t in range(TT):
                    for k in range(KD):
                        last = pe.matmul(bank[B6][:, t * E:(t + 1) * E], h3T[:, k, t * P:(t + 1) * P], gwT[:, k, :],
                                         start=(k == 0), stop=(k == KD - 1))
                last.then_inc(ga_ps, 1)

            def shared_in(jb, pb):
                for s in range(2):
                    for k in range(KD):
                        last = pe.matmul(bank[B7][:, s * T:(s + 1) * T], wsgu[:, k, s * M:(s + 1) * M], h3T[:, k, :],
                                         start=(k == 0), stop=(k == KD - 1))
                last.then_inc(sh_ps, 1)

            def rank(jb, pb):
                pe.wait_ge(ra_ok, 15 * jb + 10)
                pe.wait_ge(sco_ok, jb + 1)
                for t in range(TT):
                    dst = bank[B6][:, t * E:(t + 1) * E]
                    pe.matmul(dst, tri[:, :], chosen[:, t, :], start=True, stop=False)
                    for s in range(t):
                        pe.matmul(dst, onesb[:, :], chosen[:, s, :], start=False, stop=False)
                    last = pe.matmul(dst, onesb[:, :], seen[:, :], start=False, stop=True)
                last.then_inc(rk_ps, 1)

            def shared_down(jb, pb):
                pe.wait_ge(hid_ok, 2 * jb + 2)
                for t in range(TT):
                    last = pe.matmul(bank[B7][:, t * D:(t + 1) * D], hidT[:, t * P:(t + 1) * P], wsd[:, :], start=True, stop=True)
                last.then_inc(dn_ps, 1)

            def count_tokens(b, batches):
                pe.wait_ge(rb_ok, 6 * batches)
                pe.matmul(bank[b][:, 0:E], onesb[:, :], seen[:, :], start=True, stop=True).then_inc(cnt_ps, 1)

            def transpose_plan(b, value):
                pe.wait_ge(pcol_ok, value)
                for i in range(2):
                    last = pe.matmul(bank[b][0:1, i * P:(i + 1) * P], plan[:, 4 + i:5 + i], identf[:, :], start=True, stop=True)
                last.then_inc(plan_ps, 1)

            def project_v(jf):
                if isinstance(jf, int) and jf == 0:
                    pe.wait_ge(wv_in, 16)
                pe.wait_ge(ro_ok, 2 * jf + 2)
                for t in range(TT):
                    for k in range(KD):
                        last = pe.matmul(bank[FB][:, t * D:(t + 1) * D], hT[:, k, t * P:(t + 1) * P], wv_w[:, k, :],
                                         start=(k == 0), stop=(k == KD - 1))
                last.then_inc(v_ps, 1)

            def transpose_xn(jf):
                pe.wait_ge(xn_ok, jf + 1)
                wait(pe, c_ok, jf)
                for t in range(TT):
                    for k in range(KD):
                        last = pe.transpose(bank[FB][:, (t * KD + k) * P:(t * KD + k + 1) * P], xn[:, t, k * P:(k + 1) * P], identf[:, :])
                last.then_inc(tx_ps, 1)

            def sum_v(jf):
                pe.wait_ge(qkT_ok, 4 * jf + 4)
                pe.wait_ge(vp_ok, jf + 1)
                for g in range(GROUPS):
                    last = pe.matmul(bank[FB][:, g:g + 1],
                                     vpair[:, HPG * g:HPG * g + HPG, :].rearrange("p h d -> p (h d)"),
                                     onesf[:, 0:1], start=True, stop=True)
                last.then_inc(c_ps, 1)

            columns = []

            def expert(n, c, m):
                small = isinstance(n, int)
                if c == 0:
                    columns[:] = read_plan(pe, n + P, 4 + XRING, (E - 1) * WE)
                if not small or n < SLOTS:
                    q = n // XRING + 1 if small else m + 1
                    pe.wait_ge(xs_in[c], q * 16)
                    if not small or n >= 2:
                        pe.wait_ge(exT_ok, n - 1)
                    for k in range(KD):
                        last = pe.transpose(bank[c % 2][:, k * P:(k + 1) * P], xs[:, c, k * P:(k + 1) * P], identf[:, :])
                    last.then_inc(etx_ps, 1)
                if not small or 1 <= n <= SLOTS:
                    r = (c - 1) % 2
                    w = columns[c + 3]
                    pe.wait_ge(exT_ok, n)
                    if not small or n >= 3:
                        pe.wait_ge(ehd_ok, n - 2)
                    for k in range(KD):
                        last = pe.matmul(bank[2 + r][:, 0:2 * M], exT[:, r, k, :], wex[:, bass.ds(w + k * 2 * M, 2 * M)],
                                         start=(k == 0), stop=(k == KD - 1))
                    last.then_inc(gu_ps, 1)
                if not small or 2 <= n <= SLOTS + 1:
                    r = (c - 2) % 2
                    pe.wait_ge(ehd_ok, n - 1)
                    if small and 3 <= n < EARLY:
                        pe.wait_ge(ehT_ok, n - 2)
                    elif not small or n >= EARLY:
                        pe.wait_ge(ehT_ok, n - 3)
                    pe.transpose(bank[4 if small and n < EARLY else 4 + r][:, 0:P], ehd[:, r, :], identf[:, :]).then_inc(etd_ps, 1)
                if not small or n >= 3:
                    r = (c - 3) % 2
                    w = columns[c + 1]
                    pe.wait_ge(ehT_ok, n - 2)
                    if small and 4 <= n < EARLY:
                        pe.wait_ge(ys_ok, n - 3)
                    elif not small or n >= EARLY:
                        pe.wait_ge(ys_ok, n - 4)
                    pe.matmul(bank[5 if small and n < EARLY else 6 + r][:, 0:D], ehT[:, r, :], wex[:, bass.ds(w + KD * 2 * M, D)], start=True, stop=True).then_inc(edn_ps, 1)

            def step(att, back, front, nxt):
                ja = num(att) if att else None
                jb, pb = (num(back), back[1]) if back else (None, None)
                jf = num(front) if front else None
                if back:
                    transpose_out(jb, pb)
                if front:
                    transpose_xn(jf)
                if att:
                    scores(ja, att, 0)
                    scores(ja, att, 1)
                if back:
                    transpose_wv(jb, pb)
                if front:
                    project_qk(jf, 0)
                if back:
                    project_out(jb, pb)
                    spread_context(jb, pb)
                if front:
                    project_qk(jf, 1)
                if att:
                    scores(ja, att, 2)
                    scores(ja, att, 3)
                    weighted(ja, att, 0)
                    scores(ja, att, 4)
                if front:
                    project_v(jf)
                if att:
                    scores(ja, att, 5)
                    weighted(ja, att, 1)
                if front:
                    transpose_qk(jf, 0, 0)
                if back:
                    transpose_rows(jb, pb)
                if att:
                    scores(ja, att, 6)
                if front:
                    transpose_qk(jf, 0, 1)
                if att:
                    scores(ja, att, 7)
                if back:
                    gate(jb, pb)
                if front:
                    transpose_qk(jf, 1, 0)
                if back:
                    shared_in(jb, pb)
                if front:
                    transpose_qk(jf, 1, 1)
                if att:
                    weighted(ja, att, 2)
                if back:
                    rank(jb, pb)
                if att:
                    weighted(ja, att, 3)
                if back:
                    shared_down(jb, pb)
                if front:
                    sum_v(jf)

            pipeline(pe, step)

            transpose_out(NB - 2, 0)
            pe.wait_ge(c_ok, NB)
            count_tokens(FB, PLANNED)
            transpose_wv(NB - 2, 0)
            scores(NB - 1, LAST, 0)
            scores(NB - 1, LAST, 1)
            project_out(NB - 2, 0)
            spread_context(NB - 2, 0)
            transpose_plan(FB, 2)
            scores(NB - 1, LAST, 2)
            scores(NB - 1, LAST, 3)
            weighted(NB - 1, LAST, 0)
            scores(NB - 1, LAST, 4)
            scores(NB - 1, LAST, 5)
            weighted(NB - 1, LAST, 1)
            scores(NB - 1, LAST, 6)
            scores(NB - 1, LAST, 7)
            weighted(NB - 1, LAST, 2)
            weighted(NB - 1, LAST, 3)
            pe.wait_ge(sq_ok, 8 * NB)
            pe.wait_ge(o_ok, 2 * NB)
            pe.wait_ge(plan_ok, 2)
            pe.wait_ge(wex_in, 16 * 5)
            transpose_rows(NB - 2, 0)
            gate(NB - 2, 0)
            early(expert, 0, 1)
            shared_in(NB - 2, 0)
            rank(NB - 2, 0)
            early(expert, 1, 2)
            shared_down(NB - 2, 0)
            transpose_out(NB - 1, 1)
            transpose_wv(NB - 1, 1)
            early(expert, 2, 3)
            project_out(NB - 1, 1)
            spread_context(NB - 1, 1)
            early(expert, 3, 8)
            transpose_rows(NB - 1, 1)
            early(expert, 8, 10)
            gate(NB - 1, 1)
            shared_in(NB - 1, 1)
            early(expert, 10, 12)
            rank(NB - 1, 1)
            early(expert, 12, 15)
            count_tokens(B6, NB)
            early(expert, 15, 16)
            shared_down(NB - 1, 1)
            transpose_plan(B6, 4)
            early(expert, 16, EARLY)
            pe.wait_ge(plan_ok, 4)
            pe.wait_ge(acc_ok, NB)
            pe.wait_ge(ehT_ok, EARLY - 2)
            pe.wait_ge(ys_ok, EARLY - 3)
            late(pe, expert)


_INS = ["x", "ctx_1024", "L0_attn_ln_w", "L0_attn_ln_b", "L0_attn_w_q", "L0_attn_w_kv", "L0_attn_w_o", "L0_attn_theta",
        "L0_xattn_mlp_weight", "L0_xattn_mlp_bias", "L0_ffn_gate_w", "L0_ffn_w_gate", "L0_ffn_w_up", "L0_ffn_w_down",
        "L0_ffn_ws_gate", "L0_ffn_ws_up", "L0_ffn_ws_down"]


def kernel(**inputs):
    import concourse.bacc as bacc
    from concourse.bass_utils import run_bass_kernel_spmd

    nc = bacc.Bacc("TRN2", target_bir_lowering=False, num_devices=1)
    arrays, args = {}, []
    for name in _INS:
        a = np.ascontiguousarray(inputs[name])
        if name == "L0_attn_theta":
            a = a.reshape(1)
        if name == "L0_ffn_gate_w":
            a = np.ascontiguousarray(a.T)
        if name in ("L0_attn_ln_w", "L0_attn_ln_b"):
            a = np.ascontiguousarray(a.reshape(KD, P).T)
        arrays[f"in_{name}"] = a
        args.append(nc.dram_tensor(f"in_{name}", a.shape, mybir.dt.from_np(a.dtype), kind="ExternalInput").ap())
    args.append(nc.dram_tensor("out_0", (NB, T, D), F32, kind="ExternalOutput").ap())
    build(nc, *args)
    r = run_bass_kernel_spmd(nc, [arrays], core_ids=[0])
    return r.results[0]["out_0"]
```
